# Optimizing a Trainium2 kernel written in Bass

```python
import numpy as np
import jax
import jax.numpy as jnp

def _softmax(x, axis=-1):
    return jax.nn.softmax(x, axis=axis)

def _gelu(x):
    return jax.nn.gelu(x, approximate=True)

def _silu(x):
    return jax.nn.silu(x)

def _sigmoid(x):
    return jax.nn.sigmoid(x)

def _layernorm(x, axis=-1, eps=1e-05):
    m = jnp.mean(x, axis=axis, keepdims=True)
    v = jnp.var(x, axis=axis, keepdims=True)
    return (x - m) / jnp.sqrt(v + eps)

def _scatter_add(tgt, idx, src, axis=0):
    return tgt.at[idx].add(src)

def _segment_sum(src, seg, n):
    return jax.ops.segment_sum(src, seg, n)
kernel_name = 'mk_macaron_d2_jaxref_r4_42736c'

def setup_inputs(seed: int=0):
    np.random.seed(seed)
    _w = jnp.asarray

    def _L0_attn_setup():
        import jax, jax.numpy as jnp
        import numpy as np
        from jax import lax
        D = 256
        K = 3
        LN_EPS = 1e-05

        def _dwconv(v, conv_w, conv_b):
            vt = jnp.transpose(v, (0, 2, 1))
            out = lax.conv_general_dilated(vt, conv_w, window_strides=(1,), padding=[(K // 2, K // 2)], dimension_numbers=('NCH', 'OIH', 'NCH'), feature_group_count=D)
            out = out + conv_b[None, :, None]
            return jnp.transpose(out, (0, 2, 1))
        key = jax.random.key(seed)
        ks = jax.random.split(key, 8)
        B, T = (8, 1024)
        x = jax.random.normal(ks[0], (B, T, D), dtype=jnp.float32)
        s = 1.0 / np.sqrt(D)
        in_proj_w = jax.random.uniform(ks[1], (D, 2 * D), jnp.float32, -s, s)
        in_proj_b = jax.random.uniform(ks[2], (2 * D,), jnp.float32, -s, s)
        conv_w = jax.random.uniform(ks[3], (D, 1, K), jnp.float32, -1.0 / np.sqrt(K), 1.0 / np.sqrt(K))
        conv_b = jax.random.uniform(ks[4], (D,), jnp.float32, -1.0 / np.sqrt(K), 1.0 / np.sqrt(K))
        logit_a = jnp.zeros((D,), jnp.float32)
        ssm_b = jnp.full((D,), 0.1, jnp.float32)
        ssm_c = jnp.ones((D,), jnp.float32)
        ssm_d = jnp.zeros((D,), jnp.float32)
        out_proj_w = jax.random.uniform(ks[5], (D, D), jnp.float32, -s, s)
        out_proj_b = jax.random.uniform(ks[6], (D,), jnp.float32, -s, s)
        ln_w = jnp.ones((D,), jnp.float32)
        ln_b = jnp.zeros((D,), jnp.float32)
        return {'x': x, 'in_proj_w': in_proj_w, 'in_proj_b': in_proj_b, 'conv_w': conv_w, 'conv_b': conv_b, 'logit_a': logit_a, 'ssm_b': ssm_b, 'ssm_c': ssm_c, 'ssm_d': ssm_d, 'out_proj_w': out_proj_w, 'out_proj_b': out_proj_b, 'ln_w': ln_w, 'ln_b': ln_b}
    _L0_attn_in = _L0_attn_setup()

    def _L0_ffn_setup():
        import jax, jax.numpy as jnp
        import numpy as np
        HIDDEN = 256
        INTER = 1024
        key = jax.random.key(seed)
        k1, k2, k3, k4, k5 = jax.random.split(key, 5)
        hidden_states = jax.random.normal(k1, (4, 512, HIDDEN), dtype=jnp.float32)
        W1 = jax.random.normal(k2, (HIDDEN, INTER), dtype=jnp.float32) * (1.0 / np.sqrt(HIDDEN))
        b1 = jax.random.normal(k3, (INTER,), dtype=jnp.float32) * 0.02
        W2 = jax.random.normal(k4, (INTER, HIDDEN), dtype=jnp.float32) * (1.0 / np.sqrt(INTER))
        b2 = jax.random.normal(k5, (HIDDEN,), dtype=jnp.float32) * 0.02
        return {'hidden_states': hidden_states, 'W1': W1, 'b1': b1, 'W2': W2, 'b2': b2}
    _L0_ffn_in = _L0_ffn_setup()

    def _L1_attn_setup():
        import jax, jax.numpy as jnp
        import numpy as np
        B, S, D = (2, 512, 256)
        H = 16
        HD = D // H
        SCALE = HD ** (-0.5)

        def _rope_tables(seq_len, dim, dtype=jnp.float32):
            inv_freq = 1.0 / 10000.0 ** (jnp.arange(0, dim, 2, dtype=jnp.float32) / dim)
            t = jnp.arange(seq_len, dtype=jnp.float32)
            freqs = t[:, None] * inv_freq[None, :]
            return (jnp.cos(freqs).astype(dtype), jnp.sin(freqs).astype(dtype))

        def _apply_rope(x, cos, sin):
            half = x.shape[-1] // 2
            x1, x2 = (x[..., :half], x[..., half:])
            c = cos[None, None, :, :]
            s = sin[None, None, :, :]
            rx1 = x1 * c - x2 * s
            rx2 = x1 * s + x2 * c
            return jnp.concatenate([rx1, rx2], axis=-1)
        key = jax.random.key(seed)
        k1, k2, k3 = jax.random.split(key, 3)
        x = jax.random.normal(k1, (B, S, D), dtype=jnp.float32)
        w_qkv = jax.random.normal(k2, (3 * D, D), dtype=jnp.float32) * D ** (-0.5)
        w_out = jax.random.normal(k3, (D, D), dtype=jnp.float32) * D ** (-0.5)
        b_out = jnp.zeros((D,), dtype=jnp.float32)
        return {'x': x, 'w_qkv': w_qkv, 'w_out': w_out, 'b_out': b_out}
    _L1_attn_in = _L1_attn_setup()

    def _L1_ffn_setup():
        import jax, jax.numpy as jnp
        import numpy as np
        B, L, D = (4, 512, 256)
        H = 16
        E = 16
        NS = 16
        S = NS // E
        F = 1024
        EPS = 1e-05

        def _layernorm(x, g, b):
            mu = jnp.mean(x, axis=-1, keepdims=True)
            var = jnp.mean(jnp.square(x - mu), axis=-1, keepdims=True)
            return (x - mu) * jax.lax.rsqrt(var + EPS) * g + b

        def _mha(q, k, v, Wq, bq, Wk, bk, Wv, bv, Wo, bo):
            Bq, Lq, Dm = q.shape
            dh = Dm // H
            qh = (q @ Wq + bq).reshape(Bq, Lq, H, dh)
            kh = (k @ Wk + bk).reshape(Bq, -1, H, dh)
            vh = (v @ Wv + bv).reshape(Bq, -1, H, dh)
            scores = jnp.einsum('bqhd,bkhd->bhqk', qh, kh) / jnp.asarray(np.sqrt(dh), q.dtype)
            attn = jax.nn.softmax(scores, axis=-1)
            out = jnp.einsum('bhqk,bkhd->bqhd', attn, vh).reshape(Bq, Lq, Dm)
            return out @ Wo + bo
        key = jax.random.key(seed)
        ks = jax.random.split(key, 32)
        s = 0.02
        d = {}
        d['x'] = jax.random.normal(ks[0], (B, L, D), jnp.float32)
        d['slot_query'] = jax.random.normal(ks[1], (1, NS, D), jnp.float32) * 0.01
        for i, nm in enumerate(['d_Wq', 'd_Wk', 'd_Wv', 'd_Wo']):
            d[nm] = jax.random.normal(ks[2 + i], (D, D), jnp.float32) * s
        for nm in ['d_bq', 'd_bk', 'd_bv', 'd_bo']:
            d[nm] = jnp.zeros((D,), jnp.float32)
        for i, nm in enumerate(['c_Wq', 'c_Wk', 'c_Wv', 'c_Wo']):
            d[nm] = jax.random.normal(ks[6 + i], (D, D), jnp.float32) * s
        for nm in ['c_bq', 'c_bk', 'c_bv', 'c_bo']:
            d[nm] = jnp.zeros((D,), jnp.float32)
        d['e_ln_g'] = jnp.ones((E, D), jnp.float32)
        d['e_ln_b'] = jnp.zeros((E, D), jnp.float32)
        d['e_W1'] = jax.random.normal(ks[10], (E, D, F), jnp.float32) * s
        d['e_b1'] = jnp.zeros((E, F), jnp.float32)
        d['e_Wg'] = jax.random.normal(ks[11], (E, D, F), jnp.float32) * s
        d['e_bg'] = jnp.zeros((E, F), jnp.float32)
        d['e_W2'] = jax.random.normal(ks[12], (E, F, D), jnp.float32) * s
        d['e_b2'] = jnp.zeros((E, D), jnp.float32)
        return d
    _L1_ffn_in = _L1_ffn_setup()
    _d = {'L0_attn_x': _L0_attn_in['x'], 'L0_attn_in_proj_w': _L0_attn_in['in_proj_w'], 'L0_attn_in_proj_b': _L0_attn_in['in_proj_b'], 'L0_attn_conv_w': _L0_attn_in['conv_w'], 'L0_attn_conv_b': _L0_attn_in['conv_b'], 'L0_attn_logit_a': _L0_attn_in['logit_a'], 'L0_attn_ssm_b': _L0_attn_in['ssm_b'], 'L0_attn_ssm_c': _L0_attn_in['ssm_c'], 'L0_attn_ssm_d': _L0_attn_in['ssm_d'], 'L0_attn_out_proj_w': _L0_attn_in['out_proj_w'], 'L0_attn_out_proj_b': _L0_attn_in['out_proj_b'], 'L0_attn_ln_w': _L0_attn_in['ln_w'], 'L0_attn_ln_b': _L0_attn_in['ln_b'], 'L0_ffn_W1': _L0_ffn_in['W1'], 'L0_ffn_b1': _L0_ffn_in['b1'], 'L0_ffn_W2': _L0_ffn_in['W2'], 'L0_ffn_b2': _L0_ffn_in['b2'], 'L1_attn_w_qkv': _L1_attn_in['w_qkv'], 'L1_attn_w_out': _L1_attn_in['w_out'], 'L1_attn_b_out': _L1_attn_in['b_out'], 'L1_ffn_slot_query': _L1_ffn_in['slot_query'], 'L1_ffn_d_Wq': _L1_ffn_in['d_Wq'], 'L1_ffn_d_Wk': _L1_ffn_in['d_Wk'], 'L1_ffn_d_Wv': _L1_ffn_in['d_Wv'], 'L1_ffn_d_Wo': _L1_ffn_in['d_Wo'], 'L1_ffn_d_bq': _L1_ffn_in['d_bq'], 'L1_ffn_d_bk': _L1_ffn_in['d_bk'], 'L1_ffn_d_bv': _L1_ffn_in['d_bv'], 'L1_ffn_d_bo': _L1_ffn_in['d_bo'], 'L1_ffn_c_Wq': _L1_ffn_in['c_Wq'], 'L1_ffn_c_Wk': _L1_ffn_in['c_Wk'], 'L1_ffn_c_Wv': _L1_ffn_in['c_Wv'], 'L1_ffn_c_Wo': _L1_ffn_in['c_Wo'], 'L1_ffn_c_bq': _L1_ffn_in['c_bq'], 'L1_ffn_c_bk': _L1_ffn_in['c_bk'], 'L1_ffn_c_bv': _L1_ffn_in['c_bv'], 'L1_ffn_c_bo': _L1_ffn_in['c_bo'], 'L1_ffn_e_ln_g': _L1_ffn_in['e_ln_g'], 'L1_ffn_e_ln_b': _L1_ffn_in['e_ln_b'], 'L1_ffn_e_W1': _L1_ffn_in['e_W1'], 'L1_ffn_e_b1': _L1_ffn_in['e_b1'], 'L1_ffn_e_Wg': _L1_ffn_in['e_Wg'], 'L1_ffn_e_bg': _L1_ffn_in['e_bg'], 'L1_ffn_e_W2': _L1_ffn_in['e_W2'], 'L1_ffn_e_b2': _L1_ffn_in['e_b2']}
    _x0 = _d['L0_attn_x']
    _d['L0_attn_x'] = jax.random.normal(jax.random.fold_in(jax.random.key(seed), 1), (1, 4096, 256), dtype=_x0.dtype)
    del _x0
    return _d

def reference(L0_attn_x, L0_attn_in_proj_w, L0_attn_in_proj_b, L0_attn_conv_w, L0_attn_conv_b, L0_attn_logit_a, L0_attn_ssm_b, L0_attn_ssm_c, L0_attn_ssm_d, L0_attn_out_proj_w, L0_attn_out_proj_b, L0_attn_ln_w, L0_attn_ln_b, L0_ffn_W1, L0_ffn_b1, L0_ffn_W2, L0_ffn_b2, L1_attn_w_qkv, L1_attn_w_out, L1_attn_b_out, L1_ffn_slot_query, L1_ffn_d_Wq, L1_ffn_d_Wk, L1_ffn_d_Wv, L1_ffn_d_Wo, L1_ffn_d_bq, L1_ffn_d_bk, L1_ffn_d_bv, L1_ffn_d_bo, L1_ffn_c_Wq, L1_ffn_c_Wk, L1_ffn_c_Wv, L1_ffn_c_Wo, L1_ffn_c_bq, L1_ffn_c_bk, L1_ffn_c_bv, L1_ffn_c_bo, L1_ffn_e_ln_g, L1_ffn_e_ln_b, L1_ffn_e_W1, L1_ffn_e_b1, L1_ffn_e_Wg, L1_ffn_e_bg, L1_ffn_e_W2, L1_ffn_e_b2):

    def _L0_attn_ref(x, in_proj_w, in_proj_b, conv_w, conv_b, logit_a, ssm_b, ssm_c, ssm_d, out_proj_w, out_proj_b, ln_w, ln_b):
        import jax, jax.numpy as jnp
        import numpy as np
        from jax import lax
        D = 256
        K = 3
        LN_EPS = 1e-05

        def _dwconv(v, conv_w, conv_b):
            vt = jnp.transpose(v, (0, 2, 1))
            out = lax.conv_general_dilated(vt, conv_w, window_strides=(1,), padding=[(K // 2, K // 2)], dimension_numbers=('NCH', 'OIH', 'NCH'), feature_group_count=D)
            out = out + conv_b[None, :, None]
            return jnp.transpose(out, (0, 2, 1))
        B, T, _ = x.shape
        residual = x
        uv = x @ in_proj_w + in_proj_b
        u, v = (uv[..., :D], uv[..., D:])
        v = jax.nn.silu(v)
        v_local = _dwconv(v, conv_w, conv_b)
        a = jax.nn.sigmoid(logit_a).astype(v_local.dtype)

        def step(h, vt):
            h = a * h + ssm_b * vt
            return (h, ssm_c * h + ssm_d * vt)
        h0 = jnp.zeros((B, D), v_local.dtype)
        _, y_seq = lax.scan(step, h0, jnp.transpose(v_local, (1, 0, 2)))
        y_seq = jnp.transpose(y_seq, (1, 0, 2))
        out = u * jax.nn.silu(y_seq)
        out = out @ out_proj_w + out_proj_b
        h = out + residual
        mu = jnp.mean(h, axis=-1, keepdims=True)
        var = jnp.mean(jnp.square(h - mu), axis=-1, keepdims=True)
        return (h - mu) * lax.rsqrt(var + LN_EPS) * ln_w + ln_b

    def _L0_ffn_ref(hidden_states, W1, b1, W2, b2):
        import jax, jax.numpy as jnp
        import numpy as np
        HIDDEN = 256
        INTER = 1024
        h = jax.nn.relu(jnp.einsum('bsh,hi->bsi', hidden_states, W1) + b1)
        return jnp.einsum('bsi,ih->bsh', h, W2) + b2

    def _L1_attn_ref(x, w_qkv, w_out, b_out):
        import jax, jax.numpy as jnp
        import numpy as np
        B, S, D = (2, 512, 256)
        H = 16
        HD = D // H
        SCALE = HD ** (-0.5)

        def _rope_tables(seq_len, dim, dtype=jnp.float32):
            inv_freq = 1.0 / 10000.0 ** (jnp.arange(0, dim, 2, dtype=jnp.float32) / dim)
            t = jnp.arange(seq_len, dtype=jnp.float32)
            freqs = t[:, None] * inv_freq[None, :]
            return (jnp.cos(freqs).astype(dtype), jnp.sin(freqs).astype(dtype))

        def _apply_rope(x, cos, sin):
            half = x.shape[-1] // 2
            x1, x2 = (x[..., :half], x[..., half:])
            c = cos[None, None, :, :]
            s = sin[None, None, :, :]
            rx1 = x1 * c - x2 * s
            rx2 = x1 * s + x2 * c
            return jnp.concatenate([rx1, rx2], axis=-1)
        b, s, d = x.shape
        qkv = jnp.einsum('bsd,ed->bse', x, w_qkv)
        qkv = qkv.reshape(b, s, 3, H, HD).transpose(2, 0, 3, 1, 4)
        q, k, v = (qkv[0], qkv[1], qkv[2])
        cos, sin = _rope_tables(s, HD, x.dtype)
        q = _apply_rope(q, cos, sin)
        k = _apply_rope(k, cos, sin)
        scores = jnp.einsum('bhsd,bhtd->bhst', q, k) * SCALE
        attn = jax.nn.softmax(scores, axis=-1)
        out = jnp.einsum('bhst,bhtd->bhsd', attn, v)
        out = out.transpose(0, 2, 1, 3).reshape(b, s, d)
        return jnp.einsum('bsd,ed->bse', out, w_out) + b_out

    def _L1_ffn_ref(x, slot_query, d_Wq, d_Wk, d_Wv, d_Wo, d_bq, d_bk, d_bv, d_bo, c_Wq, c_Wk, c_Wv, c_Wo, c_bq, c_bk, c_bv, c_bo, e_ln_g, e_ln_b, e_W1, e_b1, e_Wg, e_bg, e_W2, e_b2):
        import jax, jax.numpy as jnp
        import numpy as np
        B, L, D = (4, 512, 256)
        H = 16
        E = 16
        NS = 16
        S = NS // E
        F = 1024
        EPS = 1e-05

        def _layernorm(x, g, b):
            mu = jnp.mean(x, axis=-1, keepdims=True)
            var = jnp.mean(jnp.square(x - mu), axis=-1, keepdims=True)
            return (x - mu) * jax.lax.rsqrt(var + EPS) * g + b

        def _mha(q, k, v, Wq, bq, Wk, bk, Wv, bv, Wo, bo):
            Bq, Lq, Dm = q.shape
            dh = Dm // H
            qh = (q @ Wq + bq).reshape(Bq, Lq, H, dh)
            kh = (k @ Wk + bk).reshape(Bq, -1, H, dh)
            vh = (v @ Wv + bv).reshape(Bq, -1, H, dh)
            scores = jnp.einsum('bqhd,bkhd->bhqk', qh, kh) / jnp.asarray(np.sqrt(dh), q.dtype)
            attn = jax.nn.softmax(scores, axis=-1)
            out = jnp.einsum('bhqk,bkhd->bqhd', attn, vh).reshape(Bq, Lq, Dm)
            return out @ Wo + bo
        Bx = x.shape[0]
        q = jnp.broadcast_to(slot_query, (Bx, NS, D))
        o = q + _mha(q, x, x, d_Wq, d_bq, d_Wk, d_bk, d_Wv, d_bv, d_Wo, d_bo)
        os = o.reshape(Bx, E, S, D)
        h = _layernorm(os, e_ln_g[None, :, None, :], e_ln_b[None, :, None, :])
        u = jax.nn.silu(jnp.einsum('besd,edf->besf', h, e_W1) + e_b1[None, :, None, :])
        g = jax.nn.silu(jnp.einsum('besd,edf->besf', h, e_Wg) + e_bg[None, :, None, :])
        y = jnp.einsum('besf,efd->besd', u * g, e_W2) + e_b2[None, :, None, :]
        o = o + y.reshape(Bx, NS, D)
        out = _mha(x, o, o, c_Wq, c_bq, c_Wk, c_bk, c_Wv, c_bv, c_Wo, c_bo)
        return out
    x = L0_attn_x
    x = x + 0.5 * _L0_ffn_ref(_layernorm(x, axis=-1), L0_ffn_W1, L0_ffn_b1, L0_ffn_W2, L0_ffn_b2)
    x = x + _L0_attn_ref(_layernorm(x, axis=-1), L0_attn_in_proj_w, L0_attn_in_proj_b, L0_attn_conv_w, L0_attn_conv_b, L0_attn_logit_a, L0_attn_ssm_b, L0_attn_ssm_c, L0_attn_ssm_d, L0_attn_out_proj_w, L0_attn_out_proj_b, L0_attn_ln_w, L0_attn_ln_b)
    x = x + 0.5 * _L0_ffn_ref(_layernorm(x, axis=-1), L0_ffn_W1, L0_ffn_b1, L0_ffn_W2, L0_ffn_b2)
    x = x + 0.5 * _L1_ffn_ref(_layernorm(x, axis=-1), L1_ffn_slot_query, L1_ffn_d_Wq, L1_ffn_d_Wk, L1_ffn_d_Wv, L1_ffn_d_Wo, L1_ffn_d_bq, L1_ffn_d_bk, L1_ffn_d_bv, L1_ffn_d_bo, L1_ffn_c_Wq, L1_ffn_c_Wk, L1_ffn_c_Wv, L1_ffn_c_Wo, L1_ffn_c_bq, L1_ffn_c_bk, L1_ffn_c_bv, L1_ffn_c_bo, L1_ffn_e_ln_g, L1_ffn_e_ln_b, L1_ffn_e_W1, L1_ffn_e_b1, L1_ffn_e_Wg, L1_ffn_e_bg, L1_ffn_e_W2, L1_ffn_e_b2)
    x = x + _L1_attn_ref(_layernorm(x, axis=-1), L1_attn_w_qkv, L1_attn_w_out, L1_attn_b_out)
    x = x + 0.5 * _L1_ffn_ref(_layernorm(x, axis=-1), L1_ffn_slot_query, L1_ffn_d_Wq, L1_ffn_d_Wk, L1_ffn_d_Wv, L1_ffn_d_Wo, L1_ffn_d_bq, L1_ffn_d_bk, L1_ffn_d_bv, L1_ffn_d_bo, L1_ffn_c_Wq, L1_ffn_c_Wk, L1_ffn_c_Wv, L1_ffn_c_Wo, L1_ffn_c_bq, L1_ffn_c_bk, L1_ffn_c_bv, L1_ffn_c_bo, L1_ffn_e_ln_g, L1_ffn_e_ln_b, L1_ffn_e_W1, L1_ffn_e_b1, L1_ffn_e_Wg, L1_ffn_e_bg, L1_ffn_e_W2, L1_ffn_e_b2)
    return x

_drawn_inputs = setup_inputs


def setup_inputs(seed=0):
    import zlib

    import numpy as np

    out = dict(_drawn_inputs(seed))
    spreads = {'L0_attn_logit_a': (0.0, 0.8),
     'L0_attn_ssm_b': (0.10000000149011612, 0.6),
     'L0_attn_ssm_c': (1.0, 0.6),
     'L0_attn_ssm_d': (0.0, 0.8),
     'L0_attn_ln_w': (1.0, 0.2),
     'L0_attn_ln_b': (0.0, 0.1),
     'L1_attn_b_out': (0.0, 0.301),
     'L1_ffn_d_bq': (0.0, 0.8),
     'L1_ffn_d_bk': (0.0, 2.0),
     'L1_ffn_d_bv': (0.0, 0.8),
     'L1_ffn_d_bo': (0.0, 0.8),
     'L1_ffn_c_bq': (0.0, 0.8),
     'L1_ffn_c_bk': (0.0, 2.0),
     'L1_ffn_c_bv': (0.0, 0.496),
     'L1_ffn_c_bo': (0.0, 0.569),
     'L1_ffn_e_ln_g': (1.0, 0.6),
     'L1_ffn_e_ln_b': (0.0, 0.8),
     'L1_ffn_e_b1': (0.0, 0.8),
     'L1_ffn_e_bg': (0.0, 0.8),
     'L1_ffn_e_b2': (0.0, 0.8)}
    factors = {'L0_attn_in_proj_w': 8.0,
     'L0_attn_in_proj_b': 8.0,
     'L0_attn_conv_w': 8.0,
     'L0_attn_conv_b': 8.0,
     'L0_attn_out_proj_w': 8.0,
     'L0_attn_out_proj_b': 2.939,
     'L0_ffn_b1': 5.809,
     'L0_ffn_b2': 3.792,
     'L1_ffn_slot_query': 8.0,
     'L1_ffn_d_Wq': 8.0,
     'L1_ffn_d_Wk': 8.0,
     'L1_ffn_d_Wv': 8.0,
     'L1_ffn_d_Wo': 8.0,
     'L1_ffn_c_Wq': 8.0,
     'L1_ffn_c_Wk': 8.0,
     'L1_ffn_c_Wv': 8.0,
     'L1_ffn_c_Wo': 3.46,
     'L1_ffn_e_W1': 8.0,
     'L1_ffn_e_Wg': 8.0,
     'L1_ffn_e_W2': 8.0}
    for name, (base, spread) in spreads.items():
        noise = np.random.default_rng([zlib.crc32(name.encode()), seed]).standard_normal(out[name].shape)
        drawn = base * np.exp(spread * noise) if base else spread * noise
        out[name] = jnp.asarray(drawn.astype(out[name].dtype))
    for name, factor in factors.items():
        out[name] = (out[name] * factor).astype(out[name].dtype)
    return out
```

```python
import numpy as np
import concourse.bass as bass
from concourse import mybir
from contextlib import ExitStack

f32 = mybir.dt.float32
bf16 = mybir.dt.bfloat16
ALU = mybir.AluOpType
ACT = mybir.ActivationFunctionType
AX = mybir.AxisListType
ds = bass.ds

P = 128
T = 4096
D = 256
KD = D // P
TILES = T // P
CH = 512
NCH = T // CH
TPC = CH // P
F = 1024
KF = F // P
H = 16
HD = D // H
E = 16
PAIRS = H * E
EPS = 1e-5
SCALE = HD ** -0.5
GROUPS = 4
RING = 4
UNITS = 6 * GROUPS
SPLITS = 3
TERMS = 6
Q_PART = (0, 0, 0, 1, 1, 2)
K_PART = (0, 1, 2, 0, 1, 0)
QK_ROWS = TERMS * HD
ROWS = QK_ROWS + SPLITS
HALF = T // 2
ROUNDS = 2 * H
KT = TILES
MAXES = (HALF // P) * NCH
SLOTS = MAXES + 4
MRING = 3
PRING = 8
STATS = 5


class Steps:

    def __init__(self, engine, sem, base=0):
        self.engine, self.sem, self.at = engine, sem, base

    def add(self, instruction):
        instruction.then_inc(self.sem, 1)
        self.at = self.at + 1

    def wait(self):
        self.engine.wait_ge(self.sem, self.at)

    def wait_alone(self):
        self.wait()
        self.engine.sem_inc(self.sem, 1)
        self.at = self.at + 1


def constants():
    half = HD // 2
    inv = (1.0 / np.float32(10000.0) ** (np.arange(0, HD, 2, dtype=np.float32) / np.float32(HD))).astype(np.float32)
    ang = (np.arange(T, dtype=np.float32)[:, None] * inv[None, :]).astype(np.float32)
    cos, sin = np.cos(ang).astype(np.float32), np.sin(ang).astype(np.float32)
    rope = np.zeros((P, 2, T), np.float32)
    for p in range(P):
        j = p % HD
        rope[p, 0] = cos[:, j % half]
        rope[p, 1] = -sin[:, j % half] if j < half else sin[:, j % half]
    e = np.arange(P)
    head_of = (np.arange(KD)[None, :, None] * P + e[:, None, None]) // HD
    mask = (head_of == np.arange(H)[None, None, :]).astype(np.float32)
    slot = (e[:, None] % E == np.arange(E)[None, :]).astype(np.float32)
    pick = np.zeros((P, GROUPS, 4), np.float32)
    for g in range(GROUPS):
        for j in range(4):
            pick[32 * j + 4 * j + g, g, j] = 1.0
    return {"c_rope": rope, "c_ident": np.eye(P, dtype=np.float32), "c_mask": mask, "c_slot": slot, "c_pick": pick}


def build(nc, A, out, stop=99):
    with ExitStack() as ctx:
        program(nc, A, out, ctx, stop)


def program(nc, A, out, ctx, stop):
    taken = set()

    def sb(name, shape, dt=f32, stack=ctx):
        name += "_again" * (name in taken)
        taken.add(name)
        return stack.enter_context(nc.sbuf_tensor(name, shape, dt))

    sems = {}

    def sem(name):
        if name not in sems:
            sems[name] = ctx.enter_context(nc.semaphore(name))
        return sems[name]

    X = sb("X", [P, TILES, D])
    mv = sb("mv", [P, TILES, 2])
    st6 = sb("st6", [P, TPC, 6])
    mv4 = sb("mv4", [P, TPC, 2])
    sd = sb("sd", [P, TILES])
    rstd = sb("rstd", [P, TILES])
    eps = sb("eps", [P, 1])
    ident = sb("ident", [P, P])
    identb = sb("identb", [P, P], bf16)
    mask = sb("mask", [P, KD, H])
    slotsel = sb("slotsel", [P, E])
    pick = sb("pick", [P, GROUPS, 4])
    ones = sb("ones", [1, P])
    zeros = sb("zeros", [P, D])
    SLOT_W = ("d_Wq", "d_WkT", "d_Wv", "d_Wo", "c_WqT", "c_Wk", "c_Wv", "c_Wo")
    dW = {n: sb(n, [P, KD, D]) for n in SLOT_W}
    cols = sb("cols", [P, 6, KD])
    rows16 = sb("rows16", [E, 5, D])
    eb = sb("eb", [P, 2, GROUPS, KF, 4])
    bo_half = sb("bo_half", [P, D])
    pool_q = sb("pool_q", [P, KD, PAIRS])
    pool_c = sb("pool_c", [P, 2])
    ps = ctx.enter_context(nc.psum_tensor("ps", [P, 8, CH], f32))
    front = [0, 0]

    def norm_tiles(dst, chunk, src=None, m=None, r=None):
        src, m, r = src or X, m or mv, r or rstd
        for t in range(TPC):
            k = chunk * TPC + t
            last = nc.vector.tensor_scalar(dst[:, t:t + 1, :], src[:, ds(k, 1), :], m[:, ds(k, 1), 0:1],
                                           r[:, ds(k, 1)], ALU.subtract, ALU.mult)
        return last

    def transposes(nchunk):
        for k in range(KD):
            for t in range(TPC):
                last = nc.tensor.transpose(ps[:, k, t * P:(t + 1) * P], nchunk[:, t, k * P:(k + 1) * P], ident[:, :])
        return last

    def stats(dve, steps, chunk, src=None, m=None):
        src, m = src or X, m or mv
        steps.wait_alone()
        for t in range(TPC):
            i = nc.vector.bn_stats(st6[:, t, :], src[:, ds(chunk * TPC + t, 1), :])
        steps.add(i)
        steps.wait_alone()
        for t in range(TPC):
            i = nc.vector.bn_aggr(mv4[:, t, :], st6[:, t, :])
        steps.add(i)
        steps.wait()
        steps.add(nc.vector.tensor_scalar(m[:, ds(chunk * TPC, TPC), :], mv4[:, :, :], 1.0, None, ALU.mult))

    def root(m=None):
        nc.scalar.activation(sd[:, :], (m or mv)[:, :, 1], ACT.Sqrt, bias=eps[:, :]).then_inc(sem("sd_ready"), 1)

    def reciprocal_of_root(dve, nth, dst=None):
        dve.wait_ge(sem("sd_ready"), nth)
        nc.vector.reciprocal((dst or rstd)[:, :], sd[:, :]).then_inc(sem("rstd_ready"), 1)
        dve.wait_ge(sem("rstd_ready"), nth)

    def ffn(inst, W, x_sems):
        (base, nbase), b8 = front, inst * NCH
        front[0] += NCH + 1
        front[1] += NCH + 1
        w1, w2, b1, b2h, nbuf, nT, hT = (W[k] for k in ("w1", "w2", "b1", "b2h", "nbuf", "nT", "hT"))
        with nc.Block() as block:
            if inst == 0:
                @block.sync
                def _(sp):
                    xv = A["x"].rearrange("a (n p) d -> (a p) n d", p=P)
                    for n in range(NCH):
                        sp.dma_start(X[:, n * TPC:(n + 1) * TPC, :], xv[:, n * TPC:(n + 1) * TPC, :]).then_inc(x_sems[n], 16)
                        if n == 0:
                            sp.dma_start(w1[:, :, :], A["W1"].rearrange("(k p) f -> p k f", p=P)).then_inc(sem("w_loaded"), 16)
                            sp.dma_start(w2[:, :, :], A["W2"].rearrange("(k p) f -> p k f", p=P)).then_inc(sem("w_loaded"), 16)
                            sp.dma_start(ident[:, :], A["c_ident"]).then_inc(sem("w_loaded"), 16)
                            sp.dma_start(b1[:, :], A["b1"]).then_inc(sem("w_loaded"), 16)
                            sp.dma_start(b2h[:, :], A["b2"].partition_broadcast(P)).then_inc(sem("w_loaded"), 16)
                    later = [(W["win"], A["in_proj_w"].rearrange("(k p) f -> p k f", p=P)),
                             (W["wo"], A["out_proj_w"].rearrange("(k p) f -> p k f", p=P)),
                             (W["c0"], A["ssm_cols"]), (W["ob"], A["out_proj_b"].partition_broadcast(P)),
                             (W["lnw"], A["ln_w"].partition_broadcast(P)), (W["lnb"], A["ln_b"].partition_broadcast(P)),
                             (mask, A["c_mask"]), (slotsel, A["c_slot"]), (pick, A["c_pick"]), (cols, A["cols"]),
                             (rows16, A["rows16"]), (eb, A["eb"]), (bo_half, A["c_bo"].partition_broadcast(P)),
                             ]
                    later += [(dW[n], A[n].rearrange("(k p) f -> p k f", p=P)) for n in SLOT_W]
                    for dst, src in later:
                        sp.dma_start(dst[...], src).then_inc(sem("later_loaded"), 16)
                    sp.wait_ge(sem("later_loaded"), 16 * len(later))

            @block.scalar
            def _(act):
                if inst == 0:
                    act.wait_ge(sem("stats0"), NCH)
                root()
                act.wait_ge(sem("w_loaded"), 80)
                act.preload_act_table(ACT.Relu)
                if inst == 0:
                    act.sem_inc(sem("relu_done"), 4)

                def chunk(n, par):
                    for f in range(KF):
                        if f == 0:
                            act.wait_ge(sem("down_done"), b8 + n + 1)
                        act.wait_ge(sem("up_done"), (b8 + n) * KF + f + 1)
                        nc.scalar.activation(hT[:, f, :], ps[:, 2 + f % 4, :], ACT.Relu,
                                             bias=b1[:, f:f + 1]).then_inc(sem("relu_done"), 1)

                with act.Fori(0, NCH // 2) as i:
                    chunk(2 * i, 0)
                    chunk(2 * i + 1, 1)

            @block.tensor
            def _(pe):
                if inst == 0:
                    pe.wait_ge(sem("w_loaded"), 80)
                    pe.sem_inc(sem("down_done"), 1)

                def turn(n, par):
                    pe.wait_ge(sem("normed"), nbase + n + 1)
                    pe.wait_ge(sem("nT_ready"), base + n)
                    transposes(nbuf[:, par]).then_inc(sem("transposed"), 1)

                def chunk(n, par):
                    pe.wait_ge(sem("nT_ready"), base + n + 1)
                    for f in range(KF):
                        pe.wait_ge(sem("relu_done"), (b8 + n) * KF + f + 1)
                        for k in range(KD):
                            i = nc.tensor.matmul(ps[:, 2 + f % 4, :], w1[:, k, f * P:(f + 1) * P], nT[:, par, k, :],
                                                 start=(k == 0), stop=(k == KD - 1))
                        i.then_inc(sem("up_done"), 1)
                    turn(n + 1, 1 - par)
                    pe.wait_ge(sem("relu_done"), (b8 + n + 1) * KF + 4)
                    pe.wait_ge(sem("x_updated"), b8 + n)
                    for t in range(TPC):
                        for f in range(KF):
                            i = nc.tensor.matmul(ps[:, 6 + t // 2, (t % 2) * D:(t % 2 + 1) * D],
                                                 hT[:, f, t * P:(t + 1) * P], w2[:, f, :],
                                                 start=(f == 0), stop=(f == KF - 1))
                    i.then_inc(sem("down_done"), 1)

                turn(0, 0)
                with pe.Fori(0, NCH // 2) as i:
                    chunk(2 * i, 0)
                    chunk(2 * i + 1, 1)

            @block.vector
            def _(dve):
                if inst == 0:
                    s = Steps(dve, sem("dve_start"))
                    s.add(nc.vector.memset(eps[:, :], EPS))
                    s.add(nc.vector.memset(ones[:, :], 1.0))
                    s.add(nc.vector.memset(zeros[:, :], 0.0))
                    for n in range(NCH):
                        dve.wait_ge(x_sems[n], 16)
                        stats(dve, s, n)
                        s.wait()
                        dve.sem_inc(sem("stats0"), 1)
                    dve.wait_ge(sem("w_loaded"), 80)
                    s.add(nc.vector.tensor_scalar(b2h[:, :], b2h[:, :], 0.5, None, ALU.mult))
                    s.add(nc.vector.tensor_copy(identb[:, :], ident[:, :]))
                    s.wait()
                reciprocal_of_root(dve, 1 + 3 * inst)
                PER = 1 + STATS
                steps = Steps(dve, sem("ffn_dve"), b8 * PER)
                norm_tiles(nbuf[:, 0], 0).then_inc(sem("normed"), 1)

                def turned(n, par):
                    dve.wait_ge(sem("transposed"), base + n + 1)
                    nc.vector.tensor_copy(nT[:, par, :, :], ps[:, 0:2, :]).then_inc(sem("nT_ready"), 1)

                def chunk(n, par):
                    steps.at = (n + b8) * PER
                    dve.wait_ge(sem("transposed"), base + n)
                    norm_tiles(nbuf[:, 1 - par], (n + 1) % NCH).then_inc(sem("normed"), 1)
                    dve.wait_ge(sem("up_done"), (b8 + n) * KF)
                    turned(n + 1, 1 - par)
                    dve.wait_ge(sem("down_done"), b8 + n + 2)
                    xc = X[:, ds(n * TPC, TPC), :]
                    steps.wait()
                    nc.vector.scalar_tensor_tensor(xc, ps[:, 6:8, :].rearrange("p b (t d) -> p (b t) d", d=D),
                                                   0.5, xc, ALU.mult, ALU.add).then_inc(sem("x_updated"), 1)
                    dve.wait_ge(sem("x_updated"), b8 + n + 1)
                    steps.add(nc.vector.tensor_tensor(xc, xc, b2h[:, None, :].to_broadcast([P, TPC, D]), ALU.add))
                    stats(dve, steps, n)

                turned(0, 0)
                with dve.Fori(0, NCH // 2) as i:
                    chunk(2 * i, 0)
                    chunk(2 * i + 1, 1)


    def scan_layer(W):
        base, nbase = front
        front[0] += NCH + 1
        front[1] += NCH + 2
        nbuf, nT, win, wo, c0, ob, lnw, lnb = (W[k] for k in ("nbuf", "nT", "win", "wo", "c0", "ob", "lnw", "lnb"))
        BU, BV, W0, W1, W2, CB, LOGIT, SB, SC, SD = range(10)
        with ExitStack() as s2:
            uT = sb("uT", [P, NCH + 1, KD, CH], stack=s2)
            vT = sb("vT", [P, KD, T + 2], stack=s2)
            Hb = uT[:, 0:NCH, :, :].rearrange("p n k c -> p (n k c)").rearrange("p (n d) -> p n d", d=D)
            mvH = sb("mvH", [P, TILES, 2], stack=s2)
            rH = sb("rH", [P, TILES], stack=s2)
            decay = sb("decay", [P, KD], stack=s2)
            decays = sb("decays", [P, KD, CH], stack=s2)
            t1 = sb("t1", [P, CH], stack=s2)
            vl = W["hT"][:, 0:2, :]
            bv = W["hT"][:, 2:4, :]
            dv = W["hT"][:, 4:6, :]
            hs = W["hT"][:, 6:8, :]
            hl = sb("hl", [P, KD], stack=s2)
            y = hs
            oT = sb("oT", [P, 2, KD, CH], stack=s2)
            rn = sb("rn", [P, TPC, D], stack=s2)
            col = lambda j, k: c0[:, j, k:k + 1]
            with nc.Block() as block:
                @block.scalar
                def _(act):
                    root()
                    nc.scalar.activation(decay[:, :], c0[:, LOGIT, :], ACT.Sigmoid).then_inc(sem("decay_ready"), 1)
                    act.preload_act_table(ACT.Silu)

                    def project(n):
                        for k in range(KD):
                            act.wait_ge(sem("uv_done"), 2 * n + 1)
                            nc.scalar.activation(uT[:, ds(n, 1), k, :], ps[:, 2 + k:3 + k, :], ACT.Identity, bias=col(BU, k))
                        for k in range(KD):
                            act.wait_ge(sem("uv_done"), 2 * n + 2)
                            i = nc.scalar.activation(vT[:, k, ds((n % NCH) * CH + 1, CH)], ps[:, 4 + k, :], ACT.Silu, bias=col(BV, k))
                        i.then_inc(sem("uv_saved"), 1)

                    def turned(n, par):
                        act.wait_ge(sem("transposed"), base + n + 1)
                        nc.scalar.activation(nT[:, par, :, :], ps[:, 0:2, :], ACT.Copy).then_inc(sem("nT_ready"), 1)

                    def chunk(n, par):
                        turned(n + 1, 1 - par)
                        project(n + 1)
                        act.wait_ge(sem("y_ready"), n + 1)
                        nc.scalar.activation(y[:, :, :], y[:, :, :], ACT.Silu).then_inc(sem("gate_ready"), 1)

                    turned(0, 0)
                    project(0)
                    with act.Fori(0, NCH // 2) as i:
                        chunk(2 * i, 0)
                        chunk(2 * i + 1, 1)
                    act.wait_ge(sem("h_saved"), NCH)
                    root(mvH)

                @block.tensor
                def _(pe):
                    def turn(n, par):
                        pe.wait_ge(sem("normed"), nbase + n + 1)
                        pe.wait_ge(sem("nT_ready"), base + n)
                        transposes(nbuf[:, par]).then_inc(sem("transposed"), 1)

                    def project(n, par):
                        pe.wait_ge(sem("nT_ready"), base + n + 1)
                        pe.wait_ge(sem("uv_saved"), n)
                        for c in range(2 * KD):
                            for k in range(KD):
                                i = nc.tensor.matmul(ps[:, 2 + c, :], win[:, k, c * P:(c + 1) * P], nT[:, par, k, :],
                                                     start=(k == 0), stop=(k == KD - 1))
                            if c % KD == KD - 1:
                                i.then_inc(sem("uv_done"), 1)

                    def chunk(n, par):
                        turn(n + 1, 1 - par)
                        project(n + 1, 1 - par)
                        pe.wait_ge(sem("gated"), n + 1)
                        pe.wait_ge(sem("h_saved"), n)
                        for t in range(TPC):
                            for k in range(KD):
                                i = nc.tensor.matmul(ps[:, 6 + t // 2, (t % 2) * D:(t % 2 + 1) * D],
                                                     oT[:, par, k, t * P:(t + 1) * P], wo[:, k, :],
                                                     start=(k == 0), stop=(k == KD - 1))
                        i.then_inc(sem("wo_done"), 1)

                    turn(0, 0)
                    project(0, 0)
                    with pe.Fori(0, NCH // 2) as i:
                        chunk(2 * i, 0)
                        chunk(2 * i + 1, 1)

                @block.gpsimd
                def _(pool):
                    def chunk(n, par):
                        for k in range(KD):
                            pool.wait_ge(sem("conv_done"), 2 * n + k + 1)
                            pool.sem_inc(sem("conv_seen"), 1)
                            nc.gpsimd.tensor_scalar(bv[:, k, :], vl[:, k, :], col(SB, k), None, ALU.mult)
                            nc.gpsimd.tensor_scalar(dv[:, k, :], vl[:, k, :], col(SD, k), None, ALU.mult).then_inc(sem("bd_ready"), 1)
                        pool.wait_ge(sem("rn_ready"), n + 1)
                        nc.gpsimd.tensor_tensor(rn[:, :, :], rn[:, :, :], ob[:, None, :].to_broadcast([P, TPC, D]),
                                                ALU.add).then_inc(sem("rnb_ready"), 1)

                    with pool.Fori(0, NCH // 2) as i:
                        chunk(2 * i, 0)
                        chunk(2 * i + 1, 1)
                    pool.wait_ge(sem("h_saved"), NCH)
                    with pool.Fori(0, NCH) as n:
                        xc = X[:, ds(n * TPC, TPC), :]
                        nc.gpsimd.tensor_tensor(xc, xc, lnb[:, None, :].to_broadcast([P, TPC, D]), ALU.add).then_inc(sem("xb_ready"), 1)

                @block.vector
                def _(dve):
                    s = Steps(dve, sem("scan_start"))
                    s.add(nc.vector.memset(hl[:, :], 0.0))
                    s.add(nc.vector.memset(vT[:, :, 0:1], 0.0))
                    s.add(nc.vector.memset(vT[:, :, T + 1:T + 2], 0.0))
                    s.add(nc.vector.memset(decays[:, :, :], 1.0))
                    s.wait()
                    dve.wait_ge(sem("decay_ready"), 1)
                    for k in range(KD):
                        s.add(nc.vector.tensor_scalar(decays[:, k, :], decays[:, k, :], decay[:, k:k + 1], None, ALU.mult))
                    s.wait()
                    reciprocal_of_root(dve, 2)
                    norm_tiles(nbuf[:, 0], 0).then_inc(sem("normed"), 1)
                    norm_tiles(nbuf[:, 1], 1).then_inc(sem("normed"), 1)
                    PER = 8 + STATS
                    steps = Steps(dve, sem("scan_dve"))

                    def chunk(n, par):
                        steps.at = n * PER
                        dve.wait_ge(sem("uv_saved"), n + 2)
                        for k in range(KD):
                            v = lambda o: vT[:, k, ds(n * CH + o, CH)]
                            steps.wait()
                            steps.add(nc.vector.tensor_scalar(t1[:, :], v(0), col(W0, k), col(CB, k), ALU.mult, ALU.add))
                            steps.wait()
                            steps.add(nc.vector.scalar_tensor_tensor(t1[:, :], v(1), col(W1, k), t1[:, :], ALU.mult, ALU.add))
                            steps.wait()
                            dve.wait_ge(sem("bd_ready"), 2 * n)
                            nc.vector.scalar_tensor_tensor(vl[:, k, :], v(2), col(W2, k), t1[:, :], ALU.mult,
                                                           ALU.add).then_inc(sem("conv_done"), 1)
                            dve.wait_ge(sem("conv_done"), 2 * n + k + 1)
                        dve.wait_ge(sem("h_saved"), n)
                        norm_tiles(rn, n).then_inc(sem("rn_ready"), 1)
                        dve.wait_ge(sem("gated"), n)
                        for k in range(KD):
                            dve.wait_ge(sem("bd_ready"), 2 * n + k + 1)
                            steps.add(nc.vector.tensor_tensor_scan(hs[:, k, :], decays[:, k, :], bv[:, k, :], hl[:, k:k + 1],
                                                                   ALU.mult, ALU.add))
                        steps.wait()
                        steps.add(nc.vector.tensor_copy(hl[:, :], hs[:, :, CH - 1]))
                        steps.wait()
                        for k in range(KD):
                            i = nc.vector.scalar_tensor_tensor(y[:, k, :], hs[:, k, :], col(SC, k), dv[:, k, :], ALU.mult, ALU.add)
                        i.then_inc(sem("y_ready"), 1)
                        dve.wait_ge(sem("transposed"), base + n + 1)
                        norm_tiles(nbuf[:, par], (n + 2) % NCH).then_inc(sem("normed"), 1)
                        dve.wait_ge(sem("gate_ready"), n + 1)
                        dve.wait_ge(sem("wo_done"), n)
                        nc.vector.tensor_tensor(oT[:, par, :, :], y[:, :, :], uT[:, ds(n, 1), :, :].rearrange("p a k c -> p (a k) c"), ALU.mult).then_inc(sem("gated"), 1)
                        dve.wait_ge(sem("rnb_ready"), n + 1)
                        dve.wait_ge(sem("wo_done"), n + 1)
                        steps.add(nc.vector.tensor_tensor(Hb[:, ds(n * TPC, TPC), :], rn[:, :, :],
                                                          ps[:, 6:8, :].rearrange("p b (t d) -> p (b t) d", d=D), ALU.add))
                        stats(dve, steps, n, Hb, mvH)
                        steps.wait()
                        dve.sem_inc(sem("h_saved"), 1)

                    with dve.Fori(0, NCH // 2) as i:
                        chunk(2 * i, 0)
                        chunk(2 * i + 1, 1)

                    reciprocal_of_root(dve, 3, rH)
                    FPER = 3 + STATS
                    fin = Steps(dve, sem("scan_fin"))
                    with dve.Fori(0, NCH) as n:
                        fin.at = n * FPER
                        hc = Hb[:, ds(n * TPC, TPC), :]
                        xc = X[:, ds(n * TPC, TPC), :]
                        for t in range(TPC):
                            k = n * TPC + t
                            i = nc.vector.tensor_scalar(Hb[:, ds(k, 1), :], Hb[:, ds(k, 1), :], mvH[:, ds(k, 1), 0:1],
                                                        rH[:, ds(k, 1)], ALU.subtract, ALU.mult)
                        fin.add(i)
                        fin.wait()
                        fin.add(nc.vector.tensor_tensor(hc, hc, lnw[:, None, :].to_broadcast([P, TPC, D]), ALU.mult))
                        fin.wait()
                        dve.wait_ge(sem("xb_ready"), n + 1)
                        fin.add(nc.vector.tensor_tensor(xc, xc, hc, ALU.add))
                        stats(dve, fin, n)


    def slots(inst):
        n8 = inst * NCH
        first = inst == 0
        with ExitStack() as s3:
            ring = sb("ring", [P, RING, 4 * F], stack=s3)
            nbuf = sb("s_nbuf", [P, 2, TPC, D], stack=s3)
            nT = sb("s_nT", [P, 2, KD, CH], stack=s3)
            zs = sb("zs", [P, KD, PAIRS], stack=s3)
            rsum = sb("rsum", [P, 2], stack=s3)
            pool_pairs(inst, n8, first, ring, nbuf, nT, zs, rsum)
            xq = sb("xq", [P, KD, PAIRS], stack=s3)
            xb = sb("xb", [1, PAIRS], stack=s3)
            xm = sb("xm", [P, KD, D], stack=s3)
            experts(inst, ring, zs, rsum, xq, xb, xm)
            cross(inst, n8, nbuf, nT, xq, xb, xm)

    def unit_loads(sp, inst, units):
        for u in units:
            g, kind, half = u // 6, u // 2 % 3, u % 2
            use = inst * 4 * 6 + u
            if use >= RING:
                sp.wait_ge(sem("unit_used"), use - RING + 1)
            dst = ring_of[0][:, u % RING, :]
            if kind < 2:
                src = A[("e_W1", "e_Wg")[kind]].rearrange("(j g) (k p) f -> g k p j f", g=GROUPS, p=P)[g, half]
                sp.dma_start(dst.rearrange("p (j f) -> p j f", j=4), src).then_inc(sem(f"unit_loaded{u % RING}"), 16)
            else:
                src = A["e_W2"].rearrange("(j g) (h p c) d -> g h p j (c d)", g=GROUPS, h=2, c=4)[g, half]
                sp.dma_start(dst.rearrange("p (j f) -> p j f", j=4), src).then_inc(sem(f"unit_loaded{u % RING}"), 16)

    ring_of = [None]

    def pool_pairs(inst, n8, first, ring, nbuf, nT, zs, rsum):
        ring_of[0] = ring
        base, nbase = front
        front[0] += NCH + 1
        front[1] += 2 * NCH + 3
        with ExitStack() as s4:
            scores = sb("scores", [P, 2, T], stack=s4)
            prob = sb("prob", [P, 2, 2, CH], stack=s4)
            probT = sb("probT", [P, 2, TPC, PAIRS], stack=s4)
            mx8 = sb("mx8", [P, 2, NCH], stack=s4)
            mx = sb("mx", [P, 2], stack=s4)
            nb = sb("nb", [P, 2], stack=s4)
            sums = sb("sums", [P, 2, NCH], stack=s4)
            ssum = sb("ssum", [P, 2], stack=s4)
            sqT = sb("sqT", [P, KD, E], stack=s4)
            qb = prob[:, 0, :, 0:PAIRS]
            with nc.Block() as block:
                @block.sync
                def _(sp):
                    unit_loads(sp, inst, range(RING))

                @block.scalar
                def _(act):
                    root()
                    act.preload_act_table(ACT.Exp)

                    def turned(n, par):
                        act.wait_ge(sem("transposed"), base + n + 1)
                        nc.scalar.activation(nT[:, par, :, :], ps[:, 0:2, :], ACT.Copy).then_inc(sem("nT_ready"), 1)

                    def chunk(n, par):
                        turned(n + 1, 1 - par)
                        act.wait_ge(sem("pool_scored"), n8 + n + 1)
                        nc.scalar.activation(scores[:, :, ds(n * CH, CH)], ps[:, 2 + 2 * par:4 + 2 * par, :],
                                             ACT.Copy).then_inc(sem("scores_saved"), 1)

                    turned(0, 0)
                    with act.Fori(0, NCH // 2) as i:
                        chunk(2 * i, 0)
                        chunk(2 * i + 1, 1)

                    def weigh(n, par):
                        act.wait_ge(sem("prob_turned"), inst * (NCH + 1) + n)
                        for c in range(2):
                            i = nc.scalar.activation(prob[:, par, c, :], scores[:, c, ds((n % NCH) * CH, CH)], ACT.Exp,
                                                     bias=nb[:, c:c + 1], scale=SCALE, accum_out=sums[:, c, ds(n % NCH, 1)])
                        i.then_inc(sem("weighed"), 1)

                    act.wait_ge(sem("shift_ready"), inst + 1)
                    weigh(0, 0)
                    with act.Fori(0, NCH // 2) as i:
                        weigh(2 * i + 1, 1)
                        weigh(2 * i + 2, 0)

                @block.tensor
                def _(pe):
                    if first:
                        for k in range(KD):
                            i = nc.tensor.transpose(ps[:, 7, k * E:(k + 1) * E], rows16[:, 0, k * P:(k + 1) * P], ident[0:E, 0:E])
                        i.then_inc(sem("fold_pe"), 1)
                        pe.wait_ge(sem("fold_dve"), 1)
                        for c in range(KD):
                            for k in range(KD):
                                i = nc.tensor.matmul(ps[:, 6, c * E:(c + 1) * E], dW["d_Wq"][:, k, c * P:(c + 1) * P],
                                                     sqT[:, k, :], start=(k == 0), stop=(k == KD - 1))
                        i.then_inc(sem("fold_pe"), 1)
                        pe.wait_ge(sem("fold_dve"), 2)
                        for c in range(KD):
                            for k in range(KD):
                                i = nc.tensor.matmul(ps[:, 7, c * PAIRS:(c + 1) * PAIRS], dW["d_WkT"][:, k, c * P:(c + 1) * P],
                                                     qb[:, k, :], start=(k == 0), stop=(k == KD - 1))
                        for c in range(2):
                            for k in range(KD):
                                i = nc.tensor.matmul(ps[:, 6, c:c + 1], qb[:, k, c * P:(c + 1) * P], cols[:, 1, k:k + 1],
                                                     start=(k == 0), stop=(k == KD - 1))
                        i.then_inc(sem("fold_pe"), 1)
                        pe.wait_ge(sem("fold_dve"), 3)

                    def turn(n, par):
                        pe.wait_ge(sem("normed"), nbase + n + 1)
                        pe.wait_ge(sem("nT_ready"), base + n)
                        transposes(nbuf[:, par]).then_inc(sem("transposed"), 1)

                    def chunk(n, par):
                        turn(n + 1, 1 - par)
                        pe.wait_ge(sem("nT_ready"), base + n + 1)
                        pe.wait_ge(sem("scores_saved"), n8 + n)
                        for c in range(2):
                            for k in range(KD):
                                i = nc.tensor.matmul(ps[:, 2 + 2 * par + c, :], pool_q[:, k, c * P:(c + 1) * P],
                                                     nT[:, par, k, :], start=(k == 0), stop=(k == KD - 1))
                        i.then_inc(sem("pool_scored"), 1)

                    turn(0, 0)
                    with pe.Fori(0, NCH // 2) as i:
                        chunk(2 * i, 0)
                        chunk(2 * i + 1, 1)

                    def turn_probs(n, par):
                        pe.wait_ge(sem("weighed"), inst * (NCH + 1) + n + 1)
                        for t in range(TPC):
                            for c in range(2):
                                i = nc.tensor.transpose(ps[:, 2 + 2 * par + t // 2, (t % 2) * PAIRS + c * P:(t % 2) * PAIRS + (c + 1) * P],
                                                        prob[:, par, c, t * P:(t + 1) * P], ident[:, :])
                        i.then_inc(sem("prob_turned"), 1)

                    def pool(n, par):
                        pe.wait_ge(sem("probT_ready"), inst * (NCH + 1) + n + 1)
                        pe.wait_ge(sem("normed"), nbase + NCH + 2 + n + 1)
                        for t in range(TPC):
                            for c in range(KD):
                                i = nc.tensor.matmul(ps[:, 6 + c, 0:PAIRS], nbuf[:, par, t, c * P:(c + 1) * P], probT[:, par, t, :],
                                                     start=False, stop=False)
                        i.then_inc(sem("pooled"), 1)

                    for c in range(KD):
                        nc.tensor.matmul(ps[:, 6 + c, 0:PAIRS], ident[:, :], zeros[:, :], start=True, stop=False)
                    turn_probs(0, 0)
                    with pe.Fori(0, NCH // 2) as i:
                        turn_probs(2 * i + 1, 1)
                        pool(2 * i, 0)
                        turn_probs(2 * i + 2, 0)
                        pool(2 * i + 1, 1)
                    for c in range(KD):
                        i = nc.tensor.matmul(ps[:, 6 + c, 0:PAIRS], ident[:, :], zeros[:, :], start=False, stop=True)
                    i.then_inc(sem("pool_summed"), 1)

                @block.vector
                def _(dve):
                    s = Steps(dve, sem("pool_start"), inst * 5)
                    if first:
                        f = Steps(dve, sem("fold_step"))
                        dve.wait_ge(sem("fold_pe"), 1)
                        nc.vector.tensor_copy(sqT[:, :, :], ps[:, 7, 0:KD * E].rearrange("p (k e) -> p k e", k=KD)).then_inc(sem("fold_dve"), 1)
                        dve.wait_ge(sem("fold_pe"), 2)
                        for k in range(KD):
                            f.add(nc.vector.tensor_scalar(sqT[:, k, :], ps[:, 6, k * E:(k + 1) * E], cols[:, 0, k:k + 1], None, ALU.add))
                        f.wait()
                        for k in range(KD):
                            i = nc.vector.tensor_tensor(qb[:, k, :].rearrange("p (h s) -> p h s", h=H),
                                                        sqT[:, k, None, :].to_broadcast([P, H, E]),
                                                        mask[:, k, :, None].to_broadcast([P, H, E]), ALU.mult)
                        i.then_inc(sem("fold_dve"), 1)
                        dve.wait_ge(sem("fold_pe"), 3)
                        nc.vector.tensor_copy(pool_q[:, :, :], ps[:, 7, :].rearrange("p (k e) -> p k e", k=KD))
                        nc.vector.tensor_copy(pool_c[:, :], ps[:, 6, 0:2]).then_inc(sem("fold_dve"), 1)
                        dve.wait_ge(sem("fold_dve"), 3)
                    reciprocal_of_root(dve, 5 + inst * 2)
                    norm_tiles(nbuf[:, 0], 0).then_inc(sem("normed"), 1)
                    norm_tiles(nbuf[:, 1], 1).then_inc(sem("normed"), 1)

                    def chunk(n, par):
                        dve.wait_ge(sem("transposed"), base + n + 1)
                        norm_tiles(nbuf[:, par], (n + 2) % NCH).then_inc(sem("normed"), 1)
                        dve.wait_ge(sem("scores_saved"), n8 + n + 1)
                        nc.vector.tensor_reduce(mx8[:, :, ds(n, 1)], scores[:, :, ds(n * CH, CH)], AX.X, ALU.max).then_inc(sem("chunk_max"), 1)

                    with dve.Fori(0, NCH // 2) as i:
                        chunk(2 * i, 0)
                        chunk(2 * i + 1, 1)
                    dve.wait_ge(sem("chunk_max"), n8 + NCH)
                    s.add(nc.vector.tensor_reduce(mx[:, :], mx8[:, :, :], AX.X, ALU.max))
                    s.wait()
                    s.add(nc.vector.tensor_tensor(mx[:, :], mx[:, :], pool_c[:, :], ALU.add))
                    s.wait()
                    s.add(nc.vector.tensor_tensor(nb[:, :], pool_c[:, :], mx[:, :], ALU.subtract))
                    s.wait()
                    nc.vector.tensor_scalar(nb[:, :], nb[:, :], SCALE, None, ALU.mult).then_inc(sem("shift_ready"), 1)
                    dve.wait_ge(sem("transposed"), base + NCH + 1)
                    norm_tiles(nbuf[:, 0], 0).then_inc(sem("normed"), 1)

                    def evacuate(n, par):
                        dve.wait_ge(sem("prob_turned"), inst * (NCH + 1) + n + 1)
                        nc.vector.tensor_copy(probT[:, par, :, :], ps[:, 2 + 2 * par:4 + 2 * par, :].rearrange("p b (t e) -> p (b t) e", e=PAIRS)).then_inc(sem("probT_ready"), 1)

                    def pool(n, par):
                        dve.wait_ge(sem("pooled"), n8 + n)
                        norm_tiles(nbuf[:, 1 - par], (n + 1) % NCH).then_inc(sem("normed"), 1)
                        evacuate(n + 1, 1 - par)

                    evacuate(0, 0)
                    with dve.Fori(0, NCH // 2) as i:
                        pool(2 * i, 0)
                        pool(2 * i + 1, 1)
                    dve.wait_ge(sem("weighed"), (inst + 1) * (NCH + 1))
                    s.add(nc.vector.tensor_reduce(ssum[:, :], sums[:, :, :], AX.X, ALU.add))
                    s.wait()
                    s.add(nc.vector.reciprocal(rsum[:, :], ssum[:, :]))
                    dve.wait_ge(sem("pool_summed"), inst + 1)
                    nc.vector.tensor_copy(zs[:, :, :], ps[:, 6:8, 0:PAIRS])

    def experts(inst, ring, zs, rsum, xq, xb, xm):
        W = dW
        with ExitStack() as s5:
            rm = sb("rm", [P, 2, D], stack=s5)
            aT = sb("aT", [P, KD, E], stack=s5)
            o16 = sb("o16", [E, D], stack=s5)
            h16 = sb("h16", [E, D], stack=s5)
            s16 = sb("s16", [E, 6], stack=s5)
            m16 = sb("m16", [E, 2], stack=s5)
            r16 = sb("r16", [E, 1], stack=s5)
            hT = sb("e_hT", [P, KD, 32], stack=s5)
            ug = sb("ug", [P, 2, F], stack=s5)
            ua = sb("ua", [P, 2, KF, 4], stack=s5)
            ac = sb("ac", [P, KF, 4], stack=s5)
            ys = sb("ys", [P, F], stack=s5)
            y16 = sb("y16", [E, D], stack=s5)
            oT = sb("e_oT", [P, KD, E], stack=s5)
            kv = sb("kv", [P, 2, KD, E], stack=s5)
            kb = sb("kb", [P, 2, KD, PAIRS], stack=s5)
            a0, p0, v0, g0 = inst * 2, inst * 6, inst * 9, inst * GROUPS
            with nc.Block() as block:
                @block.sync
                def _(sp):
                    unit_loads(sp, inst, range(RING, UNITS))
                    sp.wait_ge(sem("y_rows"), inst + 1)
                    sp.dma_start(y16[:, :], ys[0:P:32, :].rearrange("j (g d) -> j g d", g=GROUPS)).then_inc(sem("y_loaded"), 16)

                @block.scalar
                def _(act):
                    act.wait_ge(sem("o_var"), inst + 1)
                    nc.scalar.activation(r16[:, :], m16[:, 1:2], ACT.Sqrt, bias=eps[0:E, :]).then_inc(sem("o_root"), 1)
                    act.preload_act_table(ACT.Silu)
                    for g in range(GROUPS):
                        act.wait_ge(sem("g_up"), g0 + g + 1)
                        act.wait_ge(sem("picked"), g0 + g)
                        nc.scalar.activation(ug[:, 1, :], ps[:, 2:4, :].rearrange("p b c -> p (b c)"), ACT.Copy).then_inc(sem("g_saved"), 1)
                        act.wait_ge(sem("biased"), g0 + g + 1)
                        nc.scalar.activation(ua[:, :, :, :], ua[:, :, :, :], ACT.Silu).then_inc(sem("silu_done"), 1)

                @block.tensor
                def _(pe):
                    for c in range(2):
                        for k in range(KD):
                            i = nc.tensor.matmul(ps[:, 0, c * D:(c + 1) * D], zs[:, k, c * P:(c + 1) * P], W["d_Wv"][:, k, :],
                                                 start=(k == 0), stop=(k == KD - 1))
                    i.then_inc(sem("slot_pe"), 1)
                    pe.wait_ge(sem("slot_dve"), v0 + 1)
                    for c in range(KD):
                        for k in range(2):
                            i = nc.tensor.matmul(ps[:, 1, c * E:(c + 1) * E], rm[:, k, c * P:(c + 1) * P], slotsel[:, :],
                                                 start=(k == 0), stop=(k == 1))
                    i.then_inc(sem("slot_pe"), 1)
                    pe.wait_ge(sem("slot_dve"), v0 + 2)
                    for k in range(KD):
                        i = nc.tensor.matmul(ps[0:E, 2, 0:D], aT[:, k, :], W["d_Wo"][:, k, :], start=(k == 0), stop=(k == KD - 1))
                    i.then_inc(sem("slot_pe"), 1)
                    pe.wait_ge(sem("slot_dve"), v0 + 3)
                    for k in range(KD):
                        i = nc.tensor.transpose(ps[:, 7, k * E:(k + 1) * E], h16[:, k * P:(k + 1) * P], ident[0:E, 0:E])
                    i.then_inc(sem("slot_pe"), 1)
                    pe.wait_ge(sem("slot_dve"), v0 + 4)
                    u = 0

                    def arrived():
                        before = inst * ((UNITS - u % RING + RING - 1) // RING)
                        pe.wait_ge(sem(f"unit_loaded{u % RING}"), 16 * (before + u // RING + 1))

                    for g in range(GROUPS):
                        for m in range(2):
                            if g or inst:
                                pe.wait_ge(sem(("u_saved", "g_saved")[m]), g0 + g)
                            for k in range(KD):
                                arrived()
                                for b in range(2):
                                    for j in range(4):
                                        i = nc.tensor.matmul(ps[32 * j:32 * j + 32, 2 * m + b, :], hT[:, k, :],
                                                             ring[:, u % RING, j * F + b * CH:j * F + (b + 1) * CH],
                                                             start=(k == 0), stop=(k == KD - 1))
                                if k == 0:
                                    i.then_inc(sem("unit_used"), 1)
                                u += 1
                            i.then_inc(sem("unit_used"), 1)
                            pe.wait_ge(sem("unit_used"), inst * UNITS + u)
                            pe.sem_inc(sem(("u_up", "g_up")[m]), 1)
                        pe.wait_ge(sem("u_saved"), g0 + g + 1)
                        pe.wait_ge(sem("g_saved"), g0 + g + 1)
                        for m in range(2):
                            for f in range(KF):
                                at = (f // 4) * CH + f % 4
                                i = nc.tensor.matmul(ps[:, 4, (m * KF + f) * 4:(m * KF + f + 1) * 4],
                                                     ug[:, m, at:at + 4 * (P - 1) + 1:4], pick[:, g, :], start=True, stop=True)
                        i.then_inc(sem("picked"), 1)
                        pe.wait_ge(sem("gated16"), g0 + g + 1)
                        for half in range(2):
                            arrived()
                            for c in range(4):
                                for j in range(4):
                                    i = nc.tensor.matmul(ps[32 * j:32 * j + 1, 5 + g // 2, (g % 2) * D:(g % 2 + 1) * D],
                                                         ac[:, 4 * half + c, j:j + 1],
                                                         ring[:, u % RING, j * F + c * D:j * F + (c + 1) * D],
                                                         start=(half + c == 0), stop=(half + c == 4))
                            i.then_inc(sem("unit_used"), 1)
                            u += 1
                    pe.wait_ge(sem("slot_dve"), v0 + 5)
                    for k in range(KD):
                        i = nc.tensor.transpose(ps[:, 7, k * E:(k + 1) * E], o16[:, k * P:(k + 1) * P], ident[0:E, 0:E])
                    i.then_inc(sem("slot_pe"), 1)
                    pe.wait_ge(sem("slot_dve"), v0 + 6)
                    for m, name in enumerate(("c_Wk", "c_Wv")):
                        for c in range(KD):
                            for k in range(KD):
                                i = nc.tensor.matmul(ps[:, 0, (m * KD + c) * E:(m * KD + c + 1) * E], W[name][:, k, c * P:(c + 1) * P],
                                                     oT[:, k, :], start=(k == 0), stop=(k == KD - 1))
                    i.then_inc(sem("slot_pe"), 1)
                    pe.wait_ge(sem("slot_dve"), v0 + 8)
                    for c in range(KD):
                        for k in range(KD):
                            nc.tensor.matmul(ps[:, 1, c * PAIRS:(c + 1) * PAIRS], W["c_WqT"][:, k, c * P:(c + 1) * P],
                                             kb[:, 0, k, :], start=(k == 0), stop=(k == KD - 1))
                    for k in range(KD):
                        nc.tensor.matmul(ps[0:1, 2, 0:PAIRS], cols[:, 3, k:k + 1], kb[:, 0, k, :], start=(k == 0), stop=(k == KD - 1))
                    for c in range(2):
                        for k in range(KD):
                            i = nc.tensor.matmul(ps[:, 3, c * D:(c + 1) * D], kb[:, 1, k, c * P:(c + 1) * P], W["c_Wo"][:, k, :],
                                                 start=(k == 0), stop=(k == KD - 1))
                    i.then_inc(sem("folded"), 1)

                @block.vector
                def _(dve):
                    s = Steps(dve, sem("slot_step"), inst * 7)
                    dve.wait_ge(sem("slot_pe"), p0 + 1)
                    for c in range(2):
                        i = nc.vector.scalar_tensor_tensor(rm[:, c, :].rearrange("p (h d) -> p h d", h=H),
                                                           ps[:, 0, c * D:(c + 1) * D].rearrange("p (h d) -> p h d", h=H),
                                                           rsum[:, c:c + 1], mask[:, c, :, None].to_broadcast([P, H, HD]),
                                                           ALU.mult, ALU.mult)
                    i.then_inc(sem("slot_dve"), 1)
                    dve.wait_ge(sem("slot_pe"), p0 + 2)
                    for k in range(KD):
                        i = nc.vector.tensor_scalar(aT[:, k, :], ps[:, 1, k * E:(k + 1) * E], cols[:, 2, k:k + 1], None, ALU.add)
                    i.then_inc(sem("slot_dve"), 1)
                    dve.wait_ge(sem("slot_pe"), p0 + 3)
                    s.add(nc.vector.tensor_tensor(o16[:, :], ps[0:E, 2, 0:D], rows16[:, 1, :], ALU.add))
                    s.wait()
                    s.add(nc.vector.tensor_tensor(o16[:, :], o16[:, :], rows16[:, 0, :], ALU.add))
                    s.wait()
                    s.add(nc.vector.bn_stats(s16[:, :], o16[:, :]))
                    s.wait()
                    nc.vector.bn_aggr(m16[:, :], s16[:, :]).then_inc(sem("o_var"), 1)
                    dve.wait_ge(sem("o_root"), inst + 1)
                    s.add(nc.vector.reciprocal(r16[:, :], r16[:, :]))
                    s.wait()
                    s.add(nc.vector.tensor_scalar(h16[:, :], o16[:, :], m16[:, 0:1], r16[:, :], ALU.subtract, ALU.mult))
                    s.wait()
                    s.add(nc.vector.tensor_tensor(h16[:, :], h16[:, :], rows16[:, 2, :], ALU.mult))
                    s.wait()
                    nc.vector.tensor_tensor(h16[:, :], h16[:, :], rows16[:, 3, :], ALU.add).then_inc(sem("slot_dve"), 1)
                    dve.wait_ge(sem("slot_pe"), p0 + 4)
                    hp = ps[:, 7, 0:KD * E].rearrange("p (k e) -> p k e", k=KD)
                    nc.vector.tensor_copy(hT[:, :, 0:E], hp)
                    nc.vector.tensor_copy(hT[:, :, E:2 * E], hp).then_inc(sem("slot_dve"), 1)
                    for g in range(GROUPS):
                        dve.wait_ge(sem("u_up"), g0 + g + 1)
                        dve.wait_ge(sem("picked"), g0 + g)
                        nc.vector.tensor_copy(ug[:, 0, :], ps[:, 0:2, :].rearrange("p b c -> p (b c)")).then_inc(sem("u_saved"), 1)
                        dve.wait_ge(sem("picked"), g0 + g + 1)
                        nc.vector.tensor_tensor(ua[:, :, :, :].rearrange("p m f j -> p m (f j)"),
                                                ps[:, 4, 0:2 * KF * 4].rearrange("p (m x) -> p m x", m=2),
                                                eb[:, :, g, :, :].rearrange("p m f j -> p m (f j)"), ALU.add).then_inc(sem("biased"), 1)
                        dve.wait_ge(sem("silu_done"), g0 + g + 1)
                        nc.vector.tensor_tensor(ac[:, :, :], ua[:, 0, :, :], ua[:, 1, :, :], ALU.mult).then_inc(sem("gated16"), 1)
                    dve.wait_ge(sem("unit_used"), (inst + 1) * UNITS)
                    for j in range(4):
                        i = nc.vector.tensor_copy(ys[32 * j:32 * j + 1, :], ps[32 * j:32 * j + 1, 5:7, :].rearrange("p b c -> p (b c)"))
                    i.then_inc(sem("y_rows"), 1)
                    s.add(nc.vector.tensor_tensor(o16[:, :], o16[:, :], rows16[:, 4, :], ALU.add))
                    s.wait()
                    dve.wait_ge(sem("y_loaded"), 16 * (inst + 1))
                    nc.vector.tensor_tensor(o16[:, :], o16[:, :], y16[:, :], ALU.add).then_inc(sem("slot_dve"), 1)
                    dve.wait_ge(sem("slot_pe"), p0 + 5)
                    nc.vector.tensor_copy(oT[:, :, :], hp).then_inc(sem("slot_dve"), 1)
                    dve.wait_ge(sem("slot_pe"), p0 + 6)
                    for m in range(2):
                        for k in range(KD):
                            i = nc.vector.tensor_scalar(kv[:, m, k, :], ps[:, 0, (m * KD + k) * E:(m * KD + k + 1) * E],
                                                        cols[:, 4 + m, k:k + 1], None, ALU.add)
                    i.then_inc(sem("slot_dve"), 1)
                    dve.wait_ge(sem("slot_dve"), v0 + 7)
                    for m in range(2):
                        for k in range(KD):
                            i = nc.vector.tensor_tensor(kb[:, m, k, :].rearrange("p (h s) -> p h s", h=H),
                                                        kv[:, m, k, None, :].to_broadcast([P, H, E]),
                                                        mask[:, k, :, None].to_broadcast([P, H, E]), ALU.mult)
                    i.then_inc(sem("slot_dve"), 1)
                    dve.wait_ge(sem("folded"), inst + 1)
                    nc.vector.tensor_copy(xq[:, :, :], ps[:, 1, :].rearrange("p (k e) -> p k e", k=KD))
                    nc.vector.tensor_copy(xb[:, :], ps[0:1, 2, 0:PAIRS])
                    nc.vector.tensor_copy(xm[:, :, :], ps[:, 3, :].rearrange("p (k e) -> p k e", k=KD)).then_inc(sem("slot_dve"), 1)

    def cross(inst, n8, nbuf, nT, xq, xb, xm):
        base, nbase = front
        front[0] += NCH + 1
        front[1] += NCH + 2
        with ExitStack() as s6:
            pr = sb("pr", [P, 2, TPC, H, E], stack=s6)
            prT = sb("prT", [P, TPC, 2, P], stack=s6)
            mxh = sb("mxh", [P, TPC * H], stack=s6)
            smh = sb("smh", [P, TPC * H], stack=s6)
            flat = [pr[:, par, :, :, :].rearrange("p t h s -> p (t h) s") for par in range(2)]
            sbank = ps[:, 2:4, :].rearrange("p b (t s) -> p (b t) s", s=E)

            def steps_of(engine, step):
                for n in range(2):
                    step(n, n, False)
                with engine.Fori(1, NCH // 2 - 1) as i:
                    step(2 * i, 0, False)
                    step(2 * i + 1, 1, False)
                for n in range(NCH - 2, NCH):
                    step(n, n % 2, True)

            with nc.Block() as block:
                if inst == 1:
                    @block.sync
                    def _(sp):
                        ov = out.rearrange("a (n p) d -> (a p) n d", p=P)
                        for n in range(NCH):
                            sp.wait_ge(sem("xx_updated"), n8 + n + 1)
                            sp.dma_start(ov[:, n * TPC:(n + 1) * TPC, :], X[:, n * TPC:(n + 1) * TPC, :]).then_inc(sem("stored"), 16)
                        sp.wait_ge(sem("stored"), 16 * NCH)

                @block.gpsimd
                def _(pool):
                    pool.wait_ge(sem("bo_step"), 1)
                    with pool.Fori(0, NCH) as n:
                        pool.wait_ge(sem("normed"), nbase + n + 1)
                        xc = X[:, ds(n * TPC, TPC), :]
                        nc.gpsimd.tensor_tensor(xc, xc, bo_half[:, None, :].to_broadcast([P, TPC, D]), ALU.add).then_inc(sem("xbias_added"), 1)

                @block.scalar
                def _(act):
                    act.preload_act_table(ACT.Exp)

                    def turned(n, par):
                        act.wait_ge(sem("transposed"), base + n + 1)
                        nc.scalar.activation(nT[:, par, :, :], ps[:, 0:2, :], ACT.Copy).then_inc(sem("nT_ready"), 1)

                    def weigh(n, par):
                        act.wait_ge(sem("x_shifted"), n8 + n + 1)
                        nc.scalar.activation(pr[:, par], pr[:, par], ACT.Exp, scale=SCALE).then_inc(sem("x_exp"), 1)

                    def step(n, par, tail):
                        if not (tail and n == NCH - 1):
                            weigh(n + 1, 1 - par)
                        act.wait_ge(sem("pr_turned"), n8 + n + 1)
                        act.wait_ge(sem("x_out"), n8 + n)
                        nc.scalar.activation(prT[:, :, :, :], ps[:, 4:6, :], ACT.Copy).then_inc(sem("prT_ready"), 1)
                        if not tail:
                            turned(n + 3, 1 - par)

                    for n in range(2):
                        turned(n, n)
                    weigh(0, 0)
                    turned(2, 0)
                    steps_of(act, step)

                @block.tensor
                def _(pe):
                    def turn(n, par):
                        pe.wait_ge(sem("normed"), nbase + n + 1)
                        pe.wait_ge(sem("nT_ready"), base + n)
                        transposes(nbuf[:, par]).then_inc(sem("transposed"), 1)

                    def score(n, par):
                        pe.wait_ge(sem("nT_ready"), base + n + 1)
                        pe.wait_ge(sem("x_shifted"), n8 + n)
                        for t in range(TPC):
                            o = ps[:, 2 + t // 2, (t % 2) * PAIRS:(t % 2 + 1) * PAIRS]
                            for k in range(KD):
                                nc.tensor.matmul(o, nT[:, par, k, t * P:(t + 1) * P], xq[:, k, :], start=(k == 0), stop=False)
                            i = nc.tensor.matmul(o, ones[:, :], xb[:, :], start=False, stop=True)
                        i.then_inc(sem("x_scored"), 1)

                    def step(n, par, tail):
                        if not tail:
                            score(n + 2, par)
                        pe.wait_ge(sem("pr_ready"), n8 + n + 1)
                        pe.wait_ge(sem("prT_ready"), n8 + n)
                        for t in range(TPC):
                            for c in range(2):
                                i = nc.tensor.transpose(ps[:, 4 + t // 2, (t % 2) * 2 * P + c * P:(t % 2) * 2 * P + (c + 1) * P],
                                                        pr[:, par, t, 8 * c:8 * c + 8, :].rearrange("p h s -> p (h s)"), ident[:, :])
                        i.then_inc(sem("pr_turned"), 1)
                        if not tail:
                            turn(n + 3, 1 - par)
                        pe.wait_ge(sem("prT_ready"), n8 + n + 1)
                        pe.wait_ge(sem("xx_updated"), n8 + n)
                        for t in range(TPC):
                            for c in range(2):
                                i = nc.tensor.matmul(ps[:, 6 + t // 2, (t % 2) * D:(t % 2 + 1) * D], prT[:, t, c, :], xm[:, c, :],
                                                     start=(c == 0), stop=(c == 1))
                        i.then_inc(sem("x_out"), 1)

                    turn(0, 0)
                    turn(1, 1)
                    score(0, 0)
                    turn(2, 0)
                    score(1, 1)
                    steps_of(pe, step)

                @block.vector
                def _(dve):
                    if inst == 0:
                        nc.vector.tensor_scalar(bo_half[:, :], bo_half[:, :], 0.5, None, ALU.mult).then_inc(sem("bo_step"), 1)
                    steps = Steps(dve, sem("x_step"))
                    sums = Steps(dve, sem("x_sum_step"))

                    def norm(n, par):
                        norm_tiles(nbuf[:, par], n % NCH).then_inc(sem("normed"), 1)

                    def shift(n, par):
                        dve.wait_ge(sem("x_scored"), n8 + n + 1)
                        dve.wait_ge(sem("x_shifted"), n8 + n)
                        nc.vector.tensor_reduce(mxh[:, :], sbank, AX.X, ALU.max).then_inc(sem("x_max"), 1)
                        dve.wait_ge(sem("x_max"), n8 + n + 1)
                        nc.vector.tensor_tensor(flat[par], sbank, mxh[:, :, None].to_broadcast([P, TPC * H, E]), ALU.subtract).then_inc(sem("x_shifted"), 1)

                    def update(n):
                        dve.wait_ge(sem("x_out"), n8 + n + 1)
                        dve.wait_ge(sem("xbias_added"), n8 + n + 1)
                        xc = X[:, ds(n * TPC, TPC), :]
                        nc.vector.scalar_tensor_tensor(xc, ps[:, 6:8, :].rearrange("p b (t d) -> p (b t) d", d=D),
                                                       0.5, xc, ALU.mult, ALU.add).then_inc(sem("xx_updated"), 1)
                        if inst == 0:
                            dve.wait_ge(sem("xx_updated"), n8 + n + 1)
                            steps.at = n * STATS
                            stats(dve, steps, n)

                    def step(n, par, tail):
                        if not (tail and n == NCH - 1):
                            dve.wait_ge(sem("pr_turned"), n8 + n)
                            shift(n + 1, 1 - par)
                        dve.wait_ge(sem("x_exp"), n8 + n + 1)
                        dve.wait_ge(sem("pr_ready"), n8 + n)
                        sums.at = (n8 + n) * 2
                        sums.add(nc.vector.tensor_reduce(smh[:, :], flat[par], AX.X, ALU.add))
                        sums.wait()
                        sums.add(nc.vector.reciprocal(smh[:, :], smh[:, :]))
                        sums.wait()
                        nc.vector.tensor_tensor(flat[par], flat[par], smh[:, :, None].to_broadcast([P, TPC * H, E]), ALU.mult).then_inc(sem("pr_ready"), 1)
                        if not (isinstance(n, int) and n == 0):
                            update(n - 1)
                        if not tail:
                            dve.wait_ge(sem("transposed"), base + n + 3)
                            norm(n + 4, par)

                    norm(0, 0)
                    norm(1, 1)
                    dve.wait_ge(sem("transposed"), base + 1)
                    norm(2, 0)
                    shift(0, 0)
                    dve.wait_ge(sem("transposed"), base + 2)
                    norm(3, 1)
                    steps_of(dve, step)
                    update(NCH - 1)

    def attention():
        with ExitStack() as s7:
            wout = sb("wout", [P, KD, D], stack=s7)
            bout = sb("bout", [P, D], stack=s7)
            V = sb("V", [P, KT, D], stack=s7)
            parts = nc.dram_tensor("qk_parts", (2, SPLITS, D, T), bf16, kind="Internal").ap()
            project(wout, bout, V, parts)
            O = sb("O", [P, ROUNDS + 1, TPC, NCH // 2, HD], stack=s7)
            attend(V, O, parts)
            project_out(wout, bout, O)

    def project(wout, bout, V, parts):
        base, nbase = front
        front[0] += NCH + 1
        front[1] += NCH + 1
        with ExitStack() as s8:
            wqkv = sb("wqkv", [P, KD, 5 * D], stack=s8)
            nbuf = sb("p_nbuf", [P, 2, TPC, D], stack=s8)
            nT = sb("p_nT", [P, 2, KD, CH], stack=s8)
            rope = sb("rope", [P, 2, 2, CH], stack=s8)
            ta = sb("ta", [P, 2, CH], stack=s8)
            tb = sb("tb", [P, 2, CH], stack=s8)
            part = sb("part", [P, 2, SPLITS, CH], bf16, stack=s8)
            ITEMS = 4
            with nc.Block() as block:
                @block.sync
                def _(sp):
                    for dst, src in ((wqkv, A["wqkv"].rearrange("(k p) f -> p k f", p=P)),
                                     (wout, A["woutT"].rearrange("(k p) f -> p k f", p=P)),
                                     (bout, A["b_out"].partition_broadcast(P))):
                        sp.dma_start(dst[...], src).then_inc(sem("qkv_loaded"), 16)

                    def chunk(n, par):
                        sp.wait_ge(sem("rotated"), (n - 1) * ITEMS) if not isinstance(n, int) or n > 1 else None
                        sp.dma_start(rope[:, par, :, :], A["c_rope"][:, :, ds(n * CH, CH)]).then_inc(sem(f"rope_loaded{par}"), 16)

                    def stores(n):
                        for m in range(ITEMS):
                            sp.wait_ge(sem("split_done"), n * ITEMS + m + 1)
                            sp.dma_start(parts[m // 2, :, (m % 2) * P:(m % 2 + 1) * P, ds(n * CH, CH)].rearrange("s p c -> p s c"),
                                         part[:, m % 2, :, :]).then_inc(sem(f"part_stored{m % 2}"), 16)

                    chunk(0, 0)
                    chunk(1, 1)
                    with sp.Fori(0, NCH // 2 - 1) as i:
                        stores(2 * i)
                        chunk(2 * i + 2, 0)
                        stores(2 * i + 1)
                        chunk(2 * i + 3, 1)
                    stores(NCH - 2)
                    stores(NCH - 1)
                    for m in range(2):
                        sp.wait_ge(sem(f"part_stored{m}"), 16 * NCH * ITEMS // 2)

                @block.scalar
                def _(act):
                    root()

                    def turned(n, par):
                        act.wait_ge(sem("transposed"), base + n + 1)
                        nc.scalar.activation(nT[:, par, :, :], ps[:, 0:2, :], ACT.Copy).then_inc(sem("nT_ready"), 1)

                    def chunk(n, par):
                        turned(n + 1, 1 - par)
                        act.wait_ge(sem("v_done"), n + 1)
                        nc.scalar.activation(V[:, ds(n * TPC, TPC), :], ps[:, 6:8, :].rearrange("p b (t d) -> p (b t) d", d=D),
                                             ACT.Copy).then_inc(sem("v_saved"), 1)

                    turned(0, 0)
                    with act.Fori(0, NCH // 2) as i:
                        chunk(2 * i, 0)
                        chunk(2 * i + 1, 1)

                @block.tensor
                def _(pe):
                    def turn(n, par):
                        pe.wait_ge(sem("normed"), nbase + n + 1)
                        pe.wait_ge(sem("nT_ready"), base + n)
                        transposes(nbuf[:, par]).then_inc(sem("transposed"), 1)

                    def chunk(n, par):
                        turn(n + 1, 1 - par)
                        pe.wait_ge(sem("nT_ready"), base + n + 1)
                        pe.wait_ge(sem("v_saved"), n)
                        for t in range(TPC):
                            for k in range(KD):
                                i = nc.tensor.matmul(ps[:, 6 + t // 2, (t % 2) * D:(t % 2 + 1) * D],
                                                     nT[:, par, k, t * P:(t + 1) * P], wqkv[:, k, 2 * D:3 * D],
                                                     start=(k == 0), stop=(k == KD - 1))
                        i.then_inc(sem("v_done"), 1)
                        for m in range(ITEMS):
                            pe.wait_ge(sem("banks_read"), n * ITEMS + m + 1)
                            for b in range(2):
                                at = 3 * D * b + m * P
                                for k in range(KD):
                                    i = nc.tensor.matmul(ps[:, 2 + 2 * (m % 2) + b, :], wqkv[:, k, at:at + P], nT[:, par, k, :],
                                                         start=(k == 0), stop=(k == KD - 1))
                            i.then_inc(sem("qk_done"), 1)

                    pe.wait_ge(sem("qkv_loaded"), 48)
                    turn(0, 0)
                    with pe.Fori(0, NCH // 2) as i:
                        chunk(2 * i, 0)
                        chunk(2 * i + 1, 1)

                @block.gpsimd
                def _(pool):
                    with pool.Fori(0, NCH * ITEMS // 2) as i:
                        for b in range(2):
                            pool.wait_ge(sem("middle_done"), 2 * i + b + 1)
                            nc.gpsimd.tensor_tensor(part[:, b, 2, :], tb[:, b, :], part[:, b, 1, :], ALU.subtract).then_inc(sem("split_done"), 1)

                @block.vector
                def _(dve):
                    dve.sem_inc(sem("banks_read"), 2)
                    reciprocal_of_root(dve, 6)
                    PER = 4 * ITEMS
                    steps = Steps(dve, sem("rot_step"))
                    norm_tiles(nbuf[:, 0], 0).then_inc(sem("normed"), 1)

                    def chunk(n, par):
                        steps.at = n * PER
                        dve.wait_ge(sem("transposed"), base + n)
                        norm_tiles(nbuf[:, 1 - par], (n + 1) % NCH).then_inc(sem("normed"), 1)
                        dve.wait_ge(sem(f"rope_loaded{par}"), 16 * (n // 2) + 16)
                        for m in range(ITEMS):
                            b = m % 2
                            scale = SCALE if m < 2 else 1.0
                            dve.wait_ge(sem("qk_done"), n * ITEMS + m + 1)
                            dve.wait_ge(sem("split_done"), n * ITEMS + m - 1) if m else None
                            dve.wait_ge(sem(f"part_stored{b}"), 32 * n + 16 * (m // 2))
                            steps.add(nc.vector.scalar_tensor_tensor(ta[:, b, :], ps[:, 2 + 2 * b, :], scale, rope[:, par, 0, :], ALU.mult, ALU.mult))
                            nc.vector.scalar_tensor_tensor(tb[:, b, :], ps[:, 3 + 2 * b, :], scale, rope[:, par, 1, :],
                                                           ALU.mult, ALU.mult).then_inc(sem("banks_read"), 1)
                            steps.wait()
                            dve.wait_ge(sem("banks_read"), n * ITEMS + m + 3)
                            nc.vector.tensor_tensor(ta[:, b, :], ta[:, b, :], tb[:, b, :], ALU.add).then_inc(sem("rotated"), 1)
                            dve.wait_ge(sem("rotated"), n * ITEMS + m + 1)
                            steps.add(nc.vector.tensor_copy(part[:, b, 0, :], ta[:, b, :]))
                            steps.wait()
                            steps.add(nc.vector.tensor_tensor(tb[:, b, :], ta[:, b, :], part[:, b, 0, :], ALU.subtract))
                            steps.wait()
                            steps.add(nc.vector.tensor_copy(part[:, b, 1, :], tb[:, b, :]))
                            steps.wait()
                            dve.sem_inc(sem("middle_done"), 1)

                    with dve.Fori(0, NCH // 2) as i:
                        chunk(2 * i, 0)
                        chunk(2 * i + 1, 1)

    def attend(V, O, parts):
        SC, AV, MB = 0, 4, 5
        SLOT0 = 2 * MAXES + 2
        QL = 2 * TERMS * 16
        with ExitStack() as s9:
            qop = sb("qop", [ROWS, 3, T], bf16, stack=s9)
            kop = sb("kop", [ROWS, 3, T], bf16, stack=s9)
            vst = sb("vst", [P, KT, 32], stack=s9)
            pb = sb("pb", [P, PRING, CH], stack=s9)
            osb = sb("osb", [P, CH], stack=s9)
            mp = sb("mp", [P, HALF // P, NCH], stack=s9)
            mq = sb("mq", [P, HALF // P], stack=s9)
            mr = sb("mr", [P, HALF // P], stack=s9)
            ms = sb("ms", [P, SPLITS, HALF // P], bf16, stack=s9)
            msb = sb("msb", [SPLITS * HALF // P, P], bf16, stack=s9)
            rc = sb("rc", [P, 2, 2, 4], stack=s9)
            psb = ps[:, :, :].bitcast(bf16)

            with nc.Block() as block:
                @block.sync
                def _(sp):
                    def load(h, b):
                        for r in range(TERMS):
                            at = slice(r * HD, (r + 1) * HD)
                            sp.dma_start(qop[at, ds(b, 1), :], parts[0, Q_PART[r], ds(h * HD, HD), :][:, None, :]).then_inc(sem("head_loaded"), 16)
                            sp.dma_start(kop[at, ds(b, 1), :], parts[1, K_PART[r], ds(h * HD, HD), :][:, None, :]).then_inc(sem("head_loaded"), 16)

                    def shift_rows(event, b, half):
                        sp.wait_ge(sem("rows_ready"), event + 1)
                        for r in range(SPLITS):
                            n = HALF // P
                            sp.dma_start(qop[QK_ROWS + r:QK_ROWS + r + 1, ds(b, 1), half * HALF:(half + 1) * HALF].rearrange("r a (t q) -> r (a t) q", q=P),
                                         msb[r * n:(r + 1) * n, :]).then_inc(sem("rows_loaded"), 16)

                    load(0, 0)
                    sp.wait_ge(sem("head_loaded"), QL)
                    load(1, 1)
                    shift_rows(0, 0, 0)

                    def rows(h):
                        shift_rows(2 * h + 1, h % 3, 1)
                        shift_rows(2 * h + 2, (h + 1) % 3, 0)

                    with sp.Fori(0, H - 2) as h:
                        sp.wait_ge(sem("av_done"), 2 * KT * h + 2)
                        sp.wait_ge(sem("head_loaded"), QL * (h + 2))
                        load(h + 2, (h + 2) % 3)
                        rows(h)
                    sp.wait_ge(sem("head_loaded"), QL * H)
                    sp.sem_inc(sem("head_loaded"), QL)
                    with sp.Fori(H - 2, H) as h:
                        rows(h)
                    sp.wait_ge(sem("rows_loaded"), 16 * SPLITS * (ROUNDS + 1))

                @block.scalar
                def _(act):
                    act.sem_inc(sem("exp_done"), 4)
                    act.preload_act_table(ACT.Exp)

                    def save(it):
                        act.wait_ge(sem("av_done"), KT * it + 2)
                        act.wait_ge(sem("slot_done"), SLOT0 - SLOTS + SLOTS * it + 10)
                        nc.scalar.activation(osb[:, :], ps[:, AV, :], ACT.Copy).then_inc(sem("o_saved"), 1)

                    act.wait_ge(sem("av_cleared"), 1)
                    with act.Fori(0, ROUNDS) as it:
                        for kt in range(KT):
                            act.wait_ge(sem("av_done"), it * KT + kt + 1)
                            for j in range(4):
                                act.wait_ge(sem("score_done"), 4 * KT * it + 4 * kt + j + 1)
                                nc.scalar.activation(pb[:, (4 * kt + j) % PRING, :], ps[:, SC + j, :], ACT.Exp).then_inc(sem("exp_done"), 1)
                            if kt == 0:
                                save(it)
                    save(ROUNDS)

                @block.gpsimd
                def _(pool):
                    s = Steps(pool, sem("v_init"))
                    for b in range(3):
                        s.add(nc.gpsimd.memset(kop[QK_ROWS:ROWS, b, :], 1.0))
                        s.wait()
                    s.add(nc.gpsimd.memset(pb[:, 0, :], 1.0))
                    s.add(nc.gpsimd.memset(vst[:, :, :], 0.0))
                    s.wait()
                    s.add(nc.gpsimd.memset(vst[:, :, HD:HD + 1], 1.0))
                    s.wait()

                    def copy(h, g):
                        nc.gpsimd.tensor_copy(vst[:, 8 * g:8 * g + 8, 0:HD], V[:, 8 * g:8 * g + 8, ds(h * HD, HD)]).then_inc(sem("v_ready"), 1)

                    for g in range(4):
                        copy(0, g)
                    with pool.Fori(0, H - 1) as h:
                        for g in range(4):
                            pool.wait_ge(sem("av_done"), (2 * h + 1) * KT + 8 * (g + 1) + 2)
                            copy(h + 1, g)

                @block.tensor
                def _(pe):
                    pe.sem_inc(sem("av_done"), 2)

                    def max_slot(slot0, k, b, m, half):
                        slot = slot0 + k
                        pe.wait_ge(sem("slot_used"), slot + 1)
                        nc.tensor.matmul(ps[:, MB + k % MRING, :], qop[0:QK_ROWS, ds(b, 1), ds(half * HALF + (m // NCH) * P, P)],
                                         kop[0:QK_ROWS, ds(b, 1), (m % NCH) * CH:(m % NCH + 1) * CH],
                                         start=True, stop=True).then_inc(sem("slot_done"), 1)

                    def turn_outputs(slot0, k, ts, it):
                        pe.wait_ge(sem("slot_used"), slot0 + k + 1)
                        pe.wait_ge(sem("o_saved"), it + 1)
                        for a, t in enumerate(ts):
                            i = nc.tensor.transpose(ps[:, MB + k % MRING, a * P:(a + 1) * P], osb[:, t * P:(t + 1) * P], ident[:, :])
                        i.then_inc(sem("slot_done"), 1)

                    def turn_maxima(slot0, k, nth, inc):
                        pe.wait_ge(sem("slot_used"), slot0 + k + 1)
                        pe.wait_ge(sem("max_split"), nth)
                        n = SPLITS * HALF // P
                        nc.tensor.transpose(psb[0:n, MB + k % MRING, 0:P], ms[:, :, :].rearrange("p s t -> p (s t)"),
                                            identb[:, :]).then_inc(sem("slot_done"), inc)

                    def weigh_values(it, kt):
                        if kt == 0:
                            pe.wait_ge(sem("o_saved"), it + 1)
                        if kt % 8 == 0:
                            pe.wait_ge(sem("v_ready"), 4 * (it // 2) + kt // 8 + 1)
                        pe.wait_ge(sem("exp_done"), 4 * (it * KT + kt) + 8)
                        for j in range(4):
                            i = nc.tensor.matmul(ps[32 * j:32 * j + 32, AV, :], vst[:, kt, :], pb[:, (4 * kt + j) % PRING, :],
                                                 start=(kt == 0), stop=(kt == KT - 1))
                        i.then_inc(sem("av_done"), 1)

                    pe.wait_ge(sem("v_init"), 6)
                    nc.tensor.matmul(ps[:, AV, :], ident[:, :], pb[:, 0, :], start=True, stop=True).then_inc(sem("av_cleared"), 1)
                    pe.wait_ge(sem("head_loaded"), QL)
                    for m in range(MAXES):
                        max_slot(0, m, 0, m, 0)
                    turn_maxima(0, MAXES, 1, 2)
                    for m in range(MAXES):
                        max_slot(0, MAXES + 2 + m, 0, m, 1)
                    pe.wait_ge(sem("head_loaded"), 2 * QL)

                    with pe.Fori(0, ROUNDS) as it:
                        b, nb_, half = (it // 2) % 3, (it // 2 + 1) % 3, it % 2
                        slot0 = SLOT0 + SLOTS * it
                        pe.wait_ge(sem("rows_loaded"), 16 * SPLITS * (it + 1))
                        pe.wait_ge(sem("v_init"), 6)
                        pe.wait_ge(sem("head_loaded"), QL * (it // 2 + 2))
                        for kt in range(KT):
                            for j in range(4):
                                pe.wait_ge(sem("exp_done"), 4 * (it * KT + kt) + j + 1)
                                nc.tensor.matmul(ps[:, SC + j, :], kop[:, ds(b, 1), kt * P:(kt + 1) * P],
                                                 qop[:, ds(b, 1), ds(half * HALF + j * CH, CH)],
                                                 start=True, stop=True).then_inc(sem("score_done"), 1)
                                m = 4 * kt + j
                                max_slot(slot0, m if m < 8 else m + 4, nb_, m, half)
                                if m == 7:
                                    turn_outputs(slot0, 8, (0, 1), it)
                                    turn_outputs(slot0, 9, (2, 3), it)
                                    turn_maxima(slot0, 10, it + 2, 2)
                            if kt:
                                weigh_values(it, kt - 1)
                        weigh_values(it, KT - 1)
                    turn_outputs(SLOT0 + SLOTS * ROUNDS, 0, (0, 1), ROUNDS)
                    turn_outputs(SLOT0 + SLOTS * ROUNDS, 1, (2, 3), ROUNDS)

                @block.vector
                def _(dve):
                    dve.sem_inc(sem("slot_used"), MRING)
                    NM = 5
                    steps = Steps(dve, sem("max_step"))

                    def reduce_slot(slot0, k, m):
                        dve.wait_ge(sem("slot_done"), slot0 + k + 1)
                        nc.vector.tensor_reduce(mp[:, m // NCH, m % NCH:m % NCH + 1], ps[:, MB + k % MRING, :], AX.X, ALU.max).then_inc(sem("slot_used"), 1)

                    def split_maxima(slots, nth):
                        dve.wait_ge(sem("slot_used"), slots + MRING)
                        dve.wait_ge(sem("slot_done"), slots)
                        steps.add(nc.vector.tensor_reduce(mq[:, :], mp[:, :, :], AX.X, ALU.max))
                        steps.wait()
                        steps.add(nc.vector.tensor_scalar(ms[:, 0, :], mq[:, :], -1.0, None, ALU.mult))
                        steps.wait()
                        steps.add(nc.vector.scalar_tensor_tensor(mr[:, :], mq[:, :], -1.0, ms[:, 0, :], ALU.mult, ALU.subtract))
                        steps.wait()
                        steps.add(nc.vector.tensor_copy(ms[:, 1, :], mr[:, :]))
                        steps.wait()
                        nc.vector.tensor_tensor(ms[:, 2, :], mr[:, :], ms[:, 1, :], ALU.subtract).then_inc(sem("max_split"), 1)

                    def save_rows(slot0, k, event):
                        dve.wait_ge(sem("slot_done"), slot0 + k + 2)
                        dve.wait_ge(sem("rows_loaded"), 16 * SPLITS * event)
                        nc.vector.tensor_copy(msb[:, :], psb[0:SPLITS * HALF // P, MB + k % MRING, 0:P]).then_inc(sem("rows_ready"), 1)
                        dve.wait_ge(sem("rows_ready"), event + 1)
                        dve.sem_inc(sem("slot_used"), 2)

                    def outputs(slot0, k, t, it):
                        dve.wait_ge(sem("slot_done"), slot0 + k + 1)
                        o = ps[:, MB + k % MRING, 0:2 * P].rearrange("p (t j c) -> p t j c", t=2, j=4)
                        r = rc[:, t // 2, :, :]
                        steps.add(nc.vector.reciprocal(r, o[:, :, :, HD]))
                        steps.wait()
                        nc.vector.tensor_tensor(O[:, ds(it, 1), t:t + 2, :, :].rearrange("p a t j d -> p (a t) j d"), o[:, :, :, 0:HD],
                                                r[:, :, :, None].to_broadcast([P, 2, 4, HD]), ALU.mult).then_inc(sem("slot_used"), 1)

                    dve.wait_ge(sem("v_init"), 6)
                    for m in range(MAXES):
                        reduce_slot(0, m, m)
                    split_maxima(MAXES, 1)
                    save_rows(0, MAXES, 0)
                    for m in range(MAXES):
                        reduce_slot(0, MAXES + 2 + m, m)
                    with dve.Fori(0, ROUNDS) as it:
                        slot0 = SLOT0 + SLOTS * it
                        steps.at = 4 + it * 6
                        split_maxima(slot0, it + 2)
                        for m in range(MAXES):
                            reduce_slot(slot0, m if m < 8 else m + 4, m)
                            if m == 7:
                                outputs(slot0, 8, 0, it)
                                outputs(slot0, 9, 2, it)
                                save_rows(slot0, 10, it + 1)
                    steps.at = 4 + ROUNDS * 6
                    dve.wait_ge(sem("slot_used"), SLOT0 + SLOTS * ROUNDS + MRING)
                    outputs(SLOT0 + SLOTS * ROUNDS, 0, 0, ROUNDS)
                    outputs(SLOT0 + SLOTS * ROUNDS, 1, 2, ROUNDS)

    def project_out(wout, bout, O):
        base, nbase = front
        front[0] += NCH + 1
        front[1] += NCH + 1
        with ExitStack() as s10:
            nbuf = sb("o_nbuf", [P, 2, TPC, D], stack=s10)
            nT = sb("o_nT", [P, 2, KD, CH], stack=s10)
            Oh = O[:, 1:ROUNDS + 1, :, :, :].rearrange("p (h a) t j d -> p a h t j d", a=2)
            with nc.Block() as block:
                @block.gpsimd
                def _(pool):
                    with pool.Fori(0, NCH) as n:
                        xc = X[:, ds(n * TPC, TPC), :]
                        nc.gpsimd.tensor_tensor(xc, xc, bout[:, None, :].to_broadcast([P, TPC, D]), ALU.add).then_inc(sem("bout_added"), 1)

                @block.scalar
                def _(act):
                    def turned(n, par):
                        act.wait_ge(sem("transposed"), base + n + 1)
                        nc.scalar.activation(nT[:, par, :, :], ps[:, 0:2, :], ACT.Copy).then_inc(sem("nT_ready"), 1)

                    turned(0, 0)
                    with act.Fori(0, NCH // 2) as i:
                        turned(2 * i + 1, 1)
                        turned(2 * i + 2, 0)

                @block.tensor
                def _(pe):
                    def turn(n, par):
                        pe.wait_ge(sem("normed"), nbase + n + 1)
                        pe.wait_ge(sem("nT_ready"), base + n)
                        transposes(nbuf[:, par]).then_inc(sem("transposed"), 1)

                    def chunk(n, par):
                        turn(n + 1, 1 - par)
                        pe.wait_ge(sem("nT_ready"), base + n + 1)
                        pe.wait_ge(sem("wout_added"), n)
                        for t in range(TPC):
                            for k in range(KD):
                                i = nc.tensor.matmul(ps[:, 6 + t // 2, (t % 2) * D:(t % 2 + 1) * D],
                                                     nT[:, par, k, t * P:(t + 1) * P], wout[:, k, :], start=(k == 0), stop=(k == KD - 1))
                        i.then_inc(sem("wout_done"), 1)

                    turn(0, 0)
                    with pe.Fori(0, NCH // 2) as i:
                        chunk(2 * i, 0)
                        chunk(2 * i + 1, 1)

                @block.vector
                def _(dve):
                    steps = Steps(dve, sem("out_step"))
                    PER = STATS

                    def gather(n, par):
                        for t in range(TPC):
                            i = nc.vector.tensor_copy(nbuf[:, par, t, :].rearrange("p (h d) -> p h d", h=H),
                                                      Oh[:, ds((n // 4) % 2, 1), :, t, ds(n % 4, 1), :].rearrange("p a h j d -> p (a h) (j d)"))
                        i.then_inc(sem("normed"), 1)

                    def chunk(n, par):
                        steps.at = n * PER
                        dve.wait_ge(sem("transposed"), base + n)
                        gather(n + 1, 1 - par)
                        dve.wait_ge(sem("bout_added"), n + 1)
                        dve.wait_ge(sem("wout_done"), n + 1)
                        xc = X[:, ds(n * TPC, TPC), :]
                        nc.vector.tensor_tensor(xc, xc, ps[:, 6:8, :].rearrange("p b (t d) -> p (b t) d", d=D), ALU.add).then_inc(sem("wout_added"), 1)
                        dve.wait_ge(sem("wout_added"), n + 1)
                        stats(dve, steps, n)

                    gather(0, 0)
                    with dve.Fori(0, NCH // 2) as i:
                        chunk(2 * i, 0)
                        chunk(2 * i + 1, 1)

    with ExitStack() as s1:
        W = {"w1": sb("w1", [P, KD, F], stack=s1), "w2": sb("w2", [P, KF, D], stack=s1), "b1": sb("b1", [P, KF], stack=s1),
             "b2h": sb("b2h", [P, D], stack=s1), "win": sb("win", [P, KD, 2 * D], stack=s1),
             "wo": sb("wo", [P, KD, D], stack=s1), "c0": sb("c0", [P, 12, KD], stack=s1),
             "ob": sb("ob", [P, D], stack=s1), "lnw": sb("lnw", [P, D], stack=s1), "lnb": sb("lnb", [P, D], stack=s1),
             "nbuf": sb("nbuf", [P, 2, TPC, D], stack=s1), "nT": sb("nT", [P, 2, KD, CH], stack=s1),
             "hT": sb("hT", [P, KF, CH], stack=s1)}
        x_sems = [sem(f"x_loaded{n}") for n in range(NCH)]
        ffn(0, W, x_sems)
        if stop > 1:
            scan_layer(W)
        if stop > 2:
            ffn(1, W, x_sems)
    if stop > 3:
        slots(0)
    if stop > 4:
        attention()
    if stop > 5:
        slots(1)
    if stop < 6:
        with nc.Block() as block:
            @block.sync
            def _(sp):
                sp.dma_start(out.rearrange("a (n p) d -> (a p) n d", p=P), X[:, :, :]).then_inc(sem("stored"), 16)
                sp.wait_ge(sem("stored"), 16)


def layout(i):
    g = {k: np.asarray(v) for k, v in i.items()}
    col = lambda v: np.ascontiguousarray(v.reshape(-1, P).T)
    a = {"x": g["L0_attn_x"], "W1": g["L0_ffn_W1"], "W2": g["L0_ffn_W2"], "b1": col(g["L0_ffn_b1"]),
         "b2": g["L0_ffn_b2"], "in_proj_w": g["L0_attn_in_proj_w"], "out_proj_w": g["L0_attn_out_proj_w"],
         "out_proj_b": g["L0_attn_out_proj_b"], "ln_w": g["L0_attn_ln_w"], "ln_b": g["L0_attn_ln_b"]}
    b = g["L0_attn_in_proj_b"]
    cw = g["L0_attn_conv_w"]
    a["ssm_cols"] = np.stack([col(v) for v in (b[:D], b[D:], cw[:, 0, 0], cw[:, 0, 1], cw[:, 0, 2], g["L0_attn_conv_b"],
                                               g["L0_attn_logit_a"], g["L0_attn_ssm_b"], g["L0_attn_ssm_c"],
                                               g["L0_attn_ssm_d"], b[:D], b[:D])], axis=1)
    s = "L1_ffn_"
    for n in ("d_Wq", "d_Wv", "d_Wo", "c_Wk", "c_Wv", "c_Wo"):
        a[n] = g[s + n]
    a["d_WkT"], a["c_WqT"] = g[s + "d_Wk"].T, g[s + "c_Wq"].T
    a["cols"] = np.stack([col(g[s + n]) for n in ("d_bq", "d_bk", "d_bv", "c_bq", "c_bk", "c_bv")], axis=1)
    rep = lambda v: np.broadcast_to(v, (E, D))
    a["rows16"] = np.stack([g[s + "slot_query"][0], rep(g[s + "d_bo"]), g[s + "e_ln_g"], g[s + "e_ln_b"], g[s + "e_b2"]], axis=1)
    a["eb"] = np.stack([g[s + n].reshape(4, GROUPS, 2, P, 4).transpose(3, 1, 2, 4, 0).reshape(P, GROUPS, KF, 4)
                        for n in ("e_b1", "e_bg")], axis=1)
    a["c_bo"] = g[s + "c_bo"]
    for n in ("e_W1", "e_Wg", "e_W2"):
        a[n] = g[s + n]
    w = g["L1_attn_w_qkv"]
    swap = lambda m: m.reshape(H, 2, HD // 2, D)[:, ::-1].reshape(D, D)
    a["wqkv"] = np.concatenate([w, swap(w[:D]), swap(w[D:2 * D])], axis=0).T
    a["woutT"] = g["L1_attn_w_out"].T
    a["b_out"] = g["L1_attn_b_out"]
    return {k: np.ascontiguousarray(v) for k, v in {**a, **constants()}.items()}


def kernel(**inputs):
    import concourse.bacc as _bacc
    from concourse.bass_utils import run_bass_kernel_spmd as _run

    nc = _bacc.Bacc("TRN2", target_bir_lowering=False, num_devices=1)
    arrays = layout(inputs)
    A = {n: nc.dram_tensor("in_" + n, a.shape, mybir.dt.from_np(a.dtype), kind="ExternalInput").ap() for n, a in arrays.items()}
    out = nc.dram_tensor("out_x", (1, T, D), f32, kind="ExternalOutput").ap()
    build(nc, A, out)
    r = _run(nc, [{"in_" + n: a for n, a in arrays.items()}], core_ids=[0])
    return r.results[0]["out_x"]
```

```python
import numpy as np
import concourse.bass as bass
from concourse import mybir
from contextlib import ExitStack

f32 = mybir.dt.float32
bf16 = mybir.dt.bfloat16
ALU = mybir.AluOpType
ACT = mybir.ActivationFunctionType
AX = mybir.AxisListType
ds = bass.ds

P = 128
T = 4096
D = 256
KD = D // P
TILES = T // P
CH = 512
NCH = T // CH
TPC = CH // P
F = 1024
KF = F // P
H = 16
HD = D // H
E = 16
PAIRS = H * E
EPS = 1e-5
SCALE = HD ** -0.5
GROUPS = 4
RING = 6
UNITS = 6 * GROUPS
SPLITS = 3
TERMS = 6
RUNS = ((0, 0, 3), (0, 1, 2), (0, 2, 1))
QK_ROWS = TERMS * HD
ROWS = QK_ROWS + SPLITS
HALF = T // 2
ROUNDS = 2 * H
KT = TILES
MAXES = (HALF // P) * NCH
AHEAD = 20
OUT_AT = (7, 31)
MAX_AT = MAXES - AHEAD + 11
SLOTS = MAXES + 4
MRING = 3
PRING = 8
STATS = 5


class Steps:

    def __init__(self, engine, sem, base=0):
        self.engine, self.sem, self.at = engine, sem, base

    def add(self, instruction):
        instruction.then_inc(self.sem, 1)
        self.at = self.at + 1

    def wait(self):
        self.engine.wait_ge(self.sem, self.at)

    def wait_alone(self):
        self.wait()
        self.engine.sem_inc(self.sem, 1)
        self.at = self.at + 1


def constants():
    half = HD // 2
    inv = (1.0 / np.float32(10000.0) ** (np.arange(0, HD, 2, dtype=np.float32) / np.float32(HD))).astype(np.float32)
    ang = (np.arange(T, dtype=np.float32)[:, None] * inv[None, :]).astype(np.float32)
    cos, sin = np.cos(ang).astype(np.float32), np.sin(ang).astype(np.float32)
    rope = np.zeros((P, 2, T), np.float32)
    for p in range(P):
        j = p % HD
        rope[p, 0] = cos[:, j % half]
        rope[p, 1] = -sin[:, j % half] if j < half else sin[:, j % half]
    e = np.arange(P)
    head_of = (np.arange(KD)[None, :, None] * P + e[:, None, None]) // HD
    mask = (head_of == np.arange(H)[None, None, :]).astype(np.float32)
    slot = (e[:, None] % E == np.arange(E)[None, :]).astype(np.float32)
    pick = np.zeros((P, GROUPS, 4), np.float32)
    for g in range(GROUPS):
        for j in range(4):
            pick[32 * j + 4 * j + g, g, j] = 1.0
    return {"c_rope": rope, "c_ident": np.eye(P, dtype=np.float32), "c_mask": mask, "c_slot": slot, "c_pick": pick}


def build(nc, A, out):
    with ExitStack() as ctx:
        program(nc, A, out, ctx)


def program(nc, A, out, ctx):
    taken = set()

    def sb(name, shape, dt=f32, stack=ctx):
        name += "_again" * (name in taken)
        taken.add(name)
        return stack.enter_context(nc.sbuf_tensor(name, shape, dt))

    sems = {}

    def sem(name):
        if name not in sems:
            sems[name] = ctx.enter_context(nc.semaphore(name))
        return sems[name]

    X = sb("X", [P, TILES, D])
    mv = sb("mv", [P, TILES, 2])
    st6 = sb("st6", [P, TPC, 6])
    mv4 = sb("mv4", [P, TPC, 2])
    sd = sb("sd", [P, TILES])
    rstd = sb("rstd", [P, TILES])
    eps = sb("eps", [P, 1])
    ident = sb("ident", [P, P])
    identb = sb("identb", [P, P], bf16)
    mask = sb("mask", [P, KD, H])
    slotsel = sb("slotsel", [P, E])
    pick = sb("pick", [P, GROUPS, 4])
    ones = sb("ones", [SPLITS, P], bf16)
    zeros = sb("zeros", [P, D])
    SLOT_W = ("d_Wq", "d_WkT", "d_Wv", "d_Wo", "c_WqT", "c_Wk", "c_Wv", "c_Wo")
    dW = {n: sb(n, [P, KD, D]) for n in SLOT_W}
    cols = sb("cols", [P, 6, KD])
    rows16 = sb("rows16", [E, 2, D])
    eb = sb("eb", [P, 2, GROUPS, KF, 4])
    bo_half = sb("bo_half", [P, D])
    pool_q = sb("pool_q", [P, KD, PAIRS])
    pool_c = sb("pool_c", [P, 2])
    ps = ctx.enter_context(nc.psum_tensor("ps", [P, 8, CH], f32))
    front = [0, 0]

    def norm_tiles(dst, chunk, src=None, m=None, r=None):
        src, m, r = src or X, m or mv, r or rstd
        for t in range(TPC):
            k = chunk * TPC + t
            last = nc.vector.tensor_scalar(dst[:, t:t + 1, :], src[:, ds(k, 1), :], m[:, ds(k, 1), 0:1],
                                           r[:, ds(k, 1)], ALU.subtract, ALU.mult)
        return last

    def transposes(nchunk):
        for k in range(KD):
            for t in range(TPC):
                last = nc.tensor.transpose(ps[:, k, t * P:(t + 1) * P], nchunk[:, t, k * P:(k + 1) * P], ident[:, :])
        return last

    def stats(dve, steps, chunk, src=None, m=None):
        src, m = src or X, m or mv
        steps.wait_alone()
        for t in range(TPC):
            i = nc.vector.bn_stats(st6[:, t, :], src[:, ds(chunk * TPC + t, 1), :])
        steps.add(i)
        steps.wait_alone()
        for t in range(TPC):
            i = nc.vector.bn_aggr(mv4[:, t, :], st6[:, t, :])
        steps.add(i)
        steps.wait()
        steps.add(nc.vector.tensor_scalar(m[:, ds(chunk * TPC, TPC), :], mv4[:, :, :], 1.0, None, ALU.mult))

    def root(m=None):
        nc.scalar.activation(sd[:, :], (m or mv)[:, :, 1], ACT.Sqrt, bias=eps[:, :]).then_inc(sem("sd_ready"), 1)

    def reciprocal_of_root(dve, nth, dst=None):
        dve.wait_ge(sem("sd_ready"), nth)
        nc.vector.reciprocal((dst or rstd)[:, :], sd[:, :]).then_inc(sem("rstd_ready"), 1)
        dve.wait_ge(sem("rstd_ready"), nth)

    def ffn(inst, W):
        (base, nbase), b8, b10 = front, inst * NCH, inst * (NCH + 2)
        front[0] += NCH + 1
        front[1] += NCH + 1
        w1, w2, b1, b2h, nbuf, nT, hT = (W[k] for k in ("w1", "w2", "b1", "b2h", "nbuf", "nT", "hT"))
        Hb, mvH, rH, lnw, lnb = (W[k] for k in ("Hb", "mvH", "rH", "lnw", "lnb"))
        with nc.Block() as block:
            if inst == 0:
                @block.sync
                def _(sp):
                    xv = A["x"].rearrange("a (n p) d -> (a p) n d", p=P)
                    def load_x(n):
                        sp.dma_start(X[:, n * TPC:(n + 1) * TPC, :], xv[:, n * TPC:(n + 1) * TPC, :]).then_inc(sem(f"x_loaded{n}"), 16)

                    load_x(0)
                    sp.dma_start(ident[:, :], A["c_ident"]).then_inc(sem("ident_loaded"), 16)
                    sp.dma_start(w1[:, :, :], A["W1"].rearrange("(k p) f -> p k f", p=P)).then_inc(sem("w1_loaded"), 16)
                    load_x(1)
                    sp.dma_start(b1[:, :], A["b1"]).then_inc(sem("b_loaded"), 16)
                    sp.dma_start(b2h[:, :], A["b2"].partition_broadcast(P)).then_inc(sem("b_loaded"), 16)
                    sp.dma_start(w2[:, :, :], A["W2"].rearrange("(k p) f -> p k f", p=P)).then_inc(sem("w2_loaded"), 16)
                    for n in range(2, NCH):
                        load_x(n)
                    later = [(W["win"], A["in_proj_w"].rearrange("(k p) f -> p k f", p=P)),
                             (W["wo"], A["out_proj_w"].rearrange("(k p) f -> p k f", p=P)),
                             (W["c0"], A["ssm_cols"]), (W["ob"], A["out_proj_b"].partition_broadcast(P)),
                             (W["lnw"], A["ln_w"].partition_broadcast(P)), (W["lnb"], A["ln_b"].partition_broadcast(P)),
                             (mask, A["c_mask"]), (slotsel, A["c_slot"]), (pick, A["c_pick"]), (cols, A["cols"]),
                             (rows16, A["rows16"]), (eb, A["eb"]), (bo_half, A["c_bo"].partition_broadcast(P)),
                             ]
                    later += [(dW[n], A[n].rearrange("(k p) f -> p k f", p=P)) for n in SLOT_W]
                    for dst, src in later:
                        sp.dma_start(dst[...], src).then_inc(sem("later_loaded"), 16)
                    sp.wait_ge(sem("later_loaded"), 16 * len(later))

            @block.scalar
            def _(act):
                if inst == 0:
                    act.preload_act_table(ACT.Sqrt)
                    act.wait_ge(sem("const_ready"), 1)
                    act.sem_inc(sem("relu_done"), 4)
                else:
                    root(mvH)

                def root_of(n):
                    act.wait_ge(sem("chunk_stats"), b10 + n + 1)
                    c = (n % NCH) * TPC
                    nc.scalar.activation(sd[:, ds(c, TPC)], mv[:, ds(c, TPC), 1], ACT.Sqrt, bias=eps[:, :]).then_inc(sem("root_done"), 1)

                root_of(0)
                root_of(1)
                if inst == 0:
                    act.wait_ge(sem("b_loaded"), 32)

                def chunk(n, par):
                    for f in range(KF):
                        if f == 0:
                            act.wait_ge(sem("down_done"), b8 + n + 1)
                        act.wait_ge(sem("up_done"), (b8 + n) * KF + f + 1)
                        nc.scalar.activation(hT[:, f, :], ps[:, 2 + f % 4, :], ACT.Relu,
                                             bias=b1[:, f:f + 1]).then_inc(sem("relu_done"), 1)
                    root_of(n + 2)

                with act.Fori(0, NCH // 2) as i:
                    chunk(2 * i, 0)
                    chunk(2 * i + 1, 1)

            @block.tensor
            def _(pe):
                if inst == 0:
                    pe.wait_ge(sem("ident_loaded"), 16)
                    pe.sem_inc(sem("down_done"), 1)

                def turn(n, par):
                    pe.wait_ge(sem("normed"), nbase + n + 1)
                    pe.wait_ge(sem("nT_ready"), base + n)
                    transposes(nbuf[:, par]).then_inc(sem("transposed"), 1)

                def chunk(n, par):
                    pe.wait_ge(sem("nT_ready"), base + n + 1)
                    for f in range(KF):
                        pe.wait_ge(sem("relu_done"), (b8 + n) * KF + f + 1)
                        for k in range(KD):
                            i = nc.tensor.matmul(ps[:, 2 + f % 4, :], w1[:, k, f * P:(f + 1) * P], nT[:, par, k, :],
                                                 start=(k == 0), stop=(k == KD - 1))
                        i.then_inc(sem("up_done"), 1)
                    turn(n + 1, 1 - par)
                    pe.wait_ge(sem("relu_done"), (b8 + n + 1) * KF + 4)
                    pe.wait_ge(sem("x_updated"), b8 + n)
                    for t in range(TPC):
                        for f in range(KF):
                            i = nc.tensor.matmul(ps[:, 6 + t // 2, (t % 2) * D:(t % 2 + 1) * D],
                                                 hT[:, f, t * P:(t + 1) * P], w2[:, f, :],
                                                 start=(f == 0), stop=(f == KF - 1))
                    i.then_inc(sem("down_done"), 1)

                turn(0, 0)
                if inst == 0:
                    pe.wait_ge(sem("w1_loaded"), 16)
                    pe.wait_ge(sem("w2_loaded"), 16)
                with pe.Fori(0, NCH // 2) as i:
                    chunk(2 * i, 0)
                    chunk(2 * i + 1, 1)

            if inst == 1:
                @block.gpsimd
                def _(pool):
                    with pool.Fori(0, NCH) as n:
                        hc = Hb[:, ds(n * TPC, TPC), :]
                        xc = X[:, ds(n * TPC, TPC), :]
                        steps = Steps(pool, sem("fin_step"), 3 * n)
                        steps.add(nc.gpsimd.tensor_tensor(xc, xc, lnb[:, None, :].to_broadcast([P, TPC, D]), ALU.add))
                        pool.wait_ge(sem("H_normed"), n + 1)
                        pool.sem_inc(sem("H_seen"), 1)
                        steps.add(nc.gpsimd.tensor_tensor(hc, hc, lnw[:, None, :].to_broadcast([P, TPC, D]), ALU.mult))
                        steps.wait_alone()
                        nc.gpsimd.tensor_tensor(xc, xc, hc, ALU.add).then_inc(sem("fin_done"), 1)
                    pool.wait_ge(sem("chunk_stats"), b10 + NCH)
                    pool.sem_inc(sem("fin_done"), 2)

            @block.vector
            def _(dve):
                def recip(n):
                    dve.wait_ge(sem("root_done"), b10 + n + 1)
                    c = (n % NCH) * TPC
                    nc.vector.reciprocal(rstd[:, ds(c, TPC)], sd[:, ds(c, TPC)]).then_inc(sem("rstd_chunk"), 1)

                def norm_H(n):
                    for t in range(TPC):
                        k = (n % NCH) * TPC + t
                        i = nc.vector.tensor_scalar(Hb[:, ds(k, 1), :], Hb[:, ds(k, 1), :], mvH[:, ds(k, 1), 0:1],
                                                    rH[:, ds(k, 1)], ALU.subtract, ALU.mult)
                    i.then_inc(sem("H_normed"), 1)

                if inst == 0:
                    s = Steps(dve, sem("dve_start"))
                    s.add(nc.vector.memset(eps[:, :], EPS))
                    s.add(nc.vector.memset(ones[:, :], 1.0))
                    s.add(nc.vector.memset(zeros[:, :], 0.0))
                    s.wait()
                    dve.sem_inc(sem("const_ready"), 1)
                else:
                    s = Steps(dve, sem("fin_start"))
                    reciprocal_of_root(dve, 2, rH)
                    norm_H(0)
                    norm_H(1)
                    norm_H(2)
                for n in range(2):
                    if inst == 0:
                        dve.wait_ge(sem(f"x_loaded{n}"), 16)
                    else:
                        dve.wait_ge(sem("fin_done"), n + 1)
                    stats(dve, s, n)
                    s.wait()
                    dve.sem_inc(sem("chunk_stats"), 1)
                    recip(n)
                    if n == 0:
                        dve.wait_ge(sem("rstd_chunk"), b10 + 1)
                        norm_tiles(nbuf[:, 0], 0).then_inc(sem("normed"), 1)
                PER = 1 + STATS * (1 + inst)
                steps = Steps(dve, sem(f"ffn_dve{inst}"))

                def turned(n, par):
                    dve.wait_ge(sem("transposed"), base + n + 1)
                    nc.vector.tensor_copy(nT[:, par, :, :], ps[:, 0:2, :]).then_inc(sem("nT_ready"), 1)

                def chunk(n, par):
                    steps.at = n * PER
                    dve.wait_ge(sem("rstd_chunk"), b10 + n + 2)
                    dve.wait_ge(sem("transposed"), base + n)
                    norm_tiles(nbuf[:, 1 - par], (n + 1) % NCH).then_inc(sem("normed"), 1)
                    dve.wait_ge(sem("up_done"), (b8 + n) * KF)
                    turned(n + 1, 1 - par)
                    if inst:
                        dve.wait_ge(sem("fin_done"), n + 3)
                        stats(dve, steps, (n + 2) % NCH)
                    steps.wait()
                    dve.sem_inc(sem("chunk_stats"), 1)
                    dve.wait_ge(sem("down_done"), b8 + n + 2)
                    xc = X[:, ds(n * TPC, TPC), :]
                    steps.wait()
                    nc.vector.scalar_tensor_tensor(xc, ps[:, 6:8, :].rearrange("p b (t d) -> p (b t) d", d=D),
                                                   0.5, xc, ALU.mult, ALU.add).then_inc(sem("x_updated"), 1)
                    dve.wait_ge(sem("x_updated"), b8 + n + 1)
                    steps.add(nc.vector.tensor_tensor(xc, xc, b2h[:, None, :].to_broadcast([P, TPC, D]), ALU.add))
                    stats(dve, steps, n)
                    if inst:
                        norm_H(n + 3)
                    recip(n + 2)

                turned(0, 0)
                if inst == 0:
                    for n in range(2, NCH):
                        dve.wait_ge(sem(f"x_loaded{n}"), 16)
                        stats(dve, s, n)
                    dve.wait_ge(sem("b_loaded"), 32)
                    s.add(nc.vector.tensor_scalar(b2h[:, :], b2h[:, :], 0.5, None, ALU.mult))
                    s.add(nc.vector.tensor_copy(identb[:, :], ident[:, :]))
                    s.wait()
                with dve.Fori(0, NCH // 2) as i:
                    chunk(2 * i, 0)
                    chunk(2 * i + 1, 1)


    def scan_layer(W):
        base, nbase = front
        front[0] += NCH + 1
        front[1] += NCH + 2
        nbuf, nT, win, wo, c0, ob = (W[k] for k in ("nbuf", "nT", "win", "wo", "c0", "ob"))
        uT, Hb, mvH = (W[k] for k in ("uT", "Hb", "mvH"))
        BU, BV, W0, W1, W2, CB, LOGIT, SB, SC, SD = range(10)
        with ExitStack() as s2:
            vT = sb("vT", [P, KD, T + 2], stack=s2)
            nmr = sb("nmr", [P, TILES], stack=s2)
            decay = sb("decay", [P, KD], stack=s2)
            decays = sb("decays", [P, KD, CH], stack=s2)
            t1 = sb("t1", [P, 2, KD, CH], stack=s2)
            hs = sb("hs", [P, 2, KD, CH], stack=s2)
            bv, dv = ([W["hT"][:, 4 * par + 2 * m:4 * par + 2 * m + 2, :] for par in range(2)] for m in range(2))
            oT = t1
            rn = nbuf
            col = lambda j, k: c0[:, j, k:k + 1]
            cols_of = lambda n: vT[:, :, ds(n * CH, CH)]
            with nc.Block() as block:
                @block.scalar
                def _(act):
                    root()
                    nc.scalar.activation(decay[:, :], c0[:, LOGIT, :], ACT.Sigmoid).then_inc(sem("decay_ready"), 1)
                    act.preload_act_table(ACT.Silu)

                    def turned(n, par):
                        act.wait_ge(sem("transposed"), base + n + 1)
                        nc.scalar.activation(nT[:, par, :, :], ps[:, 0:2, :], ACT.Copy).then_inc(sem("nT_ready"), 1)

                    def chunk(n, par):
                        turned(n + 1, 1 - par)
                        for k in range(KD):
                            act.wait_ge(sem("uv_done"), 2 * n + 1)
                            nc.scalar.activation(uT[:, ds(n, 1), k, :], ps[:, 2 + k:3 + k, :], ACT.Identity, bias=col(BU, k))
                        for k in range(KD):
                            act.wait_ge(sem("uv_done"), 2 * n + 2)
                            i = nc.scalar.activation(vT[:, k, ds(n * CH + 1, CH)], ps[:, 4 + k, :], ACT.Silu, bias=col(BV, k))
                        i.then_inc(sem("uv_saved"), 1)
                        act.wait_ge(sem("uv_saved"), n + 1)
                        act.wait_ge(sem("conv_done"), n)
                        for k in range(KD):
                            i = nc.scalar.activation(t1[:, par, k, :], vT[:, k, ds(n * CH, CH)], ACT.Identity,
                                                     bias=col(CB, k), scale=col(W0, k))
                        i.then_inc(sem("t1_ready"), 1)

                    def scan_input(n, par):
                        act.wait_ge(sem("y_done"), n)
                        act.wait_ge(sem("conv_done"), n + 2)
                        act.sem_inc(sem("conv_known"), 1)
                        for k in range(KD):
                            i = nc.scalar.activation(bv[par][:, k, :], vT[:, k, ds(n * CH, CH)], ACT.Copy, scale=col(SB, k))
                        i.then_inc(sem("bv_ready"), 1)

                    turned(0, 0)
                    chunk(0, 0)
                    chunk(1, 1)
                    scan_input(0, 0)
                    with act.Fori(1, NCH // 2) as i:
                        chunk(2 * i, 0)
                        scan_input(2 * i - 1, 1)
                        chunk(2 * i + 1, 1)
                        scan_input(2 * i, 0)
                    act.sem_inc(sem("uv_saved"), 1)
                    scan_input(NCH - 1, 1)

                    def gate_and_residual(n, par):
                        act.wait_ge(sem("y_done"), n + 2)
                        act.sem_inc(sem("y_known"), 1)
                        nc.scalar.activation(cols_of(n), cols_of(n), ACT.Silu).then_inc(sem("gate_ready"), 1)
                        act.wait_ge(sem("h_saved"), n)
                        act.sem_inc(sem("h_known"), 1)
                        for t in range(TPC):
                            k = n * TPC + t
                            i = nc.scalar.activation(rn[:, par, t:t + 1, :], X[:, ds(k, 1), :], ACT.Identity,
                                                     bias=nmr[:, ds(k, 1)], scale=rstd[:, ds(k, 1)])
                        i.then_inc(sem("rn_ready"), 1)

                    act.wait_ge(sem("transposed"), base + NCH + 1)
                    act.wait_ge(sem("nmr_ready"), 1)
                    with act.Fori(0, NCH // 2) as i:
                        gate_and_residual(2 * i, 0)
                        gate_and_residual(2 * i + 1, 1)
                    act.wait_ge(sem("gated"), NCH)
                    act.sem_inc(sem("gate_ready"), 1)

                @block.tensor
                def _(pe):
                    pe.wait_ge(sem("later_loaded"), 32)

                    def turn(n, par):
                        pe.wait_ge(sem("normed"), nbase + n + 1)
                        pe.wait_ge(sem("nT_ready"), base + n)
                        transposes(nbuf[:, par]).then_inc(sem("transposed"), 1)

                    def project(n, par):
                        turn(n + 1, 1 - par)
                        pe.wait_ge(sem("nT_ready"), base + n + 1)
                        pe.wait_ge(sem("uv_saved"), n)
                        for c in range(2 * KD):
                            for k in range(KD):
                                i = nc.tensor.matmul(ps[:, 2 + c, :], win[:, k, c * P:(c + 1) * P], nT[:, par, k, :],
                                                     start=(k == 0), stop=(k == KD - 1))
                            if c % KD == KD - 1:
                                i.then_inc(sem("uv_done"), 1)

                    def output(n, par):
                        pe.wait_ge(sem("gated"), n + 1)
                        pe.wait_ge(sem("h_saved"), n)
                        for t in range(TPC):
                            for k in range(KD):
                                i = nc.tensor.matmul(ps[:, 6 - 2 * par + t // 2, (t % 2) * D:(t % 2 + 1) * D],
                                                     oT[:, par, k, t * P:(t + 1) * P], wo[:, k, :],
                                                     start=(k == 0), stop=(k == KD - 1))
                        i.then_inc(sem("wo_done"), 1)

                    turn(0, 0)
                    with pe.Fori(0, NCH // 2) as i:
                        project(2 * i, 0)
                        project(2 * i + 1, 1)
                    with pe.Fori(0, NCH // 2) as i:
                        output(2 * i, 0)
                        output(2 * i + 1, 1)

                @block.gpsimd
                def _(pool):
                    def terms(n, par):
                        pool.wait_ge(sem("y_done"), n)
                        pool.wait_ge(sem("conv_done"), n + 2)
                        pool.sem_inc(sem("conv_seen"), 1)
                        for k in range(KD):
                            i = nc.gpsimd.tensor_tensor(dv[par][:, k, :], vT[:, k, ds(n * CH, CH)], col(SD, k).to_broadcast([P, CH]), ALU.mult)
                        i.then_inc(sem("dv_ready"), 1)

                    def residual(n, par):
                        pool.wait_ge(sem("rn_ready"), n + 1)
                        nc.gpsimd.tensor_tensor(rn[:, par, :, :], rn[:, par, :, :], ob[:, None, :].to_broadcast([P, TPC, D]),
                                                ALU.add).then_inc(sem("rnb_ready"), 1)

                    with pool.Fori(0, NCH // 2) as i:
                        terms(2 * i, 0)
                        terms(2 * i + 1, 1)
                    with pool.Fori(0, NCH // 2) as i:
                        residual(2 * i, 0)
                        residual(2 * i + 1, 1)

                @block.vector
                def _(dve):
                    s = Steps(dve, sem("scan_start"))
                    s.add(nc.vector.memset(hs[:, 1, :, CH - 1:CH], 0.0))
                    s.add(nc.vector.memset(vT[:, :, 0:1], 0.0))
                    s.add(nc.vector.memset(vT[:, :, T + 1:T + 2], 0.0))
                    s.add(nc.vector.memset(decays[:, :, :], 1.0))
                    s.wait()
                    dve.sem_inc(sem("conv_done"), 1)
                    dve.sem_inc(sem("y_done"), 1)
                    dve.sem_inc(sem("h_saved"), 1)
                    dve.wait_ge(sem("decay_ready"), 1)
                    for k in range(KD):
                        s.add(nc.vector.tensor_scalar(decays[:, k, :], decays[:, k, :], decay[:, k:k + 1], None, ALU.mult))
                    s.wait()
                    reciprocal_of_root(dve, 1)
                    nc.vector.scalar_tensor_tensor(nmr[:, :], mv[:, :, 0], -1.0, rstd[:, :], ALU.mult, ALU.mult).then_inc(sem("nmr_ready"), 1)

                    def norm(n, par):
                        norm_tiles(nbuf[:, par], n % NCH).then_inc(sem("normed"), 1)

                    PER = 2 * KD
                    steps = Steps(dve, sem("scan_dve"))

                    def convolve(n, par):
                        dve.wait_ge(sem("uv_saved"), n + 2)
                        dve.wait_ge(sem("t1_ready"), n + 1)
                        v = lambda o, k: vT[:, k, ds(n * CH + o, CH)]
                        for k in range(KD):
                            steps.add(nc.vector.scalar_tensor_tensor(t1[:, par, k, :], v(1, k), col(W1, k), t1[:, par, k, :], ALU.mult, ALU.add))
                        steps.wait()
                        for k in range(KD):
                            i = nc.vector.scalar_tensor_tensor(v(0, k), v(2, k), col(W2, k), t1[:, par, k, :], ALU.mult, ALU.add)
                        i.then_inc(sem("conv_done"), 1)

                    def scan(n, par):
                        dve.wait_ge(sem("bv_ready"), n + 1)
                        dve.wait_ge(sem("y_done"), n + 1)
                        for k in range(KD):
                            steps.add(nc.vector.tensor_tensor_scan(hs[:, par, k, :], decays[:, k, :], bv[par][:, k, :],
                                                                   hs[:, 1 - par, k, CH - 1:CH], ALU.mult, ALU.add))
                        steps.wait()
                        dve.wait_ge(sem("dv_ready"), n + 1)
                        for k in range(KD):
                            i = nc.vector.scalar_tensor_tensor(vT[:, k, ds(n * CH, CH)], hs[:, par, k, :], col(SC, k), dv[par][:, k, :],
                                                               ALU.mult, ALU.add)
                        i.then_inc(sem("y_done"), 1)

                    def step(n, par, tail=False):
                        steps.at = KD + n * PER
                        if not tail:
                            dve.wait_ge(sem("transposed"), base + n + 3)
                            norm(n + 4, par)
                        if not (tail and n == NCH - 1):
                            convolve(n + 1, 1 - par)
                        scan(n, par)

                    norm(0, 0)
                    norm(1, 1)
                    for n in range(2):
                        dve.wait_ge(sem("transposed"), base + n + 1)
                        norm(2 + n, n)
                    convolve(0, 0)
                    with dve.Fori(0, NCH // 2 - 1) as i:
                        step(2 * i, 0)
                        step(2 * i + 1, 1)
                    step(NCH - 2, 0, True)
                    step(NCH - 1, 1, True)

                    gsteps = Steps(dve, sem("h_step"))

                    def gate(n, par):
                        dve.wait_ge(sem("gate_ready"), n + 1)
                        chunk = n % NCH
                        nc.vector.tensor_tensor(oT[:, par, :, :], cols_of(chunk), uT[:, ds(chunk, 1), :, :].rearrange("p a k c -> p (a k) c"),
                                                ALU.mult).then_inc(sem("gated"), 1)

                    def output(n, par):
                        gsteps.at = n * (1 + STATS)
                        dve.wait_ge(sem("wo_done"), n)
                        gate(n + 1, 1 - par)
                        dve.wait_ge(sem("rnb_ready"), n + 1)
                        dve.wait_ge(sem("wo_done"), n + 1)
                        gsteps.add(nc.vector.tensor_tensor(Hb[:, ds(n * TPC, TPC), :], rn[:, par, :, :],
                                                           ps[:, 6 - 2 * par:8 - 2 * par, :].rearrange("p b (t d) -> p (b t) d", d=D), ALU.add))
                        gsteps.wait()
                        dve.sem_inc(sem("h_saved"), 1)
                        stats(dve, gsteps, n, Hb, mvH)

                    gate(0, 0)
                    with dve.Fori(0, NCH // 2) as i:
                        output(2 * i, 0)
                        output(2 * i + 1, 1)


    def slots(inst):
        n8 = inst * NCH
        first = inst == 0
        with ExitStack() as s3:
            ring = sb("ring", [P, RING, 4 * F], stack=s3)
            nbuf = sb("s_nbuf", [P, 2, TPC, D], stack=s3)
            nT = sb("s_nT", [P, 2, KD, CH], stack=s3)
            zs = sb("zs", [P, KD, PAIRS], stack=s3)
            rsum = sb("rsum", [P, 2], stack=s3)
            pool_pairs(inst, n8, first, ring, nbuf, nT, zs, rsum)
            xq = sb("xq", [P, KD, PAIRS], stack=s3)
            xb = sb("xb", [1, SPLITS, PAIRS], bf16, stack=s3)
            xm = sb("xm", [P, KD, D], stack=s3)
            experts(inst, ring, zs, rsum, xq, xb, xm)
            cross(inst, n8, nbuf, nT, xq, xb, xm)

    def unit_loads(sp, inst, ring, units):
        for u in units:
            g, kind, half = u // 6, u // 2 % 3, u % 2
            use = inst * 4 * 6 + u
            if use >= RING:
                sp.wait_ge(sem("unit_used"), use - RING + 1)
            dst = ring[:, u % RING, :]
            if kind < 2:
                src = A[("e_W1", "e_Wg")[kind]].rearrange("(j g) (k p) f -> g k p j f", g=GROUPS, p=P)[g, half]
                sp.dma_start(dst.rearrange("p (j f) -> p j f", j=4), src).then_inc(sem(f"unit_loaded{u % RING}"), 16)
            else:
                src = A["e_W2"].rearrange("(j g) (h p c) d -> g h p j (c d)", g=GROUPS, h=2, c=4)[g, half]
                sp.dma_start(dst.rearrange("p (j f) -> p j f", j=4), src).then_inc(sem(f"unit_loaded{u % RING}"), 16)

    def pool_pairs(inst, n8, first, ring, nbuf, nT, zs, rsum):
        base, nbase = front
        front[0] += NCH + 1
        front[1] += 2 * NCH + 3
        with ExitStack() as s4:
            scores = sb("scores", [P, 2, T], stack=s4)
            prob = sb("prob", [P, 2, CH], stack=s4)
            probT = nT[:, :, :, :].rearrange("p a k (t e) -> p a (k t) e", e=PAIRS)
            mx8 = sb("mx8", [P, 2, NCH], stack=s4)
            mx = sb("mx", [P, 2], stack=s4)
            nb = sb("nb", [P, 2], stack=s4)
            sums = sb("sums", [P, 2, NCH], stack=s4)
            ssum = sb("ssum", [P, 2], stack=s4)
            sqT = sb("sqT", [P, KD, E], stack=s4)
            qb = scores[:, :, 0:PAIRS]
            with nc.Block() as block:
                @block.sync
                def _(sp):
                    unit_loads(sp, inst, ring, range(RING))

                @block.scalar
                def _(act):
                    root()
                    act.preload_act_table(ACT.Exp)

                    def turned(n, par):
                        act.wait_ge(sem("transposed"), base + n + 1)
                        nc.scalar.activation(nT[:, par, :, :], ps[:, 0:2, :], ACT.Copy).then_inc(sem("nT_ready"), 1)

                    def chunk(n, par):
                        turned(n + 1, 1 - par)
                        act.wait_ge(sem("pool_scored"), n8 + n + 1)
                        nc.scalar.activation(scores[:, :, ds(n * CH, CH)], ps[:, 2 + 2 * par:4 + 2 * par, :],
                                             ACT.Copy).then_inc(sem("scores_saved"), 1)

                    turned(0, 0)
                    with act.Fori(0, NCH // 2) as i:
                        chunk(2 * i, 0)
                        chunk(2 * i + 1, 1)

                    def weigh(n, par):
                        act.wait_ge(sem("prob_turned"), inst * (NCH + 1) + n)
                        for c in range(2):
                            i = nc.scalar.activation(prob[:, c, :], scores[:, c, ds((n % NCH) * CH, CH)], ACT.Exp,
                                                     bias=nb[:, c:c + 1], scale=SCALE, accum_out=sums[:, c, ds(n % NCH, 1)])
                        i.then_inc(sem("weighed"), 1)

                    act.wait_ge(sem("shift_ready"), inst + 1)
                    weigh(0, 0)
                    with act.Fori(0, NCH // 2) as i:
                        weigh(2 * i + 1, 1)
                        weigh(2 * i + 2, 0)

                @block.tensor
                def _(pe):
                    if first:
                        for k in range(KD):
                            i = nc.tensor.transpose(ps[:, 7, k * E:(k + 1) * E], rows16[:, 0, k * P:(k + 1) * P], ident[0:E, 0:E])
                        i.then_inc(sem("fold_pe"), 1)
                        pe.wait_ge(sem("fold_dve"), 1)
                        for c in range(KD):
                            for k in range(KD):
                                i = nc.tensor.matmul(ps[:, 6, c * E:(c + 1) * E], dW["d_Wq"][:, k, c * P:(c + 1) * P],
                                                     sqT[:, k, :], start=(k == 0), stop=(k == KD - 1))
                        i.then_inc(sem("fold_pe"), 1)
                        pe.wait_ge(sem("fold_dve"), 2)
                        for c in range(KD):
                            for k in range(KD):
                                i = nc.tensor.matmul(ps[:, 7, c * PAIRS:(c + 1) * PAIRS], dW["d_WkT"][:, k, c * P:(c + 1) * P],
                                                     qb[:, k, :], start=(k == 0), stop=(k == KD - 1))
                        for c in range(2):
                            for k in range(KD):
                                i = nc.tensor.matmul(ps[:, 6, c:c + 1], qb[:, k, c * P:(c + 1) * P], cols[:, 1, k:k + 1],
                                                     start=(k == 0), stop=(k == KD - 1))
                        i.then_inc(sem("fold_pe"), 1)
                        pe.wait_ge(sem("fold_dve"), 3)

                    def turn(n, par):
                        pe.wait_ge(sem("normed"), nbase + n + 1)
                        pe.wait_ge(sem("nT_ready"), base + n)
                        transposes(nbuf[:, par]).then_inc(sem("transposed"), 1)

                    def chunk(n, par):
                        turn(n + 1, 1 - par)
                        pe.wait_ge(sem("nT_ready"), base + n + 1)
                        pe.wait_ge(sem("scores_saved"), n8 + n)
                        for c in range(2):
                            for k in range(KD):
                                i = nc.tensor.matmul(ps[:, 2 + 2 * par + c, :], pool_q[:, k, c * P:(c + 1) * P],
                                                     nT[:, par, k, :], start=(k == 0), stop=(k == KD - 1))
                        i.then_inc(sem("pool_scored"), 1)

                    turn(0, 0)
                    with pe.Fori(0, NCH // 2) as i:
                        chunk(2 * i, 0)
                        chunk(2 * i + 1, 1)

                    def turn_probs(n, par):
                        pe.wait_ge(sem("weighed"), inst * (NCH + 1) + n + 1)
                        for t in range(TPC):
                            for c in range(2):
                                i = nc.tensor.transpose(ps[:, 2 + 2 * par + t // 2, (t % 2) * PAIRS + c * P:(t % 2) * PAIRS + (c + 1) * P],
                                                        prob[:, c, t * P:(t + 1) * P], ident[:, :])
                        i.then_inc(sem("prob_turned"), 1)

                    def pool(n, par):
                        pe.wait_ge(sem("probT_ready"), inst * (NCH + 1) + n + 1)
                        pe.wait_ge(sem("normed"), nbase + NCH + 2 + n + 1)
                        for t in range(TPC):
                            for c in range(KD):
                                i = nc.tensor.matmul(ps[:, 6 + c, 0:PAIRS], nbuf[:, par, t, c * P:(c + 1) * P], probT[:, par, t, :],
                                                     start=False, stop=False)
                        i.then_inc(sem("pooled"), 1)

                    for c in range(KD):
                        nc.tensor.matmul(ps[:, 6 + c, 0:PAIRS], ident[:, :], zeros[:, :], start=True, stop=False)
                    turn_probs(0, 0)
                    with pe.Fori(0, NCH // 2) as i:
                        turn_probs(2 * i + 1, 1)
                        pool(2 * i, 0)
                        turn_probs(2 * i + 2, 0)
                        pool(2 * i + 1, 1)
                    for c in range(KD):
                        i = nc.tensor.matmul(ps[:, 6 + c, 0:PAIRS], ident[:, :], zeros[:, :], start=False, stop=True)
                    i.then_inc(sem("pool_summed"), 1)

                @block.vector
                def _(dve):
                    s = Steps(dve, sem("pool_start"), inst * 5)
                    if first:
                        f = Steps(dve, sem("fold_step"))
                        dve.wait_ge(sem("fold_pe"), 1)
                        nc.vector.tensor_copy(sqT[:, :, :], ps[:, 7, 0:KD * E].rearrange("p (k e) -> p k e", k=KD)).then_inc(sem("fold_dve"), 1)
                        dve.wait_ge(sem("fold_pe"), 2)
                        for k in range(KD):
                            f.add(nc.vector.tensor_scalar(sqT[:, k, :], ps[:, 6, k * E:(k + 1) * E], cols[:, 0, k:k + 1], None, ALU.add))
                        f.wait()
                        for k in range(KD):
                            i = nc.vector.tensor_tensor(qb[:, k, :].rearrange("p (h s) -> p h s", h=H),
                                                        sqT[:, k, None, :].to_broadcast([P, H, E]),
                                                        mask[:, k, :, None].to_broadcast([P, H, E]), ALU.mult)
                        i.then_inc(sem("fold_dve"), 1)
                        dve.wait_ge(sem("fold_pe"), 3)
                        nc.vector.tensor_copy(pool_q[:, :, :], ps[:, 7, :].rearrange("p (k e) -> p k e", k=KD))
                        nc.vector.tensor_copy(pool_c[:, :], ps[:, 6, 0:2]).then_inc(sem("fold_dve"), 1)
                        dve.wait_ge(sem("fold_dve"), 3)
                    reciprocal_of_root(dve, 3 + inst * 2)
                    norm_tiles(nbuf[:, 0], 0).then_inc(sem("normed"), 1)
                    norm_tiles(nbuf[:, 1], 1).then_inc(sem("normed"), 1)

                    def chunk(n, par):
                        dve.wait_ge(sem("transposed"), base + n + 1)
                        norm_tiles(nbuf[:, par], (n + 2) % NCH).then_inc(sem("normed"), 1)
                        dve.wait_ge(sem("scores_saved"), n8 + n + 1)
                        nc.vector.tensor_reduce(mx8[:, :, ds(n, 1)], scores[:, :, ds(n * CH, CH)], AX.X, ALU.max).then_inc(sem("chunk_max"), 1)

                    with dve.Fori(0, NCH // 2) as i:
                        chunk(2 * i, 0)
                        chunk(2 * i + 1, 1)
                    dve.wait_ge(sem("chunk_max"), n8 + NCH)
                    s.add(nc.vector.tensor_reduce(mx[:, :], mx8[:, :, :], AX.X, ALU.max))
                    s.wait()
                    s.add(nc.vector.tensor_tensor(mx[:, :], mx[:, :], pool_c[:, :], ALU.add))
                    s.wait()
                    s.add(nc.vector.tensor_tensor(nb[:, :], pool_c[:, :], mx[:, :], ALU.subtract))
                    s.wait()
                    nc.vector.tensor_scalar(nb[:, :], nb[:, :], SCALE, None, ALU.mult).then_inc(sem("shift_ready"), 1)
                    dve.wait_ge(sem("transposed"), base + NCH + 1)
                    norm_tiles(nbuf[:, 0], 0).then_inc(sem("normed"), 1)

                    def evacuate(n, par):
                        dve.wait_ge(sem("prob_turned"), inst * (NCH + 1) + n + 1)
                        nc.vector.tensor_copy(probT[:, par, :, :], ps[:, 2 + 2 * par:4 + 2 * par, :].rearrange("p b (t e) -> p (b t) e", e=PAIRS)).then_inc(sem("probT_ready"), 1)

                    def pool(n, par):
                        dve.wait_ge(sem("pooled"), n8 + n)
                        norm_tiles(nbuf[:, 1 - par], (n + 1) % NCH).then_inc(sem("normed"), 1)
                        evacuate(n + 1, 1 - par)

                    evacuate(0, 0)
                    with dve.Fori(0, NCH // 2) as i:
                        pool(2 * i, 0)
                        pool(2 * i + 1, 1)
                    dve.wait_ge(sem("weighed"), (inst + 1) * (NCH + 1))
                    s.add(nc.vector.tensor_reduce(ssum[:, :], sums[:, :, :], AX.X, ALU.add))
                    s.wait()
                    s.add(nc.vector.reciprocal(rsum[:, :], ssum[:, :]))
                    dve.wait_ge(sem("pool_summed"), inst + 1)
                    nc.vector.tensor_copy(zs[:, :, :], ps[:, 6:8, 0:PAIRS])

    def experts(inst, ring, zs, rsum, xq, xb, xm):
        W = dW
        with ExitStack() as s5:
            rm = sb("rm", [P, 2, D], stack=s5)
            aT = sb("aT", [P, KD, E], stack=s5)
            erows = sb("erows", [E, 3, D], stack=s5)
            o16 = sb("o16", [E, D], stack=s5)
            h16 = sb("h16", [E, D], stack=s5)
            s16 = sb("s16", [E, 6], stack=s5)
            m16 = sb("m16", [E, 2], stack=s5)
            r16 = sb("r16", [E, 1], stack=s5)
            hT = sb("e_hT", [P, KD, 32], stack=s5)
            ug = sb("ug", [P, 2, F], stack=s5)
            ua = sb("ua", [P, 2, KF, 4], stack=s5)
            ac = sb("ac", [P, KF, 4], stack=s5)
            ys = sb("ys", [P, F], stack=s5)
            y16 = sb("y16", [E, D], stack=s5)
            oT = sb("e_oT", [P, KD, E], stack=s5)
            kv = sb("kv", [P, 2, KD, E], stack=s5)
            kb = sb("kb", [P, 2, KD, PAIRS], stack=s5)
            rest = sb("rest", [1, PAIRS], stack=s5)
            a0, p0, v0, g0 = inst * 2, inst * 6, inst * 9, inst * GROUPS
            with nc.Block() as block:
                @block.sync
                def _(sp):
                    sp.dma_start(erows[:, :, :], A["erows"]).then_inc(sem("erows_loaded"), 16)
                    unit_loads(sp, inst, ring, range(RING, UNITS))
                    sp.wait_ge(sem("y_rows"), inst + 1)
                    sp.dma_start(y16[:, :], ys[0:P:32, :].rearrange("j (g d) -> j g d", g=GROUPS)).then_inc(sem("y_loaded"), 16)

                @block.scalar
                def _(act):
                    act.wait_ge(sem("o_var"), inst + 1)
                    nc.scalar.activation(r16[:, :], m16[:, 1:2], ACT.Sqrt, bias=eps[0:E, :]).then_inc(sem("o_root"), 1)
                    act.preload_act_table(ACT.Silu)
                    for g in range(GROUPS):
                        act.wait_ge(sem("g_up"), g0 + g + 1)
                        act.wait_ge(sem("picked"), g0 + g)
                        nc.scalar.activation(ug[:, 1, :], ps[:, 2:4, :].rearrange("p b c -> p (b c)"), ACT.Copy).then_inc(sem("g_saved"), 1)
                        act.wait_ge(sem("biased"), g0 + g + 1)
                        nc.scalar.activation(ua[:, :, :, :], ua[:, :, :, :], ACT.Silu).then_inc(sem("silu_done"), 1)

                @block.tensor
                def _(pe):
                    for c in range(2):
                        for k in range(KD):
                            i = nc.tensor.matmul(ps[:, 0, c * D:(c + 1) * D], zs[:, k, c * P:(c + 1) * P], W["d_Wv"][:, k, :],
                                                 start=(k == 0), stop=(k == KD - 1))
                    i.then_inc(sem("slot_pe"), 1)
                    pe.wait_ge(sem("slot_dve"), v0 + 1)
                    for c in range(KD):
                        for k in range(2):
                            i = nc.tensor.matmul(ps[:, 1, c * E:(c + 1) * E], rm[:, k, c * P:(c + 1) * P], slotsel[:, :],
                                                 start=(k == 0), stop=(k == 1))
                    i.then_inc(sem("slot_pe"), 1)
                    pe.wait_ge(sem("slot_dve"), v0 + 2)
                    for k in range(KD):
                        i = nc.tensor.matmul(ps[0:E, 2, 0:D], aT[:, k, :], W["d_Wo"][:, k, :], start=(k == 0), stop=(k == KD - 1))
                    i.then_inc(sem("slot_pe"), 1)
                    pe.wait_ge(sem("slot_dve"), v0 + 3)
                    for k in range(KD):
                        i = nc.tensor.transpose(ps[:, 7, k * E:(k + 1) * E], h16[:, k * P:(k + 1) * P], ident[0:E, 0:E])
                    i.then_inc(sem("slot_pe"), 1)
                    pe.wait_ge(sem("slot_dve"), v0 + 4)
                    u = 0

                    def arrived():
                        before = inst * ((UNITS - u % RING + RING - 1) // RING)
                        pe.wait_ge(sem(f"unit_loaded{u % RING}"), 16 * (before + u // RING + 1))

                    for g in range(GROUPS):
                        for m in range(2):
                            if g or inst:
                                pe.wait_ge(sem(("u_saved", "g_saved")[m]), g0 + g)
                            for k in range(KD):
                                arrived()
                                for b in range(2):
                                    for j in range(4):
                                        i = nc.tensor.matmul(ps[32 * j:32 * j + 32, 2 * m + b, :], hT[:, k, :],
                                                             ring[:, u % RING, j * F + b * CH:j * F + (b + 1) * CH],
                                                             start=(k == 0), stop=(k == KD - 1))
                                if k == 0:
                                    i.then_inc(sem("unit_used"), 1)
                                u += 1
                            i.then_inc(sem("unit_used"), 1)
                            pe.wait_ge(sem("unit_used"), inst * UNITS + u)
                            pe.sem_inc(sem(("u_up", "g_up")[m]), 1)
                        pe.wait_ge(sem("u_saved"), g0 + g + 1)
                        pe.wait_ge(sem("g_saved"), g0 + g + 1)
                        for m in range(2):
                            for f in range(KF):
                                at = (f // 4) * CH + f % 4
                                i = nc.tensor.matmul(ps[:, 4, (m * KF + f) * 4:(m * KF + f + 1) * 4],
                                                     ug[:, m, at:at + 4 * (P - 1) + 1:4], pick[:, g, :], start=True, stop=True)
                        i.then_inc(sem("picked"), 1)
                        pe.wait_ge(sem("gated16"), g0 + g + 1)
                        for half in range(2):
                            arrived()
                            for c in range(4):
                                for j in range(4):
                                    i = nc.tensor.matmul(ps[32 * j:32 * j + 1, 5 + g // 2, (g % 2) * D:(g % 2 + 1) * D],
                                                         ac[:, 4 * half + c, j:j + 1],
                                                         ring[:, u % RING, j * F + c * D:j * F + (c + 1) * D],
                                                         start=(half + c == 0), stop=(half + c == 4))
                            i.then_inc(sem("unit_used"), 1)
                            u += 1
                    pe.wait_ge(sem("slot_dve"), v0 + 5)
                    for k in range(KD):
                        i = nc.tensor.transpose(ps[:, 7, k * E:(k + 1) * E], o16[:, k * P:(k + 1) * P], ident[0:E, 0:E])
                    i.then_inc(sem("slot_pe"), 1)
                    pe.wait_ge(sem("slot_dve"), v0 + 6)
                    for m, name in enumerate(("c_Wk", "c_Wv")):
                        for c in range(KD):
                            for k in range(KD):
                                i = nc.tensor.matmul(ps[:, 0, (m * KD + c) * E:(m * KD + c + 1) * E], W[name][:, k, c * P:(c + 1) * P],
                                                     oT[:, k, :], start=(k == 0), stop=(k == KD - 1))
                    i.then_inc(sem("slot_pe"), 1)
                    pe.wait_ge(sem("slot_dve"), v0 + 8)
                    for c in range(KD):
                        for k in range(KD):
                            nc.tensor.matmul(ps[:, 1, c * PAIRS:(c + 1) * PAIRS], W["c_WqT"][:, k, c * P:(c + 1) * P],
                                             kb[:, 0, k, :], start=(k == 0), stop=(k == KD - 1))
                    for k in range(KD):
                        nc.tensor.matmul(ps[0:1, 2, 0:PAIRS], cols[:, 3, k:k + 1], kb[:, 0, k, :], start=(k == 0), stop=(k == KD - 1))
                    for c in range(2):
                        for k in range(KD):
                            i = nc.tensor.matmul(ps[:, 3, c * D:(c + 1) * D], kb[:, 1, k, c * P:(c + 1) * P], W["c_Wo"][:, k, :],
                                                 start=(k == 0), stop=(k == KD - 1))
                    i.then_inc(sem("folded"), 1)

                @block.vector
                def _(dve):
                    s = Steps(dve, sem("slot_step"), inst * 7)
                    dve.wait_ge(sem("slot_pe"), p0 + 1)
                    for c in range(2):
                        i = nc.vector.scalar_tensor_tensor(rm[:, c, :].rearrange("p (h d) -> p h d", h=H),
                                                           ps[:, 0, c * D:(c + 1) * D].rearrange("p (h d) -> p h d", h=H),
                                                           rsum[:, c:c + 1], mask[:, c, :, None].to_broadcast([P, H, HD]),
                                                           ALU.mult, ALU.mult)
                    i.then_inc(sem("slot_dve"), 1)
                    dve.wait_ge(sem("slot_pe"), p0 + 2)
                    for k in range(KD):
                        i = nc.vector.tensor_scalar(aT[:, k, :], ps[:, 1, k * E:(k + 1) * E], cols[:, 2, k:k + 1], None, ALU.add)
                    i.then_inc(sem("slot_dve"), 1)
                    dve.wait_ge(sem("slot_pe"), p0 + 3)
                    s.add(nc.vector.tensor_tensor(o16[:, :], ps[0:E, 2, 0:D], rows16[:, 1, :], ALU.add))
                    s.wait()
                    s.add(nc.vector.tensor_tensor(o16[:, :], o16[:, :], rows16[:, 0, :], ALU.add))
                    s.wait()
                    s.add(nc.vector.bn_stats(s16[:, :], o16[:, :]))
                    s.wait()
                    nc.vector.bn_aggr(m16[:, :], s16[:, :]).then_inc(sem("o_var"), 1)
                    dve.wait_ge(sem("o_root"), inst + 1)
                    s.add(nc.vector.reciprocal(r16[:, :], r16[:, :]))
                    s.wait()
                    s.add(nc.vector.tensor_scalar(h16[:, :], o16[:, :], m16[:, 0:1], r16[:, :], ALU.subtract, ALU.mult))
                    s.wait()
                    dve.wait_ge(sem("erows_loaded"), 16 * (inst + 1))
                    s.add(nc.vector.tensor_tensor(h16[:, :], h16[:, :], erows[:, 0, :], ALU.mult))
                    s.wait()
                    nc.vector.tensor_tensor(h16[:, :], h16[:, :], erows[:, 1, :], ALU.add).then_inc(sem("slot_dve"), 1)
                    dve.wait_ge(sem("slot_pe"), p0 + 4)
                    hp = ps[:, 7, 0:KD * E].rearrange("p (k e) -> p k e", k=KD)
                    nc.vector.tensor_copy(hT[:, :, 0:E], hp)
                    nc.vector.tensor_copy(hT[:, :, E:2 * E], hp).then_inc(sem("slot_dve"), 1)
                    def save_y(g):
                        dve.wait_ge(sem("unit_used"), inst * UNITS + 6 * (g + 1))
                        for j in range(4):
                            i = nc.vector.tensor_copy(ys[32 * j:32 * j + 1, g * D:(g + 1) * D],
                                                      ps[32 * j:32 * j + 1, 5 + g // 2, (g % 2) * D:(g % 2 + 1) * D])
                        return i

                    for g in range(GROUPS):
                        if g:
                            save_y(g - 1)
                        dve.wait_ge(sem("u_up"), g0 + g + 1)
                        dve.wait_ge(sem("picked"), g0 + g)
                        nc.vector.tensor_copy(ug[:, 0, :], ps[:, 0:2, :].rearrange("p b c -> p (b c)")).then_inc(sem("u_saved"), 1)
                        dve.wait_ge(sem("picked"), g0 + g + 1)
                        nc.vector.tensor_tensor(ua[:, :, :, :].rearrange("p m f j -> p m (f j)"),
                                                ps[:, 4, 0:2 * KF * 4].rearrange("p (m x) -> p m x", m=2),
                                                eb[:, :, g, :, :].rearrange("p m f j -> p m (f j)"), ALU.add).then_inc(sem("biased"), 1)
                        dve.wait_ge(sem("silu_done"), g0 + g + 1)
                        nc.vector.tensor_tensor(ac[:, :, :], ua[:, 0, :, :], ua[:, 1, :, :], ALU.mult).then_inc(sem("gated16"), 1)
                    save_y(GROUPS - 1).then_inc(sem("y_rows"), 1)
                    s.add(nc.vector.tensor_tensor(o16[:, :], o16[:, :], erows[:, 2, :], ALU.add))
                    s.wait()
                    dve.wait_ge(sem("y_loaded"), 16 * (inst + 1))
                    nc.vector.tensor_tensor(o16[:, :], o16[:, :], y16[:, :], ALU.add).then_inc(sem("slot_dve"), 1)
                    dve.wait_ge(sem("slot_pe"), p0 + 5)
                    nc.vector.tensor_copy(oT[:, :, :], hp).then_inc(sem("slot_dve"), 1)
                    dve.wait_ge(sem("slot_pe"), p0 + 6)
                    for m in range(2):
                        for k in range(KD):
                            i = nc.vector.tensor_scalar(kv[:, m, k, :], ps[:, 0, (m * KD + k) * E:(m * KD + k + 1) * E],
                                                        cols[:, 4 + m, k:k + 1], None, ALU.add)
                    i.then_inc(sem("slot_dve"), 1)
                    dve.wait_ge(sem("slot_dve"), v0 + 7)
                    for m in range(2):
                        for k in range(KD):
                            i = nc.vector.tensor_tensor(kb[:, m, k, :].rearrange("p (h s) -> p h s", h=H),
                                                        kv[:, m, k, None, :].to_broadcast([P, H, E]),
                                                        mask[:, k, :, None].to_broadcast([P, H, E]), ALU.mult)
                    i.then_inc(sem("slot_dve"), 1)
                    dve.wait_ge(sem("folded"), inst + 1)
                    nc.vector.tensor_copy(xq[:, :, :], ps[:, 1, :].rearrange("p (k e) -> p k e", k=KD))
                    b = Steps(dve, sem("xb_step"), inst * 3)
                    bias = ps[0:1, 2, 0:PAIRS]
                    b.add(nc.vector.tensor_copy(xb[:, 0, :], bias))
                    b.wait()
                    b.add(nc.vector.tensor_tensor(rest[:, :], bias, xb[:, 0, :], ALU.subtract))
                    b.wait()
                    b.add(nc.vector.tensor_copy(xb[:, 1, :], rest[:, :]))
                    b.wait()
                    nc.vector.tensor_tensor(xb[:, 2, :], rest[:, :], xb[:, 1, :], ALU.subtract)
                    nc.vector.tensor_copy(xm[:, :, :], ps[:, 3, :].rearrange("p (k e) -> p k e", k=KD)).then_inc(sem("slot_dve"), 1)

    def cross(inst, n8, nbuf, nT, xq, xb, xm):
        base, nbase = front
        front[0] += NCH + 1
        front[1] += NCH + 2
        with ExitStack() as s6:
            pr = sb("pr", [P, 2, TPC, H, E], stack=s6)
            xb3 = sb("xb3", [SPLITS, PAIRS], bf16, stack=s6)
            prT = sb("prT", [P, TPC, 2, P], stack=s6)
            mxh = sb("mxh", [P, TPC * H], stack=s6)
            smh = sb("smh", [P, TPC * H], stack=s6)
            flat = [pr[:, par, :, :, :].rearrange("p t h s -> p (t h) s") for par in range(2)]
            sbank = ps[:, 2:4, :].rearrange("p b (t s) -> p (b t) s", s=E)

            def steps_of(engine, step):
                for n in range(2):
                    step(n, n, False)
                with engine.Fori(1, NCH // 2 - 1) as i:
                    step(2 * i, 0, False)
                    step(2 * i + 1, 1, False)
                for n in range(NCH - 2, NCH):
                    step(n, n % 2, True)

            with nc.Block() as block:
                @block.sync
                def _(sp):
                    for r in range(SPLITS):
                        sp.dma_start(xb3[r:r + 1, :], xb[:, r, :]).then_inc(sem("xb_loaded"), 16)
                    if inst == 1:
                        ov = out.rearrange("a (n p) d -> (a p) n d", p=P)
                        for n in range(NCH):
                            sp.wait_ge(sem("xx_updated"), n8 + n + 1)
                            sp.dma_start(ov[:, n * TPC:(n + 1) * TPC, :], X[:, n * TPC:(n + 1) * TPC, :]).then_inc(sem("stored"), 16)
                        sp.wait_ge(sem("stored"), 16 * NCH)

                @block.gpsimd
                def _(pool):
                    pool.wait_ge(sem("bo_step"), 1)
                    with pool.Fori(0, NCH) as n:
                        pool.wait_ge(sem("normed"), nbase + n + 1)
                        xc = X[:, ds(n * TPC, TPC), :]
                        nc.gpsimd.tensor_tensor(xc, xc, bo_half[:, None, :].to_broadcast([P, TPC, D]), ALU.add).then_inc(sem("xbias_added"), 1)

                @block.scalar
                def _(act):
                    act.preload_act_table(ACT.Exp)

                    def turned(n, par):
                        act.wait_ge(sem("transposed"), base + n + 1)
                        nc.scalar.activation(nT[:, par, :, :], ps[:, 0:2, :], ACT.Copy).then_inc(sem("nT_ready"), 1)

                    def weigh(n, par):
                        act.wait_ge(sem("x_shifted"), n8 + n + 1)
                        nc.scalar.activation(pr[:, par], pr[:, par], ACT.Exp, scale=SCALE).then_inc(sem("x_exp"), 1)

                    def step(n, par, tail):
                        if not (tail and n == NCH - 1):
                            weigh(n + 1, 1 - par)
                        act.wait_ge(sem("pr_turned"), n8 + n + 1)
                        act.wait_ge(sem("x_out"), n8 + n)
                        nc.scalar.activation(prT[:, :, :, :], ps[:, 4:6, :], ACT.Copy).then_inc(sem("prT_ready"), 1)
                        if not tail:
                            turned(n + 3, 1 - par)

                    for n in range(2):
                        turned(n, n)
                    weigh(0, 0)
                    turned(2, 0)
                    steps_of(act, step)

                @block.tensor
                def _(pe):
                    def turn(n, par):
                        pe.wait_ge(sem("normed"), nbase + n + 1)
                        pe.wait_ge(sem("nT_ready"), base + n)
                        transposes(nbuf[:, par]).then_inc(sem("transposed"), 1)

                    def score(n, par):
                        pe.wait_ge(sem("nT_ready"), base + n + 1)
                        pe.wait_ge(sem("x_shifted"), n8 + n)
                        for t in range(TPC):
                            o = ps[:, 2 + t // 2, (t % 2) * PAIRS:(t % 2 + 1) * PAIRS]
                            for k in range(KD):
                                nc.tensor.matmul(o, nT[:, par, k, t * P:(t + 1) * P], xq[:, k, :], start=(k == 0), stop=False)
                            i = nc.tensor.matmul(o, ones[:, :], xb3[:, :], start=False, stop=True)
                        i.then_inc(sem("x_scored"), 1)

                    def step(n, par, tail):
                        if not tail:
                            score(n + 2, par)
                        pe.wait_ge(sem("pr_ready"), n8 + n + 1)
                        pe.wait_ge(sem("prT_ready"), n8 + n)
                        for t in range(TPC):
                            for c in range(2):
                                i = nc.tensor.transpose(ps[:, 4 + t // 2, (t % 2) * 2 * P + c * P:(t % 2) * 2 * P + (c + 1) * P],
                                                        pr[:, par, t, 8 * c:8 * c + 8, :].rearrange("p h s -> p (h s)"), ident[:, :])
                        i.then_inc(sem("pr_turned"), 1)
                        if not tail:
                            turn(n + 3, 1 - par)
                        pe.wait_ge(sem("prT_ready"), n8 + n + 1)
                        pe.wait_ge(sem("xx_updated"), n8 + n)
                        for t in range(TPC):
                            for c in range(2):
                                i = nc.tensor.matmul(ps[:, 6 + t // 2, (t % 2) * D:(t % 2 + 1) * D], prT[:, t, c, :], xm[:, c, :],
                                                     start=(c == 0), stop=(c == 1))
                        i.then_inc(sem("x_out"), 1)

                    turn(0, 0)
                    turn(1, 1)
                    pe.wait_ge(sem("xb_loaded"), 16 * SPLITS * (inst + 1))
                    score(0, 0)
                    turn(2, 0)
                    score(1, 1)
                    steps_of(pe, step)

                @block.vector
                def _(dve):
                    if inst == 0:
                        nc.vector.tensor_scalar(bo_half[:, :], bo_half[:, :], 0.5, None, ALU.mult).then_inc(sem("bo_step"), 1)
                    steps = Steps(dve, sem("x_step"))
                    sums = Steps(dve, sem("x_sum_step"))

                    def norm(n, par):
                        norm_tiles(nbuf[:, par], n % NCH).then_inc(sem("normed"), 1)

                    def shift(n, par):
                        dve.wait_ge(sem("x_scored"), n8 + n + 1)
                        dve.wait_ge(sem("x_shifted"), n8 + n)
                        nc.vector.tensor_reduce(mxh[:, :], sbank, AX.X, ALU.max).then_inc(sem("x_max"), 1)
                        dve.wait_ge(sem("x_max"), n8 + n + 1)
                        nc.vector.tensor_tensor(flat[par], sbank, mxh[:, :, None].to_broadcast([P, TPC * H, E]), ALU.subtract).then_inc(sem("x_shifted"), 1)

                    def update(n):
                        dve.wait_ge(sem("x_out"), n8 + n + 1)
                        dve.wait_ge(sem("xbias_added"), n8 + n + 1)
                        xc = X[:, ds(n * TPC, TPC), :]
                        nc.vector.scalar_tensor_tensor(xc, ps[:, 6:8, :].rearrange("p b (t d) -> p (b t) d", d=D),
                                                       0.5, xc, ALU.mult, ALU.add).then_inc(sem("xx_updated"), 1)
                        if inst == 0:
                            dve.wait_ge(sem("xx_updated"), n8 + n + 1)
                            steps.at = n * STATS
                            stats(dve, steps, n)

                    def step(n, par, tail):
                        if not (tail and n == NCH - 1):
                            dve.wait_ge(sem("pr_turned"), n8 + n)
                            shift(n + 1, 1 - par)
                        dve.wait_ge(sem("x_exp"), n8 + n + 1)
                        dve.wait_ge(sem("pr_ready"), n8 + n)
                        sums.at = (n8 + n) * 2
                        sums.add(nc.vector.tensor_reduce(smh[:, :], flat[par], AX.X, ALU.add))
                        sums.wait()
                        sums.add(nc.vector.reciprocal(smh[:, :], smh[:, :]))
                        sums.wait()
                        nc.vector.tensor_tensor(flat[par], flat[par], smh[:, :, None].to_broadcast([P, TPC * H, E]), ALU.mult).then_inc(sem("pr_ready"), 1)
                        if not (isinstance(n, int) and n == 0):
                            update(n - 1)
                        if not tail:
                            dve.wait_ge(sem("transposed"), base + n + 3)
                            norm(n + 4, par)

                    norm(0, 0)
                    norm(1, 1)
                    dve.wait_ge(sem("transposed"), base + 1)
                    norm(2, 0)
                    shift(0, 0)
                    dve.wait_ge(sem("transposed"), base + 2)
                    norm(3, 1)
                    steps_of(dve, step)
                    update(NCH - 1)

    def attention():
        with ExitStack() as s7:
            wout = sb("wout", [P, KD, D], stack=s7)
            bout = sb("bout", [P, D], stack=s7)
            V = sb("V", [P, KT, D], stack=s7)
            parts = nc.dram_tensor("qk_parts", (2, SPLITS, D, T), bf16, kind="Internal").ap()
            project(wout, bout, V, parts)
            O = sb("O", [P, ROUNDS + 1, TPC, NCH // 2, HD], stack=s7)
            attend(V, O, parts)
            project_out(wout, bout, O)

    def project(wout, bout, V, parts):
        base, nbase = front
        front[0] += NCH + 1
        front[1] += NCH + 2
        with ExitStack() as s8:
            wqkv = sb("wqkv", [P, KD, 3 * D], stack=s8)
            nbuf = sb("p_nbuf", [P, 2, TPC, D], stack=s8)
            nT = sb("p_nT", [P, 2, KD, CH], stack=s8)
            rope = sb("rope", [P, 2, 2, CH], stack=s8)
            ITEMS = 4
            ta = sb("ta", [P, ITEMS, CH], stack=s8)
            tb = sb("tb", [P, ITEMS, CH], stack=s8)
            part = sb("part", [P, ITEMS, SPLITS, CH], bf16, stack=s8)
            slot = lambda m, s: s if m < 2 else SPLITS - 1 - s
            with nc.Block() as block:
                @block.sync
                def _(sp):
                    for dst, src in ((wqkv, A["wqkv"].rearrange("(k p) f -> p k f", p=P)),
                                     (wout, A["woutT"].rearrange("(k p) f -> p k f", p=P)),
                                     (bout, A["b_out"].partition_broadcast(P))):
                        sp.dma_start(dst[...], src).then_inc(sem("qkv_loaded"), 16)

                    def chunk(n, par):
                        if not isinstance(n, int):
                            sp.wait_ge(sem("rotated"), (n - 1) * ITEMS)
                        sp.dma_start(rope[:, par, :, :], A["c_rope"][:, :, ds(n * CH, CH)]).then_inc(sem(f"rope_loaded{par}"), 16)

                    def stores(n):
                        for m in range(ITEMS):
                            sp.wait_ge(sem("split_done"), (n + 1) * ITEMS + m + 1)
                            sp.dma_start(parts[m // 2, :, (m % 2) * P:(m % 2 + 1) * P, ds(n * CH, CH)].rearrange("s p c -> p s c"),
                                         part[:, m, :, :]).then_inc(sem(f"part_stored{m}"), 16)

                    chunk(0, 0)
                    chunk(1, 1)
                    with sp.Fori(0, NCH // 2 - 1) as i:
                        stores(2 * i)
                        chunk(2 * i + 2, 0)
                        stores(2 * i + 1)
                        chunk(2 * i + 3, 1)
                    stores(NCH - 2)
                    stores(NCH - 1)
                    for m in range(ITEMS):
                        sp.wait_ge(sem(f"part_stored{m}"), 16 * NCH)

                @block.scalar
                def _(act):
                    root()

                    def turned(n, par):
                        act.wait_ge(sem("transposed"), base + n + 1)
                        nc.scalar.activation(nT[:, par, :, :], ps[:, 0:2, :], ACT.Copy).then_inc(sem("nT_ready"), 1)

                    def chunk(n, par):
                        turned(n + 1, 1 - par)
                        act.wait_ge(sem("v_done"), n + 1)
                        nc.scalar.activation(V[:, ds(n * TPC, TPC), :], ps[:, 6:8, :].rearrange("p b (t d) -> p (b t) d", d=D),
                                             ACT.Copy).then_inc(sem("v_saved"), 1)
                        for m in range(ITEMS + 1):
                            if m < ITEMS:
                                act.wait_ge(sem(f"part_stored{m}"), 16 * n)
                                act.wait_ge(sem("rotated"), n * ITEMS + m + 1)
                                nc.scalar.activation(part[:, m, slot(m, 0), :], ta[:, m, :], ACT.Copy).then_inc(sem("first_done"), 1)
                            if m:
                                act.wait_ge(sem("rest_done"), n * ITEMS + m)
                                nc.scalar.activation(part[:, m - 1, slot(m - 1, 1), :], tb[:, m - 1, :], ACT.Copy).then_inc(sem("middle_done"), 1)

                    turned(0, 0)
                    with act.Fori(0, NCH // 2) as i:
                        chunk(2 * i, 0)
                        chunk(2 * i + 1, 1)

                @block.tensor
                def _(pe):
                    def turn(n, par):
                        pe.wait_ge(sem("normed"), nbase + n + 1)
                        pe.wait_ge(sem("nT_ready"), base + n)
                        transposes(nbuf[:, par]).then_inc(sem("transposed"), 1)

                    def chunk(n, par):
                        turn(n + 1, 1 - par)
                        pe.wait_ge(sem("nT_ready"), base + n + 1)
                        pe.wait_ge(sem("v_saved"), n)
                        for t in range(TPC):
                            for k in range(KD):
                                i = nc.tensor.matmul(ps[:, 6 + t // 2, (t % 2) * D:(t % 2 + 1) * D],
                                                     nT[:, par, k, t * P:(t + 1) * P], wqkv[:, k, 2 * D:3 * D],
                                                     start=(k == 0), stop=(k == KD - 1))
                        i.then_inc(sem("v_done"), 1)
                        for m in range(ITEMS):
                            pe.wait_ge(sem("banks_read"), n * ITEMS + m + 1)
                            for k in range(KD):
                                i = nc.tensor.matmul(ps[:, 2 + m, :], wqkv[:, k, m * P:(m + 1) * P], nT[:, par, k, :],
                                                     start=(k == 0), stop=(k == KD - 1))
                            i.then_inc(sem("qk_done"), 1)

                    pe.wait_ge(sem("qkv_loaded"), 48)
                    turn(0, 0)
                    with pe.Fori(0, NCH // 2) as i:
                        chunk(2 * i, 0)
                        chunk(2 * i + 1, 1)

                @block.gpsimd
                def _(pool):
                    pool.sem_inc(sem("split_done"), ITEMS)
                    with pool.Fori(0, NCH) as n:
                        for m in range(ITEMS + 1):
                            if m < ITEMS:
                                pool.wait_ge(sem("first_done"), n * ITEMS + m + 1)
                                nc.gpsimd.tensor_tensor(tb[:, m, :], ta[:, m, :], part[:, m, slot(m, 0), :], ALU.subtract).then_inc(sem("rest_done"), 1)
                            if m:
                                pool.wait_ge(sem("middle_done"), n * ITEMS + m)
                                nc.gpsimd.tensor_tensor(part[:, m - 1, slot(m - 1, 2), :], tb[:, m - 1, :], part[:, m - 1, slot(m - 1, 1), :], ALU.subtract).then_inc(sem("split_done"), 1)

                @block.vector
                def _(dve):
                    dve.sem_inc(sem("banks_read"), ITEMS)
                    reciprocal_of_root(dve, 4)
                    steps = Steps(dve, sem("rot_step"))
                    norm_tiles(nbuf[:, 0], 0).then_inc(sem("normed"), 1)
                    norm_tiles(nbuf[:, 1], 1).then_inc(sem("normed"), 1)

                    def chunk(n, par):
                        steps.at = n * 2 * ITEMS
                        dve.wait_ge(sem("transposed"), base + n + 1)
                        norm_tiles(nbuf[:, par], (n + 2) % NCH).then_inc(sem("normed"), 1)
                        dve.wait_ge(sem(f"rope_loaded{par}"), 16 * (n // 2) + 16)
                        for m in range(ITEMS):
                            scale = SCALE if m < 2 else 1.0
                            dve.wait_ge(sem("qk_done"), n * ITEMS + m + 1)
                            dve.wait_ge(sem("split_done"), n * ITEMS + m + 1)
                            steps.add(nc.vector.scalar_tensor_tensor(ta[:, m, :], ps[:, 2 + m, :], scale, rope[:, par, 0, :], ALU.mult, ALU.mult))
                            nc.vector.stream_shuffle(tb[:, m, :], ps[:, 2 + m, :], [p ^ (HD // 2) for p in range(32)]).then_inc(sem("banks_read"), 1)
                            dve.wait_ge(sem("banks_read"), (n + 1) * ITEMS + m + 1)
                            steps.add(nc.vector.scalar_tensor_tensor(tb[:, m, :], tb[:, m, :], scale, rope[:, par, 1, :], ALU.mult, ALU.mult))
                            steps.wait()
                            nc.vector.tensor_tensor(ta[:, m, :], ta[:, m, :], tb[:, m, :], ALU.add).then_inc(sem("rotated"), 1)

                    with dve.Fori(0, NCH // 2) as i:
                        chunk(2 * i, 0)
                        chunk(2 * i + 1, 1)

    def attend(V, O, parts):
        SC, AV, MB = 0, 4, 5
        SLOT0 = MAXES + 2 + AHEAD
        SLOTN = SLOT0 + SLOTS * (ROUNDS - 1) + 2
        QL = 2 * len(RUNS) * 16
        with ExitStack() as s9:
            qop = sb("qop", [ROWS, 3, T], bf16, stack=s9)
            kop = sb("kop", [ROWS, 3, T], bf16, stack=s9)
            vst = sb("vst", [P, KT, 32], stack=s9)
            pb = sb("pb", [P, PRING, CH], stack=s9)
            osb = sb("osb", [P, CH], stack=s9)
            mp = sb("mp", [P, HALF // P, NCH], stack=s9)
            mq = sb("mq", [P, HALF // P], stack=s9)
            mr = sb("mr", [P, HALF // P], stack=s9)
            ms = sb("ms", [P, SPLITS, HALF // P], bf16, stack=s9)
            msb = sb("msb", [SPLITS * HALF // P, P], bf16, stack=s9)
            rc = sb("rc", [P, 2, 2, 4], stack=s9)
            psb = ps[:, :, :].bitcast(bf16)

            def turn_of(m):
                return m + (m > OUT_AT[0]) + (m > OUT_AT[1]) + 2 * (m > MAX_AT)

            def maximum_of(m):
                return (m + AHEAD) % MAXES, m + AHEAD >= MAXES

            with nc.Block() as block:
                @block.sync
                def _(sp):
                    def load(h, b):
                        r = 0
                        for q, k, n in RUNS:
                            for op, which, first in ((qop, 0, q), (kop, 1, k)):
                                sp.dma_start(op[r * HD:(r + n) * HD, ds(b, 1), :].rearrange("p a c -> p (a c)"),
                                             parts[which, first:first + n, ds(h * HD, HD), :]).then_inc(sem("head_loaded"), 16)
                            r += n

                    def shift_rows(event, b, half):
                        sp.wait_ge(sem("rows_ready"), event + 1)
                        for r in range(SPLITS):
                            n = HALF // P
                            sp.dma_start(qop[QK_ROWS + r:QK_ROWS + r + 1, ds(b, 1), half * HALF:(half + 1) * HALF].rearrange("r a (t q) -> r (a t) q", q=P),
                                         msb[r * n:(r + 1) * n, :]).then_inc(sem("rows_loaded"), 16)

                    load(0, 0)
                    sp.wait_ge(sem("head_loaded"), QL)
                    load(1, 1)
                    shift_rows(0, 0, 0)

                    def rows(h):
                        shift_rows(2 * h + 1, h % 3, 1)
                        shift_rows(2 * h + 2, (h + 1) % 3, 0)

                    with sp.Fori(0, H - 2) as h:
                        sp.wait_ge(sem("av_done"), 2 * KT * h + 2)
                        sp.wait_ge(sem("head_loaded"), QL * (h + 2))
                        load(h + 2, (h + 2) % 3)
                        rows(h)
                    sp.wait_ge(sem("head_loaded"), QL * H)
                    sp.sem_inc(sem("head_loaded"), QL)
                    rows(H - 2)
                    shift_rows(ROUNDS - 1, (H - 1) % 3, 1)
                    sp.wait_ge(sem("rows_loaded"), 16 * SPLITS * ROUNDS)

                @block.scalar
                def _(act):
                    act.sem_inc(sem("exp_done"), 4)
                    act.preload_act_table(ACT.Exp)

                    def save(it, turned):
                        act.wait_ge(sem("av_done"), KT * it + 2)
                        act.wait_ge(sem("slot_done"), turned)
                        nc.scalar.activation(osb[:, :], ps[:, AV, :], ACT.Copy).then_inc(sem("o_saved"), 1)

                    with act.Fori(0, ROUNDS) as it:
                        for kt in range(KT):
                            act.wait_ge(sem("av_done"), it * KT + kt + 1)
                            for j in range(4):
                                act.wait_ge(sem("score_done"), 4 * KT * it + 4 * kt + j + 1)
                                nc.scalar.activation(pb[:, (4 * kt + j) % PRING, :], ps[:, SC + j, :], ACT.Exp).then_inc(sem("exp_done"), 1)
                            if kt == 0:
                                save(it, SLOT0 - SLOTS + SLOTS * it + turn_of(OUT_AT[1]) + 2)
                    save(ROUNDS, SLOTN)

                @block.gpsimd
                def _(pool):
                    s = Steps(pool, sem("v_init"))
                    for b in range(3):
                        s.add(nc.gpsimd.memset(kop[QK_ROWS:ROWS, b, :], 1.0))
                        s.wait()
                    s.add(nc.gpsimd.memset(pb[:, PRING // 2:PRING, :], 1.0))
                    s.add(nc.gpsimd.memset(vst[:, :, :], 0.0))
                    s.wait()
                    s.add(nc.gpsimd.memset(vst[:, :, HD:HD + 1], 1.0))
                    s.wait()

                    def copy(h, g):
                        nc.gpsimd.tensor_copy(vst[:, 8 * g:8 * g + 8, 0:HD], V[:, 8 * g:8 * g + 8, ds(h * HD, HD)]).then_inc(sem("v_ready"), 1)

                    for g in range(4):
                        copy(0, g)
                    with pool.Fori(0, H - 1) as h:
                        for g in range(4):
                            pool.wait_ge(sem("av_done"), (2 * h + 1) * KT + 8 * (g + 1) + 2)
                            copy(h + 1, g)

                @block.tensor
                def _(pe):
                    pe.sem_inc(sem("av_done"), 1)

                    def max_slot(slot0, k, b, m, half):
                        slot = slot0 + k
                        pe.wait_ge(sem("slot_used"), slot + 1)
                        nc.tensor.matmul(ps[:, MB + k % MRING, :], qop[0:QK_ROWS, ds(b, 1), ds(half * HALF + (m // NCH) * P, P)],
                                         kop[0:QK_ROWS, ds(b, 1), (m % NCH) * CH:(m % NCH + 1) * CH],
                                         start=True, stop=True).then_inc(sem("slot_done"), 1)

                    def turn_outputs(slot0, k, ts, it):
                        pe.wait_ge(sem("slot_used"), slot0 + k + 1)
                        pe.wait_ge(sem("o_saved"), it + 1)
                        for a, t in enumerate(ts):
                            i = nc.tensor.transpose(ps[:, MB + k % MRING, a * P:(a + 1) * P], osb[:, t * P:(t + 1) * P], ident[:, :])
                        i.then_inc(sem("slot_done"), 1)

                    def turn_maxima(slot0, k, nth):
                        pe.wait_ge(sem("slot_used"), slot0 + k + 1)
                        pe.wait_ge(sem("max_split"), nth)
                        n = SPLITS * HALF // P
                        nc.tensor.transpose(psb[0:n, MB + k % MRING, 0:P], ms[:, :, :].rearrange("p s t -> p (s t)"),
                                            identb[:, :]).then_inc(sem("slot_done"), 2)

                    def weigh_values(it, kt):
                        if kt == 0:
                            pe.wait_ge(sem("o_saved"), it + 1)
                        if kt % 8 == 0:
                            pe.wait_ge(sem("v_ready"), 4 * (it // 2) + kt // 8 + 1)
                        pe.wait_ge(sem("exp_done"), 4 * (it * KT + kt) + 8)
                        sum_values(kt)

                    def sum_values(kt):
                        for j in range(4):
                            i = nc.tensor.matmul(ps[32 * j:32 * j + 32, AV, :], vst[:, kt, :], pb[:, (4 * kt + j) % PRING, :],
                                                 start=(kt == 0), stop=(kt == KT - 1))
                        i.then_inc(sem("av_done"), 1)

                    pe.wait_ge(sem("head_loaded"), QL)
                    for m in range(MAXES):
                        max_slot(0, m, 0, m, 0)
                    turn_maxima(0, MAXES, 1)
                    for m in range(AHEAD):
                        max_slot(0, MAXES + 2 + m, 0, m, 1)
                    pe.wait_ge(sem("head_loaded"), 2 * QL)
                    pe.wait_ge(sem("v_init"), 6)
                    nc.tensor.matmul(ps[:, AV, :], ident[:, :], pb[:, PRING - 1, :], start=True, stop=False)
                    pe.wait_ge(sem("v_ready"), 4)

                    def attend_round(it, last=False):
                        b, half = (it // 2) % 3, it % 2
                        ahead = (((it + 1) // 2) % 3, (it + 1) % 2), ((it // 2 + 1) % 3, half)
                        slot0 = SLOT0 + SLOTS * it
                        pe.wait_ge(sem("rows_loaded"), 16 * SPLITS * (it + 1))
                        if not last:
                            pe.wait_ge(sem("head_loaded"), QL * (it // 2 + 2))
                        for kt in range(KT):
                            for j in range(4):
                                pe.wait_ge(sem("exp_done"), 4 * (it * KT + kt) + j + 1)
                                nc.tensor.matmul(ps[:, SC + j, :], kop[:, ds(b, 1), kt * P:(kt + 1) * P],
                                                 qop[:, ds(b, 1), ds(half * HALF + j * CH, CH)],
                                                 start=True, stop=True).then_inc(sem("score_done"), 1)
                                m = 4 * kt + j
                                which, later = maximum_of(m)
                                if not last:
                                    max_slot(slot0, turn_of(m), ahead[later][0], which, ahead[later][1])
                                if m in OUT_AT:
                                    o = OUT_AT.index(m)
                                    turn_outputs(slot0, o if last else turn_of(m) + 1, (2 * o, 2 * o + 1), it)
                                if m == MAX_AT and not last:
                                    turn_maxima(slot0, turn_of(m) + 1, it + 2)
                            if kt:
                                weigh_values(it, kt - 1)
                            else:
                                pe.wait_ge(sem("exp_done"), 4 * it * KT + 4)
                                sum_values(KT - 1)

                    with pe.Fori(0, ROUNDS - 1) as it:
                        attend_round(it)
                    attend_round(ROUNDS - 1, last=True)
                    pe.wait_ge(sem("exp_done"), 4 * ROUNDS * KT + 4)
                    sum_values(KT - 1)
                    turn_outputs(SLOTN - 2, 2, (0, 1), ROUNDS)
                    turn_outputs(SLOTN - 2, 3, (2, 3), ROUNDS)

                @block.vector
                def _(dve):
                    dve.sem_inc(sem("slot_used"), MRING)
                    NM = 5
                    steps = Steps(dve, sem("max_step"))

                    def reduce_slot(slot0, k, m):
                        dve.wait_ge(sem("slot_done"), slot0 + k + 1)
                        nc.vector.tensor_reduce(mp[:, m // NCH, m % NCH:m % NCH + 1], ps[:, MB + k % MRING, :], AX.X, ALU.max).then_inc(sem("slot_used"), 1)

                    def split_maxima(part, slots=0):
                        steps.wait()
                        if part == 0:
                            dve.wait_ge(sem("slot_used"), slots + MRING)
                            steps.add(nc.vector.tensor_reduce(mq[:, :], mp[:, :, :], AX.X, ALU.max))
                            steps.wait()
                        elif part == 1:
                            steps.add(nc.vector.tensor_scalar(ms[:, 0, :], mq[:, :], -1.0, None, ALU.mult))
                        elif part == 2:
                            steps.add(nc.vector.scalar_tensor_tensor(mr[:, :], mq[:, :], -1.0, ms[:, 0, :], ALU.mult, ALU.subtract))
                        elif part == 3:
                            steps.add(nc.vector.tensor_copy(ms[:, 1, :], mr[:, :]))
                        else:
                            nc.vector.tensor_tensor(ms[:, 2, :], mr[:, :], ms[:, 1, :], ALU.subtract).then_inc(sem("max_split"), 1)

                    def save_rows(slot0, k, event):
                        dve.wait_ge(sem("slot_done"), slot0 + k + 2)
                        dve.wait_ge(sem("rows_loaded"), 16 * SPLITS * event)
                        nc.vector.tensor_copy(msb[:, :], psb[0:SPLITS * HALF // P, MB + k % MRING, 0:P]).then_inc(sem("rows_ready"), 1)
                        dve.wait_ge(sem("rows_ready"), event + 1)
                        dve.sem_inc(sem("slot_used"), 2)

                    def outputs(slot0, k, t, it):
                        dve.wait_ge(sem("slot_done"), slot0 + k + 1)
                        o = ps[:, MB + k % MRING, 0:2 * P].rearrange("p (t j c) -> p t j c", t=2, j=4)
                        r = rc[:, t // 2, :, :]
                        steps.add(nc.vector.reciprocal(r, o[:, :, :, HD]))
                        steps.wait()
                        nc.vector.tensor_tensor(O[:, ds(it, 1), t:t + 2, :, :].rearrange("p a t j d -> p (a t) j d"), o[:, :, :, 0:HD],
                                                r[:, :, :, None].to_broadcast([P, 2, 4, HD]), ALU.mult).then_inc(sem("slot_used"), 1)

                    for m in range(MAXES):
                        reduce_slot(0, m, m)
                    for part in range(5):
                        split_maxima(part, MAXES)
                    save_rows(0, MAXES, 0)
                    for m in range(AHEAD):
                        reduce_slot(0, MAXES + 2 + m, m)
                    with dve.Fori(0, ROUNDS - 1) as it:
                        slot0 = SLOT0 + SLOTS * it
                        steps.at = 4 + it * 6
                        for m in range(MAXES):
                            which, later = maximum_of(m)
                            if later and which < 5:
                                split_maxima(which, slot0 + turn_of(m))
                            reduce_slot(slot0, turn_of(m), which)
                            if m in OUT_AT:
                                outputs(slot0, turn_of(m) + 1, 2 * OUT_AT.index(m), it)
                            if m == MAX_AT:
                                save_rows(slot0, turn_of(m) + 1, it + 1)
                    steps.at = 4 + (ROUNDS - 1) * 6
                    for o in range(2):
                        outputs(SLOTN - 2, o, 2 * o, ROUNDS - 1)
                    dve.wait_ge(sem("slot_used"), SLOTN + MRING)
                    for o in range(2):
                        outputs(SLOTN - 2, 2 + o, 2 * o, ROUNDS)

    def project_out(wout, bout, O):
        base, nbase = front
        front[0] += NCH + 1
        front[1] += NCH + 2
        with ExitStack() as s10:
            nbuf = sb("o_nbuf", [P, 2, TPC, D], stack=s10)
            nT = sb("o_nT", [P, 2, KD, CH], stack=s10)
            Oh = O[:, 1:ROUNDS + 1, :, :, :].rearrange("p (h a) t j d -> p a h t j d", a=2)
            with nc.Block() as block:
                @block.gpsimd
                def _(pool):
                    with pool.Fori(0, NCH) as n:
                        xc = X[:, ds(n * TPC, TPC), :]
                        nc.gpsimd.tensor_tensor(xc, xc, bout[:, None, :].to_broadcast([P, TPC, D]), ALU.add).then_inc(sem("bout_added"), 1)

                @block.scalar
                def _(act):
                    def turned(n, par):
                        act.wait_ge(sem("transposed"), base + n + 1)
                        nc.scalar.activation(nT[:, par, :, :], ps[:, 0:2, :], ACT.Copy).then_inc(sem("nT_ready"), 1)

                    turned(0, 0)
                    with act.Fori(0, NCH // 2) as i:
                        turned(2 * i + 1, 1)
                        turned(2 * i + 2, 0)

                @block.tensor
                def _(pe):
                    def turn(n, par):
                        pe.wait_ge(sem("normed"), nbase + n + 1)
                        pe.wait_ge(sem("nT_ready"), base + n)
                        transposes(nbuf[:, par]).then_inc(sem("transposed"), 1)

                    def chunk(n, par):
                        turn(n + 1, 1 - par)
                        pe.wait_ge(sem("nT_ready"), base + n + 1)
                        pe.wait_ge(sem("wout_added"), n)
                        for t in range(TPC):
                            for k in range(KD):
                                i = nc.tensor.matmul(ps[:, 6 + t // 2, (t % 2) * D:(t % 2 + 1) * D],
                                                     nT[:, par, k, t * P:(t + 1) * P], wout[:, k, :], start=(k == 0), stop=(k == KD - 1))
                        i.then_inc(sem("wout_done"), 1)

                    turn(0, 0)
                    with pe.Fori(0, NCH // 2) as i:
                        chunk(2 * i, 0)
                        chunk(2 * i + 1, 1)

                @block.vector
                def _(dve):
                    steps = Steps(dve, sem("out_step"))
                    PER = STATS

                    def gather(n, par):
                        for t in range(TPC):
                            i = nc.vector.tensor_copy(nbuf[:, par, t, :].rearrange("p (h d) -> p h d", h=H),
                                                      Oh[:, ds((n // 4) % 2, 1), :, t, ds(n % 4, 1), :].rearrange("p a h j d -> p (a h) (j d)"))
                        i.then_inc(sem("normed"), 1)

                    def chunk(n, par):
                        steps.at = n * PER
                        dve.wait_ge(sem("transposed"), base + n + 1)
                        gather(n + 2, par)
                        dve.wait_ge(sem("bout_added"), n + 1)
                        dve.wait_ge(sem("wout_done"), n + 1)
                        xc = X[:, ds(n * TPC, TPC), :]
                        nc.vector.tensor_tensor(xc, xc, ps[:, 6:8, :].rearrange("p b (t d) -> p (b t) d", d=D), ALU.add).then_inc(sem("wout_added"), 1)
                        dve.wait_ge(sem("wout_added"), n + 1)
                        stats(dve, steps, n)

                    gather(0, 0)
                    gather(1, 1)
                    with dve.Fori(0, NCH // 2) as i:
                        chunk(2 * i, 0)
                        chunk(2 * i + 1, 1)

    with ExitStack() as s1:
        W = {"w1": sb("w1", [P, KD, F], stack=s1), "w2": sb("w2", [P, KF, D], stack=s1), "b1": sb("b1", [P, KF], stack=s1),
             "b2h": sb("b2h", [P, D], stack=s1), "win": sb("win", [P, KD, 2 * D], stack=s1),
             "wo": sb("wo", [P, KD, D], stack=s1), "c0": sb("c0", [P, 12, KD], stack=s1),
             "ob": sb("ob", [P, D], stack=s1), "lnw": sb("lnw", [P, D], stack=s1), "lnb": sb("lnb", [P, D], stack=s1),
             "nbuf": sb("nbuf", [P, 2, TPC, D], stack=s1), "nT": sb("nT", [P, 2, KD, CH], stack=s1),
             "hT": sb("hT", [P, KF, CH], stack=s1),
             "uT": sb("uT", [P, NCH, KD, CH], stack=s1), "mvH": sb("mvH", [P, TILES, 2], stack=s1), "rH": sb("rH", [P, TILES], stack=s1)}
        W["Hb"] = W["uT"][:, :, :, :].rearrange("p n k c -> p (n k c)").rearrange("p (n d) -> p n d", d=D)
        ffn(0, W)
        scan_layer(W)
        ffn(1, W)
    slots(0)
    attention()
    slots(1)


def layout(i):
    g = {k: np.asarray(v) for k, v in i.items()}
    col = lambda v: np.ascontiguousarray(v.reshape(-1, P).T)
    a = {"x": g["L0_attn_x"], "W1": g["L0_ffn_W1"], "W2": g["L0_ffn_W2"], "b1": col(g["L0_ffn_b1"]),
         "b2": g["L0_ffn_b2"], "in_proj_w": g["L0_attn_in_proj_w"], "out_proj_w": g["L0_attn_out_proj_w"],
         "out_proj_b": g["L0_attn_out_proj_b"], "ln_w": g["L0_attn_ln_w"], "ln_b": g["L0_attn_ln_b"]}
    b = g["L0_attn_in_proj_b"]
    cw = g["L0_attn_conv_w"]
    a["ssm_cols"] = np.stack([col(v) for v in (b[:D], b[D:], cw[:, 0, 0], cw[:, 0, 1], cw[:, 0, 2], g["L0_attn_conv_b"],
                                               g["L0_attn_logit_a"], g["L0_attn_ssm_b"], g["L0_attn_ssm_c"],
                                               g["L0_attn_ssm_d"], b[:D], b[:D])], axis=1)
    s = "L1_ffn_"
    for n in ("d_Wq", "d_Wv", "d_Wo", "c_Wk", "c_Wv", "c_Wo"):
        a[n] = g[s + n]
    a["d_WkT"], a["c_WqT"] = g[s + "d_Wk"].T, g[s + "c_Wq"].T
    a["cols"] = np.stack([col(g[s + n]) for n in ("d_bq", "d_bk", "d_bv", "c_bq", "c_bk", "c_bv")], axis=1)
    rep = lambda v: np.broadcast_to(v, (E, D))
    a["rows16"] = np.stack([g[s + "slot_query"][0], rep(g[s + "d_bo"])], axis=1)
    a["erows"] = np.stack([g[s + n] for n in ("e_ln_g", "e_ln_b", "e_b2")], axis=1)
    a["eb"] = np.stack([g[s + n].reshape(4, GROUPS, 2, P, 4).transpose(3, 1, 2, 4, 0).reshape(P, GROUPS, KF, 4)
                        for n in ("e_b1", "e_bg")], axis=1)
    a["c_bo"] = g[s + "c_bo"]
    for n in ("e_W1", "e_Wg", "e_W2"):
        a[n] = g[s + n]
    w = g["L1_attn_w_qkv"]
    a["wqkv"] = w.T
    a["woutT"] = g["L1_attn_w_out"].T
    a["b_out"] = g["L1_attn_b_out"]
    return {k: np.ascontiguousarray(v) for k, v in {**a, **constants()}.items()}


def kernel(**inputs):
    import concourse.bacc as _bacc
    from concourse.bass_utils import run_bass_kernel_spmd as _run

    nc = _bacc.Bacc("TRN2", target_bir_lowering=False, num_devices=1)
    arrays = layout(inputs)
    A = {n: nc.dram_tensor("in_" + n, a.shape, mybir.dt.from_np(a.dtype), kind="ExternalInput").ap() for n, a in arrays.items()}
    out = nc.dram_tensor("out_x", (1, T, D), f32, kind="ExternalOutput").ap()
    build(nc, A, out)
    r = _run(nc, [{"in_" + n: a for n, a in arrays.items()}], core_ids=[0])
    return r.results[0]["out_x"]
```
